# Optimizing a Trainium2 kernel written in Bass

```python
import numpy as np
import jax
import jax.numpy as jnp

def _softmax(x, axis=-1):
    return jax.nn.softmax(x, axis=axis)

def _gelu(x):
    return jax.nn.gelu(x, approximate=True)

def _silu(x):
    return jax.nn.silu(x)

def _sigmoid(x):
    return jax.nn.sigmoid(x)

def _layernorm(x, axis=-1, eps=1e-05):
    m = jnp.mean(x, axis=axis, keepdims=True)
    v = jnp.var(x, axis=axis, keepdims=True)
    return (x - m) / jnp.sqrt(v + eps)

def _scatter_add(tgt, idx, src, axis=0):
    return tgt.at[idx].add(src)

def _segment_sum(src, seg, n):
    return jax.ops.segment_sum(src, seg, n)
kernel_name = 'mk_audio_tower_d2_tok_audfeat512_r4_f6d1a5'

def setup_inputs(seed: int=0):
    np.random.seed(seed)
    _w = jnp.asarray

    def _rec_inputs():
        import jax
        import jax.numpy as jnp
        _rk = jax.random.key(seed)
        x = -7.10856e-05 + 0.999911 * jax.random.normal(jax.random.fold_in(_rk, 1), (8, 375, 128), jnp.float32)
        return x
    x = _rec_inputs()

    def _L0_tok_setup():
        import jax, jax.numpy as jnp
        import numpy as np
        EPS = 1e-05

        def conv1d(x, w, b, stride=1, padding=0):
            out = jax.lax.conv_general_dilated(x, w, window_strides=(stride,), padding=[(padding, padding)], dimension_numbers=('NCH', 'OIH', 'NCH'))
            return out + b[None, :, None]

        def layer_norm(x, g, b):
            mu = jnp.mean(x, axis=-1, keepdims=True)
            var = jnp.mean(jnp.square(x - mu), axis=-1, keepdims=True)
            return (x - mu) * jax.lax.rsqrt(var + EPS) * g + b
        key = jax.random.key(seed)
        ks = jax.random.split(key, 16)
        B, T, H = (64, 512, 128)
        Bn = H // 2
        s = 0.02
        return {'x': jax.random.normal(ks[0], (B, T, H), dtype=jnp.float32), 'w_compress': jax.random.normal(ks[1], (Bn, H, 1), dtype=jnp.float32) * s, 'b_compress': jnp.zeros((Bn,), dtype=jnp.float32), 'w_main': jax.random.normal(ks[2], (Bn, Bn, 3), dtype=jnp.float32) * s, 'b_main': jnp.zeros((Bn,), dtype=jnp.float32), 'w_expand': jax.random.normal(ks[3], (H, Bn, 1), dtype=jnp.float32) * s, 'b_expand': jnp.zeros((H,), dtype=jnp.float32), 'g_conv_norm': jnp.ones((H,), dtype=jnp.float32), 'b_conv_norm': jnp.zeros((H,), dtype=jnp.float32), 'w_ff1': jax.random.normal(ks[4], (Bn, H), dtype=jnp.float32) * s, 'b_ff1': jnp.zeros((Bn,), dtype=jnp.float32), 'w_ff2': jax.random.normal(ks[5], (H, Bn), dtype=jnp.float32) * s, 'b_ff2': jnp.zeros((H,), dtype=jnp.float32), 'g_ff_norm': jnp.ones((H,), dtype=jnp.float32), 'b_ff_norm': jnp.zeros((H,), dtype=jnp.float32)}
    _L0_tok_all = _L0_tok_setup()
    _L0_tok_in = {k: v for k, v in _L0_tok_all.items() if k in ('w_compress', 'b_compress', 'w_main', 'b_main', 'w_expand', 'b_expand', 'g_conv_norm', 'b_conv_norm', 'w_ff1', 'b_ff1', 'w_ff2', 'b_ff2', 'g_ff_norm', 'b_ff_norm')}
    del _L0_tok_all

    def _L0_attn_setup():
        import jax, jax.numpy as jnp
        import numpy as np
        K = 128
        H = 8
        key = jax.random.key(seed)
        k1, k2, k3, k4, k5 = jax.random.split(key, 5)
        b, s = (2, 512)
        x = jax.random.normal(k1, (b, s, K), dtype=jnp.float32)
        scale = 0.02
        Wq = jax.random.normal(k2, (H * K, K), dtype=jnp.float32) * scale
        Wk = jax.random.normal(k3, (H * K, K), dtype=jnp.float32) * scale
        Wv = jax.random.normal(k4, (H * K, K), dtype=jnp.float32) * scale
        Wu = jax.random.normal(k5, (K, H * K), dtype=jnp.float32) * scale
        return {'x': x, 'Wq': Wq, 'Wk': Wk, 'Wv': Wv, 'Wu': Wu}
    _L0_attn_all = _L0_attn_setup()
    _L0_attn_in = {k: v for k, v in _L0_attn_all.items() if k in ('Wq', 'Wk', 'Wv', 'Wu')}
    del _L0_attn_all

    def _L0_ffn_setup():
        import jax, jax.numpy as jnp
        import numpy as np
        B, S, D, F, E, K = (4, 512, 128, 512, 8, 2)
        key = jax.random.key(seed)
        kx, kg, kw, kv, k2 = jax.random.split(key, 5)
        scale = 0.02
        return {'x': jax.random.normal(kx, (B, S, D), dtype=jnp.float32), 'Wg': jax.random.normal(kg, (D, E), dtype=jnp.float32) * scale, 'W': jax.random.normal(kw, (E, D, F), dtype=jnp.float32) * scale, 'V': jax.random.normal(kv, (E, D, F), dtype=jnp.float32) * scale, 'W2': jax.random.normal(k2, (E, F, D), dtype=jnp.float32) * scale}
    _L0_ffn_all = _L0_ffn_setup()
    _L0_ffn_in = {k: v for k, v in _L0_ffn_all.items() if k in ('Wg', 'W', 'V', 'W2')}
    del _L0_ffn_all

    def _L1_attn_setup():
        import jax, jax.numpy as jnp
        import numpy as np
        EMB = 128
        HEADS = 8
        HEAD_DIM = EMB // HEADS
        LN_EPS = 1e-05

        def _layernorm(v, gamma, beta):
            mu = jnp.mean(v, axis=-1, keepdims=True)
            var = jnp.var(v, axis=-1, keepdims=True)
            return (v - mu) * jax.lax.rsqrt(var + LN_EPS) * gamma + beta
        key = jax.random.key(seed)
        ks = jax.random.split(key, 7)
        b, t, e = (2, 768, EMB)
        x = jax.random.normal(ks[0], (b, t, e), dtype=jnp.float32)
        scale = 0.02
        Wq = jax.random.normal(ks[1], (e, e), dtype=jnp.float32) * scale
        Wk = jax.random.normal(ks[2], (e, e), dtype=jnp.float32) * scale
        Wv = jax.random.normal(ks[3], (e, e), dtype=jnp.float32) * scale
        Wo = jax.random.normal(ks[4], (e, e), dtype=jnp.float32) * scale
        bo = jnp.zeros((e,), dtype=jnp.float32)
        q_gamma = jnp.ones((HEAD_DIM,), dtype=jnp.float32)
        q_beta = jnp.zeros((HEAD_DIM,), dtype=jnp.float32)
        k_gamma = jnp.ones((HEAD_DIM,), dtype=jnp.float32)
        k_beta = jnp.zeros((HEAD_DIM,), dtype=jnp.float32)
        return {'x': x, 'Wq': Wq, 'Wk': Wk, 'Wv': Wv, 'Wo': Wo, 'bo': bo, 'q_gamma': q_gamma, 'q_beta': q_beta, 'k_gamma': k_gamma, 'k_beta': k_beta}
    _L1_attn_all = _L1_attn_setup()
    _L1_attn_in = {k: v for k, v in _L1_attn_all.items() if k in ('Wq', 'Wk', 'Wv', 'Wo', 'bo', 'q_gamma', 'q_beta', 'k_gamma', 'k_beta')}
    del _L1_attn_all

    def _L1_ffn_setup():
        import jax, jax.numpy as jnp
        import numpy as np
        H = 128
        F = 512
        E = 16
        SHARED = 2
        TOP_K = 4
        B, S = (2, 512)

        def _mlp(x, w1, b1, w2, b2):
            return jax.nn.gelu(x @ w1 + b1, approximate=False) @ w2 + b2
        key = jax.random.key(seed)
        ks = jax.random.split(key, 10)
        sc = 0.02
        return {'hidden_states': jax.random.normal(ks[0], (B, S, H), dtype=jnp.float32), 'gate_w': jax.random.normal(ks[1], (E, H), dtype=jnp.float32) * sc, 're_w1': jax.random.normal(ks[2], (E, H, F), dtype=jnp.float32) * sc, 're_b1': jnp.zeros((E, F), dtype=jnp.float32), 're_w2': jax.random.normal(ks[3], (E, F, H), dtype=jnp.float32) * sc, 're_b2': jnp.zeros((E, H), dtype=jnp.float32), 'se_w1': jax.random.normal(ks[4], (SHARED, H, F), dtype=jnp.float32) * sc, 'se_b1': jnp.zeros((SHARED, F), dtype=jnp.float32), 'se_w2': jax.random.normal(ks[5], (SHARED, F, H), dtype=jnp.float32) * sc, 'se_b2': jnp.zeros((SHARED, H), dtype=jnp.float32)}
    _L1_ffn_all = _L1_ffn_setup()
    _L1_ffn_in = {k: v for k, v in _L1_ffn_all.items() if k in ('gate_w', 're_w1', 're_b1', 're_w2', 're_b2', 'se_w1', 'se_b1', 'se_w2', 'se_b2')}
    del _L1_ffn_all
    return {'x': x, 'L0_tok_w_compress': _L0_tok_in['w_compress'], 'L0_tok_b_compress': _L0_tok_in['b_compress'], 'L0_tok_w_main': _L0_tok_in['w_main'], 'L0_tok_b_main': _L0_tok_in['b_main'], 'L0_tok_w_expand': _L0_tok_in['w_expand'], 'L0_tok_b_expand': _L0_tok_in['b_expand'], 'L0_tok_g_conv_norm': _L0_tok_in['g_conv_norm'], 'L0_tok_b_conv_norm': _L0_tok_in['b_conv_norm'], 'L0_tok_w_ff1': _L0_tok_in['w_ff1'], 'L0_tok_b_ff1': _L0_tok_in['b_ff1'], 'L0_tok_w_ff2': _L0_tok_in['w_ff2'], 'L0_tok_b_ff2': _L0_tok_in['b_ff2'], 'L0_tok_g_ff_norm': _L0_tok_in['g_ff_norm'], 'L0_tok_b_ff_norm': _L0_tok_in['b_ff_norm'], 'L0_attn_Wq': _L0_attn_in['Wq'], 'L0_attn_Wk': _L0_attn_in['Wk'], 'L0_attn_Wv': _L0_attn_in['Wv'], 'L0_attn_Wu': _L0_attn_in['Wu'], 'L0_ffn_Wg': _L0_ffn_in['Wg'], 'L0_ffn_W': _L0_ffn_in['W'], 'L0_ffn_V': _L0_ffn_in['V'], 'L0_ffn_W2': _L0_ffn_in['W2'], 'L1_attn_Wq': _L1_attn_in['Wq'], 'L1_attn_Wk': _L1_attn_in['Wk'], 'L1_attn_Wv': _L1_attn_in['Wv'], 'L1_attn_Wo': _L1_attn_in['Wo'], 'L1_attn_bo': _L1_attn_in['bo'], 'L1_attn_q_gamma': _L1_attn_in['q_gamma'], 'L1_attn_q_beta': _L1_attn_in['q_beta'], 'L1_attn_k_gamma': _L1_attn_in['k_gamma'], 'L1_attn_k_beta': _L1_attn_in['k_beta'], 'L1_ffn_gate_w': _L1_ffn_in['gate_w'], 'L1_ffn_re_w1': _L1_ffn_in['re_w1'], 'L1_ffn_re_b1': _L1_ffn_in['re_b1'], 'L1_ffn_re_w2': _L1_ffn_in['re_w2'], 'L1_ffn_re_b2': _L1_ffn_in['re_b2'], 'L1_ffn_se_w1': _L1_ffn_in['se_w1'], 'L1_ffn_se_b1': _L1_ffn_in['se_b1'], 'L1_ffn_se_w2': _L1_ffn_in['se_w2'], 'L1_ffn_se_b2': _L1_ffn_in['se_b2']}

def reference(x, L0_tok_w_compress, L0_tok_b_compress, L0_tok_w_main, L0_tok_b_main, L0_tok_w_expand, L0_tok_b_expand, L0_tok_g_conv_norm, L0_tok_b_conv_norm, L0_tok_w_ff1, L0_tok_b_ff1, L0_tok_w_ff2, L0_tok_b_ff2, L0_tok_g_ff_norm, L0_tok_b_ff_norm, L0_attn_Wq, L0_attn_Wk, L0_attn_Wv, L0_attn_Wu, L0_ffn_Wg, L0_ffn_W, L0_ffn_V, L0_ffn_W2, L1_attn_Wq, L1_attn_Wk, L1_attn_Wv, L1_attn_Wo, L1_attn_bo, L1_attn_q_gamma, L1_attn_q_beta, L1_attn_k_gamma, L1_attn_k_beta, L1_ffn_gate_w, L1_ffn_re_w1, L1_ffn_re_b1, L1_ffn_re_w2, L1_ffn_re_b2, L1_ffn_se_w1, L1_ffn_se_b1, L1_ffn_se_w2, L1_ffn_se_b2):
    import jax
    import jax.numpy as jnp

    def _L0_tok_ref(x, w_compress, b_compress, w_main, b_main, w_expand, b_expand, g_conv_norm, b_conv_norm, w_ff1, b_ff1, w_ff2, b_ff2, g_ff_norm, b_ff_norm):
        import jax, jax.numpy as jnp
        import numpy as np
        EPS = 1e-05

        def conv1d(x, w, b, stride=1, padding=0):
            out = jax.lax.conv_general_dilated(x, w, window_strides=(stride,), padding=[(padding, padding)], dimension_numbers=('NCH', 'OIH', 'NCH'))
            return out + b[None, :, None]

        def layer_norm(x, g, b):
            mu = jnp.mean(x, axis=-1, keepdims=True)
            var = jnp.mean(jnp.square(x - mu), axis=-1, keepdims=True)
            return (x - mu) * jax.lax.rsqrt(var + EPS) * g + b
        xt = jnp.transpose(x, (0, 2, 1))
        identity = xt
        h = jax.nn.silu(conv1d(xt, w_compress, b_compress))
        h = jax.nn.silu(conv1d(h, w_main, b_main, stride=1, padding=1))
        h = conv1d(h, w_expand, b_expand)
        h = jnp.transpose(h, (0, 2, 1))
        identity = jnp.transpose(identity, (0, 2, 1))
        y = layer_norm(h + identity, g_conv_norm, b_conv_norm)
        ff = jnp.einsum('bth,oh->bto', y, w_ff1) + b_ff1
        ff = jax.nn.gelu(ff, approximate=False)
        ff = jnp.einsum('bto,ho->bth', ff, w_ff2) + b_ff2
        y = layer_norm(ff + y, g_ff_norm, b_ff_norm)
        yt = jnp.transpose(y, (0, 2, 1))
        pooled = jax.lax.reduce_window(yt, -jnp.inf, jax.lax.max, (1, 1, 3), (1, 1, 1), 'VALID')
        return jnp.transpose(pooled, (0, 2, 1))

    def _L0_attn_ref(x, Wq, Wk, Wv, Wu):
        import jax, jax.numpy as jnp
        import numpy as np
        K = 128
        H = 8
        b, s, _ = x.shape
        q = jnp.einsum('bsd,hed->bhse', x, Wq.reshape(H, K, K))
        kk = jnp.einsum('bsd,hed->bhse', x, Wk.reshape(H, K, K))
        v = jnp.einsum('bsd,hed->bhse', x, Wv.reshape(H, K, K))
        scale = K ** (-0.25)
        dot = jnp.einsum('bhse,bhte->bhst', q * scale, kk * scale)
        causal = jnp.tril(jnp.ones((s, s), dtype=bool))
        dot = jnp.where(causal[None, None], dot, -jnp.inf)
        weights = jax.nn.softmax(dot, axis=-1)
        heads_out = jnp.einsum('bhst,bhte->bhse', weights, v)
        heads_out = heads_out.transpose(0, 2, 1, 3).reshape(b, s, H * K)
        return heads_out @ Wu.T

    def _L0_ffn_ref(x, Wg, W, V, W2):
        import jax, jax.numpy as jnp
        import numpy as np
        B, S, D, F, E, K = (4, 512, 128, 512, 8, 2)
        gate_logits = jnp.einsum('bsd,de->bse', x, Wg)
        topv, topi = jax.lax.top_k(gate_logits, K)
        w = jax.nn.softmax(topv, axis=-1)
        gw = jnp.sum(w[..., None] * jax.nn.one_hot(topi, E, dtype=x.dtype), axis=-2)
        y = jnp.zeros_like(x)
        n_experts = W.shape[0]
        for e in range(n_experts):
            h = jax.nn.silu(jnp.einsum('bsd,df->bsf', x, W[e])) * jnp.einsum('bsd,df->bsf', x, V[e])
            y = y + gw[..., e:e + 1] * jnp.einsum('bsf,fd->bsd', h, W2[e])
        return y

    def _L1_attn_ref(x, Wq, Wk, Wv, Wo, bo, q_gamma, q_beta, k_gamma, k_beta):
        import jax, jax.numpy as jnp
        import numpy as np
        EMB = 128
        HEADS = 8
        HEAD_DIM = EMB // HEADS
        LN_EPS = 1e-05

        def _layernorm(v, gamma, beta):
            mu = jnp.mean(v, axis=-1, keepdims=True)
            var = jnp.var(v, axis=-1, keepdims=True)
            return (v - mu) * jax.lax.rsqrt(var + LN_EPS) * gamma + beta
        b, t, e = x.shape
        h, s = (HEADS, HEAD_DIM)
        q = (x @ Wq.T).reshape(b, t, h, s)
        k = (x @ Wk.T).reshape(b, t, h, s)
        v = (x @ Wv.T).reshape(b, t, h, s)
        q = _layernorm(q, q_gamma, q_beta)
        k = _layernorm(k, k_gamma, k_beta)
        scale = 1.0 / jnp.sqrt(jnp.float32(s))
        scores = jnp.einsum('bqhs,bkhs->bhqk', q, k) * scale
        rows = jnp.arange(t)[:, None]
        cols = jnp.arange(t)[None, :]
        scores = jnp.where(cols > rows, -jnp.inf, scores)
        attn = jax.nn.softmax(scores, axis=-1)
        out = jnp.einsum('bhqk,bkhs->bqhs', attn, v).reshape(b, t, e)
        return out @ Wo.T + bo

    def _L1_ffn_ref(hidden_states, gate_w, re_w1, re_b1, re_w2, re_b2, se_w1, se_b1, se_w2, se_b2):
        import jax, jax.numpy as jnp
        import numpy as np
        H = 128
        F = 512
        E = 16
        SHARED = 2
        TOP_K = 4
        B, S = (2, 512)

        def _mlp(x, w1, b1, w2, b2):
            return jax.nn.gelu(x @ w1 + b1, approximate=False) @ w2 + b2
        b, s, h = hidden_states.shape
        x = hidden_states.reshape(-1, h)
        gate_probs = jax.nn.softmax(x @ gate_w.T, axis=-1)
        top_v, top_i = jax.lax.top_k(gate_probs, TOP_K)
        top_v = jax.nn.softmax(top_v, axis=-1)
        combine = jnp.einsum('tk,tke->te', top_v, jax.nn.one_hot(top_i, E, dtype=x.dtype))
        routed = jnp.zeros_like(x)
        for e in range(E):
            routed = routed + combine[:, e:e + 1] * _mlp(x, re_w1[e], re_b1[e], re_w2[e], re_b2[e])
        shared = jnp.zeros_like(x)
        for j in range(SHARED):
            shared = shared + _mlp(x, se_w1[j], se_b1[j], se_w2[j], se_b2[j])
        shared = shared / SHARED
        return (routed + shared).reshape(b, s, h)
    h = _L0_tok_ref(x, L0_tok_w_compress, L0_tok_b_compress, L0_tok_w_main, L0_tok_b_main, L0_tok_w_expand, L0_tok_b_expand, L0_tok_g_conv_norm, L0_tok_b_conv_norm, L0_tok_w_ff1, L0_tok_b_ff1, L0_tok_w_ff2, L0_tok_b_ff2, L0_tok_g_ff_norm, L0_tok_b_ff_norm)
    h = h + _L0_attn_ref(_layernorm(h, axis=-1), L0_attn_Wq, L0_attn_Wk, L0_attn_Wv, L0_attn_Wu)
    h = h + _L0_ffn_ref(_layernorm(h, axis=-1), L0_ffn_Wg, L0_ffn_W, L0_ffn_V, L0_ffn_W2)
    h = h + _L1_attn_ref(_layernorm(h, axis=-1), L1_attn_Wq, L1_attn_Wk, L1_attn_Wv, L1_attn_Wo, L1_attn_bo, L1_attn_q_gamma, L1_attn_q_beta, L1_attn_k_gamma, L1_attn_k_beta)
    h = h + _L1_ffn_ref(_layernorm(h, axis=-1), L1_ffn_gate_w, L1_ffn_re_w1, L1_ffn_re_b1, L1_ffn_re_w2, L1_ffn_re_b2, L1_ffn_se_w1, L1_ffn_se_b1, L1_ffn_se_w2, L1_ffn_se_b2)
    return h

_drawn_inputs = setup_inputs


def setup_inputs(seed=0):
    import zlib

    import numpy as np

    out = dict(_drawn_inputs(seed))
    spreads = {'L0_tok_b_compress': (0.0, 0.8),
     'L0_tok_b_main': (0.0, 0.8),
     'L0_tok_b_expand': (0.0, 0.1),
     'L0_tok_g_conv_norm': (1.0, 0.2),
     'L0_tok_b_conv_norm': (0.0, 0.1),
     'L0_tok_b_ff1': (0.0, 0.8),
     'L0_tok_b_ff2': (0.0, 0.1),
     'L0_tok_g_ff_norm': (1.0, 0.2),
     'L0_tok_b_ff_norm': (0.0, 0.1),
     'L1_attn_bo': (0.0, 0.31),
     'L1_attn_q_gamma': (1.0, 0.6),
     'L1_attn_q_beta': (0.0, 2.0),
     'L1_attn_k_gamma': (1.0, 0.6),
     'L1_attn_k_beta': (0.0, 2.0),
     'L1_ffn_re_b1': (0.0, 2.0),
     'L1_ffn_re_b2': (0.0, 0.603),
     'L1_ffn_se_b1': (0.0, 1.558),
     'L1_ffn_se_b2': (0.0, 0.42)}
    factors = {'L0_tok_w_compress': 8.0,
     'L0_tok_w_main': 8.0,
     'L0_tok_w_expand': 6.036,
     'L0_tok_w_ff1': 3.139,
     'L0_tok_w_ff2': 2.794,
     'L0_attn_Wq': 8.0,
     'L0_attn_Wk': 8.0,
     'L0_ffn_Wg': 7.61,
     'L0_ffn_W': 6.799,
     'L0_ffn_V': 6.82,
     'L0_ffn_W2': 6.72,
     'L1_attn_Wq': 6.716,
     'L1_attn_Wk': 6.949,
     'L1_attn_Wv': 2.849,
     'L1_attn_Wo': 2.724,
     'L1_ffn_re_w1': 6.444,
     'L1_ffn_se_w1': 4.784}
    for name, (base, spread) in spreads.items():
        noise = np.random.default_rng([zlib.crc32(name.encode()), seed]).standard_normal(out[name].shape)
        drawn = base * np.exp(spread * noise) if base else spread * noise
        out[name] = jnp.asarray(drawn.astype(out[name].dtype))
    for name, factor in factors.items():
        out[name] = (out[name] * factor).astype(out[name].dtype)
    return out
```

```python
import numpy as np
import concourse.bass as bass
from concourse import mybir
from contextlib import ExitStack

B, T, D = 8, 375, 128
TP = T - 2
ST = 384
TC = T + 1
NT = TP + 1
TILES = ST // 128
BN = D // 2
HEADS = 8
HD1 = D // HEADS
FF = 512
FCH = FF // 128
E0, TOP0 = 8, 2
E1, TOP1, SHARED = 16, 4, 2
BIG = 1e30
EPS = 1e-5

F32 = mybir.dt.float32
F32R = mybir.dt.float32r
ALU = mybir.AluOpType
ACT = mybir.ActivationFunctionType
AX = mybir.AxisListType

VECS = ["b_expand", "g_conv", "b_conv", "b_ff2", "g_ff", "b_ff", "bo", "q_gamma", "q_beta", "k_gamma", "k_beta"]
LN_CONV, LN_FF, LN_ATT0, LN_MOE0, LN_ATT1, LN_Q, LN_K, LN_MOE1 = range(8)


def audio_tower(nc, A, out):
    ctx = ExitStack()
    with ctx:
        def sb(name, shape, dt=F32):
            return ctx.enter_context(nc.sbuf_tensor(name, shape, dt))

        def sem(name):
            return ctx.enter_context(nc.semaphore(name))

        res = sb("res", [D, B, ST])
        xn = sb("xn", [D, B, ST])
        cen = sb("cen", [D, B, ST])
        sqr = sb("sqr", [D, B, ST])
        frames = sb("frames", [D, B, ST])
        hid1 = sb("hid1", [D, B, ST])
        hid2 = sb("hid2", [D, B, ST])
        xh = sb("xh", [D, B, ST], F32R)
        xl = sb("xl", [D, B, ST], F32R)

        ident = sb("ident", [D, D])
        mean_w = sb("mean_w", [D, D])
        head_w = sb("head_w", [D, D])
        center_w = sb("center_w", [D, D])
        causal = sb("causal", [D, ST])
        head_mask = sb("head_mask", [D, HEADS])
        rev_idx = sb("rev_idx", [D, E1])
        vec = sb("vec", [D, len(VECS)])
        vec64 = sb("vec64", [BN, 3])
        eps = sb("eps", [D, 1])
        qaff = sb("qaff", [D, 2])
        w_comp = sb("w_comp", [D, BN])
        w_main = sb("w_main", [BN, 3, BN])
        w_exp = sb("w_exp", [BN, D])
        w_ff1 = sb("w_ff1", [D, BN])
        w_ff2 = sb("w_ff2", [BN, D])
        wg0 = sb("wg0", [D, E0])
        wg1 = sb("wg1", [D, E1])
        b1col = sb("b1col", [D, (E1 + SHARED) * FCH])
        b2col = sb("b2col", [D, E1 + SHARED])
        att_raw = sb("att_raw", [D, 4, D])

        mh = sb("mh", [D, HEADS, D], F32R)
        ml = sb("ml", [D, HEADS, D], F32R)
        nh = sb("nh", [D, HEADS, D], F32R)
        nl = sb("nl", [D, HEADS, D], F32R)
        a1c = sb("a1c", [D, 2, D])
        a1h = sb("a1h", [D, 2, D], F32R)
        a1l = sb("a1l", [D, 2, D], F32R)

        workf = sb("workf", [D, 7, ST])
        workr = sb("workr", [D, 18, ST], F32R)
        wsplit = sb("wsplit", [D, 6400], F32R)
        tt = sb("tt", [D, 4, ST])
        small = sb("small", [D, 8])

        raw_wq = xn[:, :, :].rearrange("p b c -> p (b c)")[:, 0:1024].rearrange("p (h d) -> p h d", h=HEADS)
        raw_wk = xn[:, :, :].rearrange("p b c -> p (b c)")[:, 1024:2048].rearrange("p (h d) -> p h d", h=HEADS)
        raw_wv = xn[:, :, :].rearrange("p b c -> p (b c)")[:, 2048:3072].rearrange("p (h d) -> p h d", h=HEADS)
        raw_wu = cen[:, :, :].rearrange("p b c -> p (b c)")[:, 0:1024].rearrange("p (h d) -> p h d", h=HEADS)
        prod = sqr[:, :, :].rearrange("p b c -> p (b c)")

        neg_s = workf[:, 0:2, :].rearrange("p a c -> p (a c)")
        prob = workf[:, 2:4, :].rearrange("p a c -> p (a c)")
        xb = workf[:, 4, :]
        xbh, xbl = workr[:, 0, :], workr[:, 1, :]
        xth, xtl = workr[:, 2, :], workr[:, 3, :]
        qh, ql = workr[:, 4, :], workr[:, 5, :]
        yh, yl = workr[:, 6, :], workr[:, 7, :]
        kbh, kbl = workr[:, 8, :], workr[:, 9, :]
        pth, ptl = workr[:, 10:12, :], workr[:, 12:14, :]
        qmh, qml = workr[:, 14:16, :], workr[:, 16:18, :]
        vph, vpl = wsplit[:, 0:3200], wsplit[:, 3200:6400]

        PS = ctx.enter_context(nc.psum_tensor("PS", [D, 8, 512], F32))

        S_AT = (0, 128, 384)
        S_N = (128, 256, NT)
        ROWS = (128, 128, NT - 256)
        T_AT = ((0, 0), (1, 0), (1, NT - 128))
        T_N = (NT, NT - 128, NT - 256)

        def v(name):
            return vec[:, VECS.index(name):VECS.index(name) + 1]

        ld_const, ld_frames, ld_tok, ld_att, ld_moe = map(sem, ("ld_const", "ld_frames", "ld_tok", "ld_att", "ld_moe"))
        pads_set, passed = sem("pads_set"), sem("passed")
        prod_done, prod_taken, parts_made, prod_link = map(sem, ("prod_done", "prod_taken", "parts_made", "prod_link"))
        comp_done, comp_act, main_done, main_act = map(sem, ("comp_done", "comp_act", "main_done", "main_act"))
        exp_done, exp_sum, ff1_done, ff1_act = map(sem, ("exp_done", "exp_sum", "ff1_done", "ff1_act"))
        ff2_done, ff2_sum, pool_a, pooled = map(sem, ("ff2_done", "ff2_sum", "pool_a", "pooled"))
        ln_mean, ln_cen, ln_sq, ln_var, ln_log, ln_rstd, ln_norm, ln_aff, ln_hi, ln_lo = map(
            sem, ("ln_mean", "ln_cen", "ln_sq", "ln_var", "ln_log", "ln_rstd", "ln_norm", "ln_aff", "ln_hi", "ln_lo"))
        at_in_hi, at_in_lo, at_in_f, xt_done, xt_hi, xt_lo = map(
            sem, ("at_in_hi", "at_in_lo", "at_in_f", "xt_done", "xt_hi", "xt_lo"))
        qt_done, qt_hi, qt_lo, sc_done, sc_min, ex_done, rc_done, pn_done = map(
            sem, ("qt_done", "qt_hi", "qt_lo", "sc_done", "sc_min", "ex_done", "rc_done", "pn_done"))
        pt_done, pt_hi, pt_lo, pv_done, y_hi, y_lo, o_done, o_taken = map(
            sem, ("pt_done", "pt_hi", "pt_lo", "pv_done", "y_hi", "y_lo", "o_done", "o_taken"))
        qm_hi, qm_lo, vz_done, q_done, k_done = map(sem, ("qm_hi", "qm_lo", "vz_done", "q_done", "k_done"))
        at1 = {n: sem("at1_" + n) for n in (
            "in_hi", "in_lo", "q_hi", "q_lo", "v_done", "v_hi", "v_lo", "sc_done", "sc_min", "ex_done",
            "rc_done", "pn_done", "pt_done", "pt_hi", "pt_lo", "pv_done", "y_hi", "y_lo", "o_done", "o_taken")}
        lg_done, gate, gate_ex, gate_wt, gate_sb, gate_ld = map(
            sem, ("lg_done", "gate", "gate_ex", "gate_wt", "gate_sb", "gate_ld"))
        gate_pe, half_set = sem("gate_pe"), sem("half_set")
        moe = [{n: sem(f"moe{m}_" + n) for n in (
            "w_hi", "w_lo", "up", "act", "mul", "hi", "lo", "down", "scaled", "added")} for m in range(2)]
        ld_w = [[sem(f"ld_w{m}{p}") for p in range(2)] for m in range(2)]
        ld_g = [[sem(f"ld_g{m}{p}") for p in range(2)] for m in range(2)]
        stored = sem("stored")


        FROM_ONE = {
            "tensor": [pt_done, sc_done, o_done, at1["pt_done"], at1["sc_done"], at1["o_done"], moe[0]["down"], moe[1]["down"]],
            "scalar": [ex_done, at1["ex_done"]],
            "vector": [o_taken, at1["o_taken"]] + [moe[m][n] for m in range(2) for n in ("mul", "lo", "scaled")],
            "gpsimd": [moe[0]["added"], moe[1]["added"]],
        }

        def start_counts(eng, name):
            for s in FROM_ONE[name]:
                eng.sem_inc(s, 1)

        def past(eng, s, n):
            eng.wait_ge(s, n + 1)

        def waits_passed(eng):
            eng.sem_inc(passed, 1)

        def three(pe, out_, lh, ll, rh, rl, start=True, stop=True):
            nc.tensor.matmul(out_, lh, rh, start=start, stop=False)
            nc.tensor.matmul(out_, lh, rl, start=False, stop=False)
            return nc.tensor.matmul(out_, ll, rh, start=False, stop=stop)

        def ln_tensor(pe, k, src, n, ready, mean=True, weights=None):
            w = mean_w if weights is None else weights
            if mean:
                for b in range(B):
                    ready(pe, b)
                    nc.tensor.matmul(PS[:, b, 0:n], w[:], src[:, b, 0:n], start=True, stop=True).then_inc(ln_mean, 1)
            for b in range(B):
                pe.wait_ge(ln_sq, k * B + b + 1)
                nc.tensor.matmul(PS[:, b, 0:n], w[:], sqr[:, b, 0:n], start=True, stop=True).then_inc(ln_var, 1)

        def ln_scalar(act, k, n, hi=False):
            for b in range(B):
                act.wait_ge(ln_cen, k * B + b + 1)
                nc.scalar.activation(sqr[:, b, 0:n], cen[:, b, 0:n], ACT.Square).then_inc(ln_sq, 1)
            for b in range(B):
                act.wait_ge(ln_var, k * B + b + 1)
                nc.scalar.activation(sqr[:, b, 0:n], PS[:, b, 0:n], ACT.Ln, bias=eps[:, 0:1]).then_inc(ln_log, 1)
            for b in range(B):
                act.wait_ge(ln_log, k * B + b + 1)
                nc.scalar.activation(sqr[:, b, 0:n], sqr[:, b, 0:n], ACT.Exp, scale=-0.5).then_inc(ln_rstd, 1)
            if hi:
                for b in range(B):
                    act.wait_ge(ln_norm, k * B + b + 1)
                    nc.scalar.activation(xh[:, b, 0:n], xn[:, b, 0:n], ACT.Copy).then_inc(ln_hi, 1)

        def ln_vector(dve, k, src, n, dst, hi=False, mean=True):
            if mean:
                if k:
                    dve.wait_ge(ln_norm, k * B)
                for b in range(B):
                    dve.wait_ge(ln_mean, LN_MEANS[k] * B + b + 1)
                    nc.vector.tensor_tensor(cen[:, b, 0:n], src[:, b, 0:n], PS[:, b, 0:n], ALU.subtract).then_inc(ln_cen, 1)
            for b in range(B):
                dve.wait_ge(ln_rstd, k * B + b + 1)
                nc.vector.tensor_tensor(dst[:, b, 0:n], cen[:, b, 0:n], sqr[:, b, 0:n], ALU.mult).then_inc(ln_norm, 1)
            if hi:
                base = B * [LN_MOE0, LN_MOE1].index(k)
                for b in range(B):
                    dve.wait_ge(ln_hi, base + b + 1)
                    nc.vector.tensor_tensor(xl[:, b, 0:n], xn[:, b, 0:n], xh[:, b, 0:n].bitcast(F32), ALU.subtract).then_inc(ln_lo, 1)

        LN_MEANS = {LN_CONV: 0, LN_FF: 1, LN_ATT0: 2, LN_MOE0: 3, LN_ATT1: 4, LN_MOE1: 5}
        LN_AFF = {LN_CONV: 0, LN_FF: 1, LN_Q: 2, LN_K: 3}

        def ln_gpsimd(pool, k, n, dst, gamma, beta):
            for b in range(B):
                pool.wait_ge(ln_norm, k * B + b + 1)
                nc.gpsimd.tensor_scalar(dst[:, b, 0:n], dst[:, b, 0:n], gamma, beta, ALU.mult, ALU.add).then_inc(ln_aff, 1)

        def attn_sums_vector(dve, n, s):
            past(dve, s["ex_done"], n + 1)
            nc.vector.reciprocal(small[:, 3:6], small[:, 3:6]).then_inc(s["rc_done"], 1)

        def attn_pt_vector(dve, n, s):
            dve.wait_ge(s["pt_hi"], n + 1)
            nc.vector.tensor_tensor(ptl[:, :, 0:NT], PT, pth[:, :, 0:NT].bitcast(F32), ALU.subtract).then_inc(s["pt_lo"], 1)

        def attn_softmax_vector(dve, n, s):
            past(dve, s["sc_done"], n + 1)
            past(dve, s["ex_done"], n)
            dve.wait_ge(ld_const, 16 * 6)
            waits_passed(dve)
            for i in range(TILES):
                r, c = ROWS[i], S_N[i]
                bank, at = (1, S_AT[i]) if i < 2 else (2, 0)
                mask = causal[0:r, (2 - i) * 128:(2 - i) * 128 + c]
                nc.vector.tensor_tensor_reduce(
                    out=neg_s[0:r, S_AT[i]:S_AT[i] + c], in0=PS[0:r, bank, at:at + c], in1=mask, scale=1.0,
                    scalar=3e38, op0=ALU.add, op1=ALU.min, accum_out=small[0:r, i:i + 1]).then_inc(s["sc_min"], 1)

        def attn_exp_scalar(act, n, s):
            past(act, s["pt_done"], n)
            for i in range(TILES):
                r, c = ROWS[i], S_N[i]
                act.wait_ge(s["sc_min"], n * TILES + i + 1)
                last = nc.scalar.activation(prob[0:r, S_AT[i]:S_AT[i] + c], neg_s[0:r, S_AT[i]:S_AT[i] + c], ACT.Exp,
                                            bias=small[0:r, i:i + 1], scale=-1.0, accum_out=small[0:r, 3 + i:4 + i])
            last.then_inc(s["ex_done"], 1)

        def attn_norm_gpsimd(pool, n, s):
            pool.wait_ge(s["rc_done"], n + 1)
            waits_passed(pool)
            for i in range(TILES):
                r, c = ROWS[i], S_N[i]
                p = prob[0:r, S_AT[i]:S_AT[i] + c]
                last = nc.gpsimd.tensor_scalar(p, p, small[0:r, 3 + i:4 + i], 0.0, ALU.mult, ALU.add)
            last.then_inc(s["pn_done"], 1)

        def attn_transpose_tensor(pe, n, s):
            pe.wait_ge(s["pn_done"], n + 1)
            for i in range(TILES):
                for j in range(i + 1):
                    bank, at = T_AT[j]
                    r = ROWS[i]
                    c = min(128, S_N[i] - 128 * j)
                    o = at + 128 * (i - j)
                    last = nc.tensor.transpose(PS[0:c, 3 + bank, o:o + r],
                                               prob[0:r, S_AT[i] + 128 * j:S_AT[i] + 128 * j + c], ident[0:r, 0:r])
            last.then_inc(s["pt_done"], 1)

        def attn_pv_tensor(pe, bank, lhs_hi, lhs_lo, start=True, stop=True):
            for j in range(TILES):
                tb, at = T_AT[j]
                k = ROWS[j]
                ph, pl = pth[0:k, tb, at:at + T_N[j]], ptl[0:k, tb, at:at + T_N[j]]
                last = three(pe, PS[:, bank, 128 * j:NT], lhs_hi(j, k), lhs_lo(j, k), ph, pl,
                             start=start and j == 0, stop=stop and j == TILES - 1)
            return last

        PT = PS[:, 3:5, 0:NT]

        S0 = dict(sc_done=sc_done, sc_min=sc_min, ex_done=ex_done, rc_done=rc_done, pn_done=pn_done,
                  pt_done=pt_done, pt_hi=pt_hi, pt_lo=pt_lo)


        class Experts:
            def __init__(self, m):
                self.m, self.s = m, moe[m]
                self.gated = m == 0
                self.n_up = 2 if self.gated else 1
                self.count = E0 if m == 0 else E1 + SHARED
                self.cols = self.n_up * FF + FF
                self.loads = 16 * (self.n_up + 1)

            def split_w(self, par, low):
                at = (2 * par + low) * 1536
                return wsplit[:, at:at + self.cols]

            def raw_w(self, par):
                return sqr[:, :, :].rearrange("p b c -> p (b c)")[:, par * 1536:par * 1536 + self.cols]

        UNITS, OUTS = 2 * B * FCH, 2 * B
        MOES = [Experts(0), Experts(1)]
        expert_gates = (frames, hid1)

        def moe_load_sync(sp, q, e, par, done):
            s, raw = q.s, q.raw_w(par)
            if done is not None:
                sp.wait_ge(s["w_lo"], done - 1)
            for u in range(q.n_up):
                src = A[("L0_ffn_W", "L0_ffn_V")[u] if q.gated else "re_w1"]
                sp.dma_start(raw[:, u * FF:(u + 1) * FF],
                             src[bass.ds(e, 1), :, :].rearrange("e d f -> d (e f)")).then_inc(ld_w[q.m][par], 16)
            src = A["L0_ffn_W2" if q.gated else "re_w2"]
            sp.dma_start(raw[:, q.n_up * FF:q.cols].rearrange("p (c d) -> p c d", c=FCH),
                         src[bass.ds(e, 1), :, :].rearrange("e (c p) d -> p (e c) d", p=128)).then_inc(ld_w[q.m][par], 16)
            if done is not None:
                past(sp, s["scaled"], (done - 1) * B)
            sp.dma_start(expert_gates[par][:, :, :].rearrange("p b c -> p (b c)"),
                         A[f"gates{q.m}"][bass.ds(e, 1), :].rearrange("e c -> (e c)").partition_broadcast(D)
                         ).then_inc(ld_g[q.m][par], 16)

        def moe_sync(sp, q):
            sp.wait_ge(gate_sb, q.m + 1)
            n_rows = (E0 if q.gated else E1) * B * TILES
            rows = A[f"gates{q.m}"][0:n_rows // (B * TILES), :].rearrange("e (t c) -> (e t) c", c=128)
            for i in range(-(-n_rows // 128)):
                r = min(128, n_rows - 128 * i)
                sp.dma_start(rows[128 * i:128 * i + r, :], hid2[0:r, i, 0:128]).then_inc(gate_ld, 16)
            if not q.gated:
                for e in range(SHARED):
                    sp.dma_start(A["gates1"][E1 + e, :].rearrange("(b c) -> b c", b=B), hid2[0:B, 6, :]).then_inc(gate_ld, 16)
            sp.wait_ge(gate_ld, 32 if q.gated else 32 + 80)
            moe_load_sync(sp, q, 0, 0, None)
            moe_load_sync(sp, q, 1, 1, None)
            with sp.Fori(0, q.count // 2 - 1) as p:
                for par in range(2):
                    moe_load_sync(sp, q, p * 2 + 2 + par, par, p * 2 + 2 + par)

        def moe_gpsimd(pool, q):
            s = q.s

            def split(n, loads, par, used):
                pool.wait_ge(ld_w[q.m][par], loads * q.loads)
                past(pool, s["down"], used)
                waits_passed(pool)
                nc.gpsimd.tensor_scalar(q.split_w(par, 0), q.raw_w(par), 1.0, 0.0, ALU.mult, ALU.add).then_inc(s["w_hi"], 1)
                pool.wait_ge(s["w_hi"], n + 1)
                nc.gpsimd.tensor_tensor(q.split_w(par, 1), q.raw_w(par), q.split_w(par, 0).bitcast(F32),
                                        ALU.subtract).then_inc(s["w_lo"], 1)

            def add(p, outs):
                for k in outs:
                    past(pool, s["scaled"], p * OUTS + k + 1)
                    if k % B == k:
                        past(pool, s["added"], p * OUTS)
                    else:
                        past(pool, s["added"], p * OUTS + k - B + 1)
                    nc.gpsimd.tensor_tensor(res[:, k % B, 0:NT], res[:, k % B, 0:NT], tt[:, k % 4, 0:NT], ALU.add).then_inc(s["added"], 1)

            split(0, 1, 0, 0)
            split(1, 1, 1, 0)
            with pool.Fori(0, q.count // 2 - 1) as p:
                add(p, range(B))
                split(p * 2 + 2, p + 2, 0, p * UNITS + UNITS // 2)
                add(p, range(B, 2 * B))
                split(p * 2 + 3, p + 2, 1, p * UNITS + UNITS)
            add(q.count // 2 - 1, range(2 * B))

        def moe_tensor(pe, q):
            s = q.s
            with pe.Fori(0, q.count // 2) as p:
                def up(u):
                    par, b, f = u // (B * FCH), u // FCH % B, u % FCH
                    if u % (B * FCH) == 0:
                        pe.wait_ge(s["w_lo"], p * 2 + par + 1)
                    past(pe, s["mul" if q.gated else "lo"], p * UNITS + max(0, u - 2))
                    for k in range(q.n_up):
                        at = k * FF + f * 128
                        last = three(pe, PS[:, 3 * k + u % 3, 0:NT], q.split_w(par, 0)[:, at:at + 128],
                                     q.split_w(par, 1)[:, at:at + 128], xh[:, b, 0:NT], xl[:, b, 0:NT])
                    last.then_inc(s["up"], 1)

                def down(u):
                    par, k, f = u // (B * FCH), u // FCH, u % FCH
                    if f == 0:
                        past(pe, s["scaled"], p * OUTS + max(0, k - 1))
                    past(pe, s["lo"], p * UNITS + u + 1)
                    at = q.n_up * FF + f * 128
                    three(pe, PS[:, 6 + k % 2, 0:NT], q.split_w(par, 0)[:, at:at + 128], q.split_w(par, 1)[:, at:at + 128],
                          workr[:, 2 * (u % 3), 0:NT], workr[:, 2 * (u % 3) + 1, 0:NT],
                          start=f == 0, stop=f == FCH - 1).then_inc(s["down"], 1)

                for u in range(UNITS + 2):
                    if u < UNITS:
                        up(u)
                    if u >= 2:
                        down(u - 2)

        def moe_scalar(act, q):
            s = q.s
            with act.Fori(0, q.count // 2) as p:
                for u in range(UNITS + 1):
                    if u < UNITS:
                        act.wait_ge(s["up"], p * UNITS + u + 1)
                        past(act, s["mul" if q.gated else "lo"], p * UNITS + max(0, u - 2))
                        if q.gated:
                            nc.scalar.activation(workf[:, u % 3, 0:NT], PS[:, u % 3, 0:NT], ACT.Silu).then_inc(s["act"], 1)
                        else:
                            e = p * 2 + u // (B * FCH)
                            waits_passed(act)
                            nc.scalar.activation(workf[:, u % 3, 0:NT], PS[:, u % 3, 0:NT], ACT.Gelu,
                                                 bias=b1col[:, bass.ds(e * FCH + u % FCH, 1)]).then_inc(s["act"], 1)
                    if q.gated and u >= 1:
                        past(act, s["mul"], p * UNITS + u)
                        past(act, s["down"], p * UNITS + max(0, u - 3))
                        nc.scalar.activation(workr[:, 2 * ((u - 1) % 3), 0:NT], workf[:, 3 + (u - 1) % 3, 0:NT],
                                             ACT.Copy).then_inc(s["hi"], 1)

        def moe_vector(dve, q):
            s = q.s
            with dve.Fori(0, q.count // 2) as p:
                def scale(k):
                    past(dve, s["down"], p * UNITS + FCH * (k + 1))
                    past(dve, s["added"], p * OUTS + max(0, k - 3))
                    if k % B == 0:
                        dve.wait_ge(ld_g[q.m][k // B], p * 16 + 16)
                    g = expert_gates[k // B][:, k % B, 0:NT]
                    if q.gated:
                        nc.vector.tensor_tensor(tt[:, k % 4, 0:NT], PS[:, 6 + k % 2, 0:NT], g, ALU.mult).then_inc(s["scaled"], 1)
                    else:
                        nc.vector.scalar_tensor_tensor(
                            out=tt[:, k % 4, 0:NT], in0=PS[:, 6 + k % 2, 0:NT], scalar=b2col[:, bass.ds(p * 2 + k // B, 1)],
                            in1=g, op0=ALU.add, op1=ALU.mult).then_inc(s["scaled"], 1)

                for u in range(UNITS + 1):
                    if q.gated:
                        if u < UNITS:
                            dve.wait_ge(s["act"], p * UNITS + u + 1)
                            past(dve, s["lo"], p * UNITS + max(0, u - 2))
                            nc.vector.tensor_tensor(workf[:, 3 + u % 3, 0:NT], workf[:, u % 3, 0:NT], PS[:, 3 + u % 3, 0:NT],
                                                    ALU.mult).then_inc(s["mul"], 1)
                        if u >= 1:
                            w = u - 1
                            dve.wait_ge(s["hi"], p * UNITS + u)
                            nc.vector.tensor_tensor(workr[:, 2 * (w % 3) + 1, 0:NT], workf[:, 3 + w % 3, 0:NT],
                                                    workr[:, 2 * (w % 3), 0:NT].bitcast(F32), ALU.subtract).then_inc(s["lo"], 1)
                    elif u < UNITS:
                        dve.wait_ge(s["act"], p * UNITS + u + 1)
                        past(dve, s["down"], p * UNITS + max(0, u - 2))
                        nc.vector.tensor_copy(workr[:, 2 * (u % 3), 0:NT], workf[:, u % 3, 0:NT]).then_inc(s["hi"], 1)
                        dve.wait_ge(s["hi"], p * UNITS + u + 1)
                        nc.vector.tensor_tensor(workr[:, 2 * (u % 3) + 1, 0:NT], workf[:, u % 3, 0:NT],
                                                workr[:, 2 * (u % 3), 0:NT].bitcast(F32), ALU.subtract).then_inc(s["lo"], 1)
                    if u >= 6 and (u - 6) % FCH == 0:
                        scale((u - 6) // FCH)
                scale(OUTS - 1)


        def gates_tensor(pe, q, wg, n_exp):
            k = LN_MOE0 if q.gated else LN_MOE1
            pe.wait_ge(ln_norm, (k + 1) * B)
            for t in range(B * TILES):
                b, i = divmod(t, TILES)
                last = nc.tensor.matmul(PS[:, 0, t * n_exp:(t + 1) * n_exp], xn[:, b, 128 * i:128 * i + 128], wg[:], start=True, stop=True)
            last.then_inc(lg_done, 1)
            pe.wait_ge(gate_wt, q.m + 1)
            n = B * TILES * n_exp
            flat = cen[:, :, :].rearrange("p b c -> p (b c)")[:, 7 * ST:7 * ST + n]
            for i in range(-(-n // 128)):
                r = min(128, n - 128 * i)
                last = nc.tensor.transpose(PS[0:r, 1, 128 * i:128 * i + 128], flat[:, 128 * i:128 * i + r], ident[:])
            last.then_inc(gate_pe, 1)

        def gate_views(n_exp):
            n = B * TILES * n_exp
            flat = cen[:, :, :].rearrange("p b c -> p (b c)")
            return [flat[:, j * ST:j * ST + n].rearrange("p (t e) -> p t e", e=n_exp) for j in range(7)] + \
                   [flat[:, 7 * ST:7 * ST + n].rearrange("p (e t) -> p t e", e=n_exp)]

        def gates_scalar(act, q, n_exp):
            base = 0 if q.gated else 1
            val, work, eq, sel, picked, ex, _, _ = gate_views(n_exp)
            if not q.gated:
                act.wait_ge(gate_ex, 2)
                nc.scalar.activation(val, val, ACT.Exp).then_inc(gate_wt_ex, 1)
            act.wait_ge(gate_ex, 1 if q.gated else 3)
            nc.scalar.activation(ex, ex, ACT.Exp).then_inc(gate_wt_ex, 1)

        def gates_vector(dve, q, n_exp, top):
            val, work, eq, sel, picked, ex, _, by_expert = gate_views(n_exp)
            full = [D, B * TILES, n_exp]

            def wide(row):
                return row.unsqueeze(2).to_broadcast(full)

            def link(ins):
                links[0] += 1
                ins.then_inc(gate, 1)
                dve.wait_ge(gate, links[0])

            def row(j):
                return gate_rows[:, j, :]

            dve.wait_ge(lg_done, q.m + 1)
            dve.wait_ge(ln_lo, (q.m + 1) * B)
            link(nc.vector.tensor_copy(val, PS[:, 0, 0:B * TILES * n_exp].rearrange("p (t e) -> p t e", e=n_exp)))
            if not q.gated:
                link(nc.vector.tensor_reduce(out=row(0), in_=val, axis=AX.X, op=ALU.max))
                nc.vector.tensor_tensor(val, val, wide(row(0)), ALU.subtract).then_inc(gate_ex, 1)
                dve.wait_ge(gate_wt_ex, 2)
                link(nc.vector.tensor_reduce(out=row(0), in_=val, axis=AX.X, op=ALU.add))
                link(nc.vector.reciprocal(row(0), row(0)))
                link(nc.vector.tensor_tensor(val, val, wide(row(0)), ALU.mult))
            link(nc.vector.tensor_copy(work, val))
            for k in range(top):
                link(nc.vector.tensor_reduce(out=row(1), in_=work, axis=AX.X, op=ALU.max))
                if k == 0:
                    nc.vector.tensor_tensor(ex, val, wide(row(1)), ALU.subtract).then_inc(gate_ex, 1)
                link(nc.vector.tensor_tensor(eq, work, wide(row(1)), ALU.is_equal))
                link(nc.vector.tensor_tensor(eq, eq, rev_idx[:, 0:n_exp].unsqueeze(1).to_broadcast(full), ALU.mult))
                link(nc.vector.tensor_reduce(out=row(2), in_=eq, axis=AX.X, op=ALU.max))
                link(nc.vector.tensor_tensor(sel, eq, wide(row(2)), ALU.is_equal))
                if k == 0:
                    link(nc.vector.tensor_copy(picked, sel))
                else:
                    link(nc.vector.tensor_tensor(picked, picked, sel, ALU.add))
                link(nc.vector.scalar_tensor_tensor(out=work, in0=sel, scalar=-BIG, in1=work, op0=ALU.mult, op1=ALU.add))
            dve.wait_ge(gate_wt_ex, 1 if q.gated else 3)
            link(nc.vector.tensor_tensor(ex, ex, picked, ALU.mult))
            link(nc.vector.tensor_reduce(out=row(3), in_=ex, axis=AX.X, op=ALU.add))
            link(nc.vector.reciprocal(row(3), row(3)))
            nc.vector.tensor_tensor(by_expert, ex, wide(row(3)), ALU.mult).then_inc(gate_wt, 1)
            if not q.gated:
                link(nc.vector.memset(hid2[0:B, 6, :], 1.0 / SHARED))
            dve.wait_ge(gate_pe, q.m + 1)
            n = B * TILES * n_exp
            last = None
            for i in range(-(-n // 128)):
                r = min(128, n - 128 * i)
                last = nc.vector.tensor_copy(hid2[0:r, i, 0:128], PS[0:r, 1, 128 * i:128 * i + 128])
            last.then_inc(gate_sb, 1)

        links = [0]
        gate_wt_ex = sem("gate_wt_ex")
        gate_rows = sb("gate_rows", [D, 4, B * TILES])


        block = ctx.enter_context(nc.Block())

        @block.sync
        def _(sp):
            def load(dst, src, s):
                sp.dma_start(dst, src).then_inc(s, 16)

            for h, (dst, name) in enumerate(((raw_wq, "wq0"), (raw_wk, "wk0"), (raw_wv, "wv0"), (raw_wu, "wu0"))):
                load(dst, A[name].rearrange("(h e) d -> e h d", h=HEADS), ld_att)
            for j, name in enumerate(("wq1", "wk1", "wv1", "wo1")):
                load(att_raw[:, j, :], A[name], ld_att)
            load(center_w[:], A["center_w"], ld_att)
            load(frames[:, :, 0:T], A["frames"], ld_frames)
            load(w_comp[:], A["w_comp"], ld_tok)
            load(w_main[:], A["w_main"], ld_tok)
            load(w_exp[:], A["w_exp"], ld_tok)
            load(w_ff1[:], A["w_ff1"], ld_tok)
            load(w_ff2[:], A["w_ff2"], ld_tok)
            load(vec[:], A["vec"], ld_tok)
            load(vec64[:], A["vec64"], ld_tok)
            for dst, name in ((ident, "ident"), (mean_w, "mean_w"), (head_w, "head_w"), (causal, "causal"),
                              (head_mask, "head_mask"), (rev_idx, "rev_idx")):
                load(dst[:], A[name], ld_const)
            load(wg0[:], A["wg0"], ld_moe)
            load(wg1[:], A["wg1"], ld_moe)
            load(b1col[:], A["b1col"], ld_moe)
            load(b2col[:], A["b2col"], ld_moe)
            for q in MOES:
                moe_sync(sp, q)
            for b in range(B):
                past(sp, moe[1]["added"], (E1 + SHARED - 1) * B + b + 1)
                sp.dma_start(out[:, b, :], res[:, b, 0:TP]).then_inc(stored, 16)
            sp.wait_ge(stored, 16 * B)

        @block.tensor
        def _(pe):
            start_counts(pe, "tensor")
            pe.wait_ge(ld_att, 16 * 9)
            for h in range(HEADS):
                nc.tensor.matmul(PS[:, h // 4, h % 4 * D:(h % 4 + 1) * D], raw_wq[:, h, :], raw_wk[:, h, :], start=True, stop=True)
            for h in range(HEADS):
                nc.tensor.matmul(PS[:, 2 + h // 4, h % 4 * D:(h % 4 + 1) * D], raw_wv[:, h, :], raw_wu[:, h, :], start=True, stop=True)
            for j in range(2):
                last = nc.tensor.matmul(PS[:, 4, j * D:(j + 1) * D], att_raw[:, j, :], center_w[:], start=True, stop=True)
            last.then_inc(prod_done, 1)

            pe.wait_ge(ld_frames, 16)
            pe.wait_ge(ld_tok, 16 * 7)
            pe.wait_ge(pads_set, 1)
            pe.wait_ge(prod_taken, 3)
            for b in range(B):
                nc.tensor.matmul(PS[0:BN, b, 0:TC], w_comp[:], frames[:, b, 0:TC], start=True, stop=True).then_inc(comp_done, 1)
            for b in range(B):
                pe.wait_ge(comp_act, b + 1)
                for k in range(3):
                    last = nc.tensor.matmul(PS[0:BN, b, 0:TC], w_main[:, k, :], hid1[0:BN, b, k:k + TC], start=k == 0, stop=k == 2)
                last.then_inc(main_done, 1)
            for b in range(B):
                pe.wait_ge(main_act, b + 1)
                nc.tensor.matmul(PS[:, b, 0:TC], w_exp[:], hid2[0:BN, b, 0:TC], start=True, stop=True).then_inc(exp_done, 1)
            pe.wait_ge(ld_const, 16 * 6)
            ln_tensor(pe, LN_CONV, frames, TC, lambda pe, b: pe.wait_ge(exp_sum, b + 1))
            for b in range(B):
                pe.wait_ge(ln_aff, b + 1)
                nc.tensor.matmul(PS[0:BN, b, 0:TC], w_ff1[:], xn[:, b, 0:TC], start=True, stop=True).then_inc(ff1_done, 1)
            for b in range(B):
                pe.wait_ge(ff1_act, b + 1)
                nc.tensor.matmul(PS[:, b, 0:TC], w_ff2[:], hid1[0:BN, b, 0:TC], start=True, stop=True).then_inc(ff2_done, 1)
            ln_tensor(pe, LN_FF, xn, TC, lambda pe, b: pe.wait_ge(ff2_sum, b + 1))

            ln_tensor(pe, LN_ATT0, res, NT, lambda pe, b: pe.wait_ge(pooled, b + 1))
            pe.wait_ge(parts_made, 3)
            with pe.Fori(0, B) as b:
                pe.wait_ge(at_in_f, b + 1)
                for t in range(TILES):
                    last = nc.tensor.transpose(PS[:, 7, 128 * t:128 * t + 128], xb[:, 128 * t:128 * t + 128], ident[:])
                last.then_inc(xt_done, 1)
                pe.wait_ge(at_in_lo, b + 1)

                def project_q(h):
                    three(pe, PS[:, 0, 0:NT], mh[:, h, :], ml[:, h, :], xbh[:, 0:NT], xbl[:, 0:NT]).then_inc(qt_done, 1)

                def scores(h):
                    pe.wait_ge(qt_lo, b * HEADS + h + 1)
                    for i in range(TILES):
                        r, c = ROWS[i], S_N[i]
                        bank, at = (1, S_AT[i]) if i < 2 else (2, 0)
                        last = three(pe, PS[0:r, bank, at:at + c], qh[:, 128 * i:128 * i + r], ql[:, 128 * i:128 * i + r],
                                     xbh[:, 0:c], xbl[:, 0:c])
                    last.then_inc(sc_done, 1)

                def out_project(h):
                    pe.wait_ge(y_lo, b * HEADS + h + 1)
                    if h == 0:
                        past(pe, o_taken, b)
                    last = three(pe, PS[:, 6, 0:NT], nh[:, h, :], nl[:, h, :], yh[:, 0:NT], yl[:, 0:NT],
                                 start=h == 0, stop=h == HEADS - 1)
                    if h == HEADS - 1:
                        last.then_inc(o_done, 1)

                project_q(0)
                scores(0)
                for h in range(HEADS):
                    if h + 1 < HEADS:
                        project_q(h + 1)
                    attn_transpose_tensor(pe, b * HEADS + h, S0)
                    if h + 1 < HEADS:
                        scores(h + 1)
                    if h:
                        out_project(h - 1)
                    pe.wait_ge(pt_lo, b * HEADS + h + 1)
                    if h == 0:
                        pe.wait_ge(xt_lo, b + 1)
                    attn_pv_tensor(pe, 5, lambda j, k: xth[0:k, 128 * j:128 * j + 128],
                                   lambda j, k: xtl[0:k, 128 * j:128 * j + 128]).then_inc(pv_done, 1)
                out_project(HEADS - 1)

            ln_tensor(pe, LN_MOE0, res, NT, lambda pe, b: past(pe, o_taken, B))
            pe.wait_ge(ld_moe, 16 * 4)
            gates_tensor(pe, MOES[0], wg0, E0)
            pe.wait_ge(ln_lo, B)
            moe_tensor(pe, MOES[0])

            ln_tensor(pe, LN_ATT1, res, NT, lambda pe, b: past(pe, moe[0]["added"], (E0 - 1) * B + b + 1))
            for b in range(B):
                pe.wait_ge(ln_norm, LN_ATT1 * B + b + 1)
                nc.tensor.matmul(PS[:, b, 0:NT], a1c[:, 0, :], xn[:, b, 0:NT], start=True, stop=True).then_inc(q_done, 1)
            ln_tensor(pe, LN_Q, None, NT, None, mean=False, weights=head_w)
            for b in range(B):
                pe.wait_ge(ln_log, LN_Q * B + b + 1)
                nc.tensor.matmul(PS[:, b, 0:NT], a1c[:, 1, :], xn[:, b, 0:NT], start=True, stop=True).then_inc(k_done, 1)
            ln_tensor(pe, LN_K, None, NT, None, mean=False, weights=head_w)
            s = at1
            pe.wait_ge(ln_log, (LN_K + 1) * B)
            with pe.Fori(0, B) as b:
                pe.wait_ge(s["in_lo"], b + 1)
                for t in range(TILES):
                    last = three(pe, PS[:, 7, 128 * t:128 * t + 128], xbh[:, 128 * t:128 * t + 128], xbl[:, 128 * t:128 * t + 128],
                                 a1h[:, 0, :], a1l[:, 0, :])
                last.then_inc(s["v_done"], 1)

                def scores1(h):
                    pe.wait_ge(qm_lo, b * HEADS + h + 1)
                    for i in range(TILES):
                        r, c = ROWS[i], S_N[i]
                        bank, at = (1, S_AT[i]) if i < 2 else (2, 0)
                        last = three(pe, PS[0:r, bank, at:at + c], qmh[:, h % 2, 128 * i:128 * i + r],
                                     qml[:, h % 2, 128 * i:128 * i + r], kbh[:, 0:c], kbl[:, 0:c])
                    last.then_inc(s["sc_done"], 1)

                scores1(0)
                for h in range(HEADS):
                    attn_transpose_tensor(pe, b * HEADS + h, s)
                    if h + 1 < HEADS:
                        scores1(h + 1)
                    pe.wait_ge(s["pt_lo"], b * HEADS + h + 1)
                    if h == 0:
                        pe.wait_ge(s["v_lo"], b * TILES + TILES)
                    last = attn_pv_tensor(pe, 6, lambda j, k: vph[0:k, 1024 * j + 128 * h:1024 * j + 128 * h + 128],
                                          lambda j, k: vpl[0:k, 1024 * j + 128 * h:1024 * j + 128 * h + 128],
                                          start=h == 0, stop=h == HEADS - 1)
                last.then_inc(s["pv_done"], 1)
                pe.wait_ge(s["y_lo"], b + 1)
                past(pe, s["o_taken"], b)
                three(pe, PS[:, 5, 0:NT], a1h[:, 1, :], a1l[:, 1, :], yh[:, 0:NT], yl[:, 0:NT]).then_inc(s["o_done"], 1)

            ln_tensor(pe, LN_MOE1, res, NT, lambda pe, b: past(pe, at1["o_taken"], B))
            gates_tensor(pe, MOES[1], wg1, E1)
            pe.wait_ge(ln_lo, 2 * B)
            moe_tensor(pe, MOES[1])

        @block.scalar
        def _(act):
            start_counts(act, "scalar")
            for j, (dst, src) in enumerate(((mh, prod[:, 0:1024]), (nh, prod[:, 1024:2048]))):
                act.wait_ge(prod_taken, j + 1)
                nc.scalar.activation(dst[:, :, :].rearrange("p h d -> p (h d)"), src, ACT.Copy).then_inc(prod_link, 1)
            act.wait_ge(ld_att, 16 * 9)
            nc.scalar.activation(a1h[:, :, :], att_raw[:, 2:4, :], ACT.Copy).then_inc(prod_link, 1)

            act.wait_ge(ld_tok, 16 * 7)
            act.wait_ge(pads_set, 1)
            for b in range(B):
                act.wait_ge(comp_done, b + 1)
                nc.scalar.activation(hid1[0:BN, b, 1:T + 1], PS[0:BN, b, 0:T], ACT.Silu, bias=vec64[:, 0:1]).then_inc(comp_act, 1)
            for b in range(B):
                act.wait_ge(main_done, b + 1)
                nc.scalar.activation(hid2[0:BN, b, 0:TC], PS[0:BN, b, 0:TC], ACT.Silu, bias=vec64[:, 1:2]).then_inc(main_act, 1)
            ln_scalar(act, LN_CONV, TC)
            for b in range(B):
                act.wait_ge(ff1_done, b + 1)
                nc.scalar.activation(hid1[0:BN, b, 0:TC], PS[0:BN, b, 0:TC], ACT.Gelu, bias=vec64[:, 2:3]).then_inc(ff1_act, 1)
            ln_scalar(act, LN_FF, TC)

            ln_scalar(act, LN_ATT0, NT)
            act.wait_ge(ln_norm, (LN_ATT0 + 1) * B)
            with act.Fori(0, B) as b:
                past(act, o_done, b)
                nc.scalar.activation(xbh, xn[:, bass.ds(b, 1), :].rearrange("p b c -> p (b c)"), ACT.Copy).then_inc(at_in_hi, 1)
                act.wait_ge(xt_done, b + 1)
                nc.scalar.activation(xth, PS[:, 7, 0:ST], ACT.Copy).then_inc(xt_hi, 1)

                def query_hi(h):
                    act.wait_ge(qt_done, b * HEADS + h + 1)
                    nc.scalar.activation(qh[:, 0:NT], PS[:, 0, 0:NT], ACT.Copy).then_inc(qt_hi, 1)

                query_hi(0)
                attn_exp_scalar(act, b * HEADS, S0)
                for h in range(HEADS):
                    n = b * HEADS + h
                    if h + 1 < HEADS:
                        query_hi(h + 1)
                    past(act, pt_done, n + 1)
                    nc.scalar.activation(pth[:, :, 0:NT], PT, ACT.Copy).then_inc(pt_hi, 1)
                    if h + 1 < HEADS:
                        attn_exp_scalar(act, n + 1, S0)
                    act.wait_ge(pv_done, n + 1)
                    nc.scalar.activation(yh[:, 0:NT], PS[:, 5, 0:NT], ACT.Copy).then_inc(y_hi, 1)

            ln_scalar(act, LN_MOE0, NT, hi=True)
            gates_scalar(act, MOES[0], E0)
            moe_scalar(act, MOES[0])

            ln_scalar(act, LN_ATT1, NT)
            for k, done in ((LN_Q, q_done), (LN_K, k_done)):
                for b in range(B):
                    act.wait_ge(done, b + 1)
                    act.wait_ge(ln_norm, (k - 1) * B + b + 1)
                    nc.scalar.activation(cen[:, b, 0:NT], PS[:, b, 0:NT], ACT.Copy).then_inc(ln_cen, 1)
                ln_scalar(act, k, NT)
            s = at1
            act.wait_ge(ln_aff, (LN_AFF[LN_K] + 1) * B)
            act.wait_ge(vz_done, 2)
            with act.Fori(0, B) as b:
                past(act, s["o_done"], b)
                for dst, src in ((xbh, xn), (kbh, hid1), (qh, frames)):
                    n = ST if src is xn else NT
                    last = nc.scalar.activation(dst[:, 0:n], src[:, bass.ds(b, 1), 0:n].rearrange("p b c -> p (b c)"), ACT.Copy)
                    last.then_inc(s["in_hi"], 1)
                for t in range(TILES):
                    act.wait_ge(s["v_done"], b + 1)
                    nc.scalar.activation(vph[:, 1024 * t:1024 * t + 1152].rearrange("p (h q) -> p h q", h=HEADS)[:, :, 0:HD1],
                                         PS[:, 7, 128 * t:128 * t + 128].rearrange("p (h i) -> p h i", h=HEADS),
                                         ACT.Copy).then_inc(s["v_hi"], 1)
                attn_exp_scalar(act, b * HEADS, s)
                for h in range(HEADS):
                    n = b * HEADS + h
                    past(act, s["pt_done"], n + 1)
                    nc.scalar.activation(pth[:, :, 0:NT], PT, ACT.Copy).then_inc(s["pt_hi"], 1)
                    if h + 1 < HEADS:
                        attn_exp_scalar(act, n + 1, s)
                act.wait_ge(s["pv_done"], b + 1)
                nc.scalar.activation(yh[:, 0:NT], PS[:, 6, 0:NT], ACT.Copy).then_inc(s["y_hi"], 1)

            ln_scalar(act, LN_MOE1, NT, hi=True)
            gates_scalar(act, MOES[1], E1)
            moe_scalar(act, MOES[1])

        @block.gpsimd
        def _(pool):
            start_counts(pool, "gpsimd")
            pool.wait_ge(ld_tok, 16 * 7)
            ln_gpsimd(pool, LN_CONV, TC, xn, v("g_conv"), v("b_conv"))
            ln_gpsimd(pool, LN_FF, TC, hid2, v("g_ff"), v("b_ff"))
            with pool.Fori(0, B) as b:
                for h in range(HEADS):
                    attn_norm_gpsimd(pool, b * HEADS + h, S0)
            moe_gpsimd(pool, MOES[0])
            pool.wait_ge(prod_taken, 4)
            ln_gpsimd(pool, LN_Q, NT, frames, qaff[:, 0:1], qaff[:, 1:2])
            ln_gpsimd(pool, LN_K, NT, hid1, v("k_gamma"), v("k_beta"))
            s = at1
            with pool.Fori(0, B) as b:
                def mask_q(h):
                    n = b * HEADS + h
                    pool.wait_ge(s["in_lo"], b + 1)
                    past(pool, s["sc_done"], n - 1 if h else n)
                    waits_passed(pool)
                    nc.gpsimd.tensor_scalar(qmh[:, h % 2, 0:NT], qh[:, 0:NT].bitcast(F32), head_mask[:, h:h + 1], 0.0, ALU.mult, ALU.add).then_inc(qm_hi, 1)
                    nc.gpsimd.tensor_scalar(qml[:, h % 2, 0:NT], ql[:, 0:NT].bitcast(F32), head_mask[:, h:h + 1], 0.0, ALU.mult, ALU.add).then_inc(qm_lo, 1)

                mask_q(0)
                for h in range(HEADS):
                    attn_norm_gpsimd(pool, b * HEADS + h, s)
                    if h + 1 < HEADS:
                        mask_q(h + 1)
            moe_gpsimd(pool, MOES[1])

        @block.vector
        def _(dve):
            start_counts(dve, "vector")
            nc.vector.memset(frames[:, :, T:ST], 0.0)
            nc.vector.memset(hid1[:, :, 0:1], 0.0)
            nc.vector.memset(hid1[:, :, T + 1:ST], 0.0)
            nc.vector.memset(small[:], 1.0)
            nc.vector.memset(eps[:], EPS).then_inc(pads_set, 1)
            dve.wait_ge(prod_done, 1)
            nc.vector.tensor_scalar(prod[:, 0:1024], PS[:, 0:2, :].rearrange("p a c -> p (a c)"), -float(D) ** -0.5, None, ALU.mult).then_inc(prod_taken, 1)
            nc.vector.tensor_copy(prod[:, 1024:2048], PS[:, 2:4, :].rearrange("p a c -> p (a c)")).then_inc(prod_taken, 1)
            nc.vector.tensor_copy(a1c[:, :, :].rearrange("p j d -> p (j d)"), PS[:, 4, 0:2 * D]).then_inc(prod_taken, 1)
            for j, (hi, lo, src) in enumerate(((mh, ml, prod[:, 0:1024]), (nh, nl, prod[:, 1024:2048]), (a1h, a1l, None))):
                dve.wait_ge(prod_link, j + 1)
                src = att_raw[:, 2:4, :].rearrange("p h d -> p (h d)") if src is None else src
                nc.vector.tensor_tensor(lo[:, :, :].rearrange("p h d -> p (h d)"), src,
                                        hi[:, :, :].rearrange("p h d -> p (h d)").bitcast(F32), ALU.subtract).then_inc(parts_made, 1)
            dve.wait_ge(ld_tok, 16 * 7)
            nc.vector.tensor_scalar(qaff[:, :], vec[:, VECS.index("q_gamma"):VECS.index("q_gamma") + 2],
                                    -float(HD1) ** -0.5, None, ALU.mult).then_inc(prod_taken, 1)

            for b in range(B):
                dve.wait_ge(exp_done, b + 1)
                nc.vector.scalar_tensor_tensor(out=frames[:, b, 0:TC], in0=PS[:, b, 0:TC], scalar=v("b_expand"),
                                               in1=frames[:, b, 0:TC], op0=ALU.add, op1=ALU.add).then_inc(exp_sum, 1)
            dve.wait_ge(parts_made, 3)
            ln_vector(dve, LN_CONV, frames, TC, xn)
            for b in range(B):
                dve.wait_ge(ff2_done, b + 1)
                nc.vector.scalar_tensor_tensor(out=xn[:, b, 0:TC], in0=PS[:, b, 0:TC], scalar=v("b_ff2"),
                                               in1=xn[:, b, 0:TC], op0=ALU.add, op1=ALU.add).then_inc(ff2_sum, 1)
            ln_vector(dve, LN_FF, xn, TC, hid2)
            for b in range(B):
                dve.wait_ge(ln_aff, B + b + 1)
                nc.vector.tensor_tensor(hid1[:, b, 0:NT], hid2[:, b, 0:NT], hid2[:, b, 1:NT + 1], ALU.max).then_inc(pool_a, 1)
            for b in range(B):
                dve.wait_ge(pool_a, b + 1)
                nc.vector.tensor_tensor(res[:, b, 0:NT], hid1[:, b, 0:NT], hid2[:, b, 2:NT + 2], ALU.max).then_inc(pooled, 1)

            dve.wait_ge(ln_cen, 2 * B)
            nc.vector.memset(xn[:, :, NT:ST], 0.0).then_inc(pads_set, 1)
            ln_vector(dve, LN_ATT0, res, NT, xn)
            dve.wait_ge(ln_norm, (LN_ATT0 + 1) * B)
            dve.wait_ge(pads_set, 2)
            with dve.Fori(0, B) as b:
                past(dve, o_done, b)
                xn_b = xn[:, bass.ds(b, 1), :].rearrange("p b c -> p (b c)")
                nc.vector.tensor_copy(xb, xn_b).then_inc(at_in_f, 1)
                dve.wait_ge(at_in_hi, b + 1)
                nc.vector.tensor_tensor(xbl, xn_b, xbh.bitcast(F32), ALU.subtract).then_inc(at_in_lo, 1)
                dve.wait_ge(xt_hi, b + 1)
                nc.vector.tensor_tensor(xtl, PS[:, 7, 0:ST], xth.bitcast(F32), ALU.subtract).then_inc(xt_lo, 1)

                def query_lo(h):
                    dve.wait_ge(qt_hi, b * HEADS + h + 1)
                    nc.vector.tensor_tensor(ql[:, 0:NT], PS[:, 0, 0:NT], qh[:, 0:NT].bitcast(F32), ALU.subtract).then_inc(qt_lo, 1)

                query_lo(0)
                attn_softmax_vector(dve, b * HEADS, S0)
                attn_sums_vector(dve, b * HEADS, S0)
                for h in range(HEADS):
                    n = b * HEADS + h
                    if h + 1 < HEADS:
                        query_lo(h + 1)
                    attn_pt_vector(dve, n, S0)
                    if h + 1 < HEADS:
                        attn_softmax_vector(dve, n + 1, S0)
                        attn_sums_vector(dve, n + 1, S0)
                    dve.wait_ge(y_hi, n + 1)
                    nc.vector.tensor_tensor(yl[:, 0:NT], PS[:, 5, 0:NT], yh[:, 0:NT].bitcast(F32), ALU.subtract).then_inc(y_lo, 1)
                past(dve, o_done, b + 1)
                res_b = res[:, bass.ds(b, 1), 0:NT].rearrange("p b c -> p (b c)")
                nc.vector.tensor_tensor(res_b, res_b, PS[:, 6, 0:NT], ALU.add).then_inc(o_taken, 1)

            past(dve, o_taken, B)
            ln_vector(dve, LN_MOE0, res, NT, xn, hi=True)
            gates_vector(dve, MOES[0], E0, TOP0)
            moe_vector(dve, MOES[0])

            past(dve, moe[0]["down"], (E0 // 2) * UNITS)
            nc.vector.memset(vph.bitcast(F32), 0.0).then_inc(vz_done, 1)
            nc.vector.memset(vpl.bitcast(F32), 0.0).then_inc(vz_done, 1)
            past(dve, moe[0]["added"], E0 * B)
            ln_vector(dve, LN_ATT1, res, NT, xn)
            ln_vector(dve, LN_Q, None, NT, frames, mean=False)
            ln_vector(dve, LN_K, None, NT, hid1, mean=False)
            dve.wait_ge(vz_done, 2)
            dve.wait_ge(ln_aff, (LN_AFF[LN_K] + 1) * B)
            s = at1
            with dve.Fori(0, B) as b:
                for j, (lo, hi, src) in enumerate(((xbl, xbh, xn), (kbl, kbh, hid1), (ql, qh, frames))):
                    n = ST if src is xn else NT
                    dve.wait_ge(s["in_hi"], b * 3 + j + 1)
                    last = nc.vector.tensor_tensor(lo[:, 0:n], src[:, bass.ds(b, 1), 0:n].rearrange("p b c -> p (b c)"),
                                                   hi[:, 0:n].bitcast(F32), ALU.subtract)
                last.then_inc(s["in_lo"], 1)
                for t in range(TILES):
                    dve.wait_ge(s["v_hi"], b * TILES + TILES)
                    at = slice(1024 * t, 1024 * t + 1152)
                    nc.vector.tensor_tensor(vpl[:, at].rearrange("p (h q) -> p h q", h=HEADS)[:, :, 0:HD1],
                                            PS[:, 7, 128 * t:128 * t + 128].rearrange("p (h i) -> p h i", h=HEADS),
                                            vph[:, at].rearrange("p (h q) -> p h q", h=HEADS)[:, :, 0:HD1].bitcast(F32),
                                            ALU.subtract).then_inc(s["v_lo"], 1)
                attn_softmax_vector(dve, b * HEADS, s)
                attn_sums_vector(dve, b * HEADS, s)
                for h in range(HEADS):
                    n = b * HEADS + h
                    attn_pt_vector(dve, n, s)
                    if h + 1 < HEADS:
                        attn_softmax_vector(dve, n + 1, s)
                        attn_sums_vector(dve, n + 1, s)
                dve.wait_ge(s["y_hi"], b + 1)
                nc.vector.tensor_tensor(yl[:, 0:NT], PS[:, 6, 0:NT], yh[:, 0:NT].bitcast(F32), ALU.subtract).then_inc(s["y_lo"], 1)
                past(dve, s["o_done"], b + 1)
                res_b = res[:, bass.ds(b, 1), 0:NT].rearrange("p b c -> p (b c)")
                nc.vector.scalar_tensor_tensor(out=res_b, in0=PS[:, 5, 0:NT], scalar=v("bo"), in1=res_b,
                                               op0=ALU.add, op1=ALU.add).then_inc(s["o_taken"], 1)

            past(dve, s["o_taken"], B)
            ln_vector(dve, LN_MOE1, res, NT, xn, hi=True)
            gates_vector(dve, MOES[1], E1, TOP1)
            moe_vector(dve, MOES[1])


def kernel(**inputs):
    import concourse.bacc as bacc
    from concourse.bass_utils import run_bass_kernel_spmd

    x = {k: np.asarray(a) for k, a in inputs.items()}

    def t(a):
        return np.ascontiguousarray(a)

    def cols(names):
        return t(np.stack([x[n] if x[n].shape[0] != HD1 else np.tile(x[n], HEADS) for n in names], axis=1))

    part = np.arange(D)
    same_head = (part[:, None] // HD1 == part[None, :] // HD1).astype(np.float32) / HD1
    col = np.arange(ST)
    arrays = {
        "frames": t(x["x"].transpose(2, 0, 1)),
        "w_comp": t(x["L0_tok_w_compress"][:, :, 0].T),
        "w_main": t(x["L0_tok_w_main"].transpose(1, 2, 0)),
        "w_exp": t(x["L0_tok_w_expand"][:, :, 0].T),
        "w_ff1": t(x["L0_tok_w_ff1"].T),
        "w_ff2": t(x["L0_tok_w_ff2"].T),
        "vec": cols(["L0_tok_b_expand", "L0_tok_g_conv_norm", "L0_tok_b_conv_norm", "L0_tok_b_ff2", "L0_tok_g_ff_norm",
                     "L0_tok_b_ff_norm", "L1_attn_bo", "L1_attn_q_gamma", "L1_attn_q_beta", "L1_attn_k_gamma",
                     "L1_attn_k_beta"]),
        "vec64": cols(["L0_tok_b_compress", "L0_tok_b_main", "L0_tok_b_ff1"]),
        "wq0": x["L0_attn_Wq"], "wk0": x["L0_attn_Wk"], "wv0": x["L0_attn_Wv"], "wu0": t(x["L0_attn_Wu"].T),
        "wq1": x["L1_attn_Wq"], "wk1": x["L1_attn_Wk"], "wv1": t(x["L1_attn_Wv"].T), "wo1": t(x["L1_attn_Wo"].T),
        "wg0": x["L0_ffn_Wg"], "wg1": t(x["L1_ffn_gate_w"].T),
        "L0_ffn_W": x["L0_ffn_W"], "L0_ffn_V": x["L0_ffn_V"], "L0_ffn_W2": x["L0_ffn_W2"],
        "re_w1": np.concatenate([x["L1_ffn_re_w1"], x["L1_ffn_se_w1"]]),
        "re_w2": np.concatenate([x["L1_ffn_re_w2"], x["L1_ffn_se_w2"]]),
        "b1col": t(np.concatenate([x["L1_ffn_re_b1"], x["L1_ffn_se_b1"]]).reshape((E1 + SHARED) * FCH, 128).T),
        "b2col": t(np.concatenate([x["L1_ffn_re_b2"], x["L1_ffn_se_b2"]]).T),
        "ident": np.eye(D, dtype=np.float32),
        "mean_w": np.full((D, D), 1.0 / D, np.float32),
        "head_w": same_head,
        "center_w": np.eye(D, dtype=np.float32) - same_head,
        "causal": np.where(col[None, :] - 2 * 128 > part[:, None], np.float32(BIG), np.float32(0)).astype(np.float32),
        "head_mask": (part[:, None] // HD1 == np.arange(HEADS)[None, :]).astype(np.float32),
        "rev_idx": np.tile((E1 - np.arange(E1)).astype(np.float32), (D, 1)),
    }
    nc = bacc.Bacc("TRN2", target_bir_lowering=False, num_devices=1)
    A = {n: nc.dram_tensor("in_" + n, a.shape, F32, kind="ExternalInput").ap() for n, a in arrays.items()}
    A["gates0"] = nc.dram_tensor("gates0", (E0, B * ST), F32, kind="Internal").ap()
    A["gates1"] = nc.dram_tensor("gates1", (E1 + SHARED, B * ST), F32, kind="Internal").ap()
    out = nc.dram_tensor("out", (D, B, TP), F32, kind="ExternalOutput").ap()
    audio_tower(nc, A, out)
    r = run_bass_kernel_spmd(nc, [{"in_" + n: a for n, a in arrays.items()}], core_ids=[0])
    return np.ascontiguousarray(r.results[0]["out"].transpose(1, 2, 0))
```

```python
import numpy as np
import concourse.bass as bass
from concourse import mybir
from contextlib import ExitStack

B, T, D = 8, 375, 128
TP = T - 2
ST = 384
TC = T + 1
NT = TP + 1
TILES = ST // 128
BN = D // 2
HEADS = 8
HD1 = D // HEADS
FF = 512
FCH = FF // 128
E0, TOP0 = 8, 2
E1, TOP1, SHARED = 16, 4, 2
BIG = 1e30
EPS = 1e-5

F32 = mybir.dt.float32
F32R = mybir.dt.float32r
ALU = mybir.AluOpType
ACT = mybir.ActivationFunctionType
AX = mybir.AxisListType

VECS = ["b_expand", "g_conv", "b_conv", "b_ff2", "g_ff", "b_ff", "bo", "q_gamma", "q_beta", "k_gamma", "k_beta"]
LN_CONV, LN_FF, LN_ATT0, LN_MOE0, LN_ATT1, LN_Q, LN_K, LN_MOE1 = range(8)


def audio_tower(nc, A, out):
    ctx = ExitStack()
    with ctx:
        def sb(name, shape, dt=F32):
            return ctx.enter_context(nc.sbuf_tensor(name, shape, dt))

        def sem(name):
            return ctx.enter_context(nc.semaphore(name))

        res = sb("res", [D, B, ST])
        xn = sb("xn", [D, B, ST])
        cen = sb("cen", [D, B, ST])
        sqr = sb("sqr", [D, B, ST])
        frames = sb("frames", [D, B, ST])
        hid1 = sb("hid1", [D, B, ST])
        xh = sb("xh", [D, B, ST], F32R)
        xl = sb("xl", [D, B, ST], F32R)

        ident = sb("ident", [D, D])
        mean_w = sb("mean_w", [D, D])
        head_w = sb("head_w", [D, D])
        center_w = sb("center_w", [D, D])
        causal = sb("causal", [D, ST])
        head_mask = sb("head_mask", [D, HEADS])
        rev_idx = sb("rev_idx", [D, E1])
        vec = sb("vec", [D, len(VECS)])
        vec64 = sb("vec64", [BN, 3])
        eps = sb("eps", [D, 1])
        qaff = sb("qaff", [D, 2])
        w_comp = sb("w_comp", [D, BN])
        w_main = sb("w_main", [BN, 3, BN])
        w_exp = sb("w_exp", [BN, D])
        w_ff1 = sb("w_ff1", [D, BN])
        w_ff2 = sb("w_ff2", [BN, D])
        wg0 = sb("wg0", [D, E0])
        wg1 = sb("wg1", [D, E1])
        b1col = sb("b1col", [D, (E1 + SHARED) * FCH])
        b2col = sb("b2col", [D, E1 + SHARED])
        att_raw = sb("att_raw", [D, 4, D])

        mh = sb("mh", [D, HEADS, D], F32R)
        ml = sb("ml", [D, HEADS, D], F32R)
        nh = sb("nh", [D, HEADS, D], F32R)
        nl = sb("nl", [D, HEADS, D], F32R)
        a1c = sb("a1c", [D, 2, D])
        a1h = sb("a1h", [D, 2, D], F32R)
        a1l = sb("a1l", [D, 2, D], F32R)

        workf = sb("workf", [D, 9, ST])
        workr = sb("workr", [D, 26, ST], F32R)
        wsplit = sb("wsplit", [D, 6400], F32R)
        tt = sb("tt", [D, 4, ST])
        small = sb("small", [D, 4, 6])

        raw_wq = xn[:, :, :].rearrange("p b c -> p (b c)")[:, 0:1024].rearrange("p (h d) -> p h d", h=HEADS)
        raw_wk = xn[:, :, :].rearrange("p b c -> p (b c)")[:, 1024:2048].rearrange("p (h d) -> p h d", h=HEADS)
        raw_wv = xn[:, :, :].rearrange("p b c -> p (b c)")[:, 2048:3072].rearrange("p (h d) -> p h d", h=HEADS)
        raw_wu = cen[:, :, :].rearrange("p b c -> p (b c)")[:, 0:1024].rearrange("p (h d) -> p h d", h=HEADS)
        prod = sqr[:, :, :].rearrange("p b c -> p (b c)")

        neg_s = [workf[:, 2 * k:2 * k + 2, :].rearrange("p a c -> p (a c)") for k in range(2)]
        prob = [workf[:, 4 + 2 * k:6 + 2 * k, :].rearrange("p a c -> p (a c)") for k in range(2)]
        xb = workf[:, 8, :]
        xbh, xbl = [[workr[:, 2 * k + i, :] for k in range(2)] for i in range(2)]
        xth, xtl = [[workr[:, 4 + 2 * k + i, :] for k in range(2)] for i in range(2)]
        kbh, kbl = xth, xtl
        qh, ql = [[workr[:, 8 + 2 * k + i, :] for k in range(2)] for i in range(2)]
        yh, yl = workr[:, 12, :], workr[:, 13, :]
        pth, ptl = [[workr[:, 14 + 4 * k + 2 * i:16 + 4 * k + 2 * i, :] for k in range(2)] for i in range(2)]
        qmh, qml = [[workr[:, 22 + 2 * k + i, :] for k in range(2)] for i in range(2)]
        vph, vpl = wsplit[:, 0:3200], wsplit[:, 3200:6400]

        PS = ctx.enter_context(nc.psum_tensor("PS", [D, 8, 512], F32))

        S_AT = (0, 128, 384)
        S_N = (128, 256, NT)
        ROWS = (128, 128, NT - 256)
        T_AT = ((0, 0), (1, 0), (1, NT - 128))
        T_N = (NT, NT - 128, NT - 256)

        def v(name):
            return vec[:, VECS.index(name):VECS.index(name) + 1]

        ld_const, ld_frames, ld_tok, ld_att, ld_moe = map(sem, ("ld_const", "ld_frames", "ld_tok", "ld_att", "ld_moe"))
        pads_set, passed = sem("pads_set"), sem("passed")
        prod_done, prod_taken, parts_made, prod_link = map(sem, ("prod_done", "prod_taken", "parts_made", "prod_link"))
        comp_done, comp_act, main_done, main_act = map(sem, ("comp_done", "comp_act", "main_done", "main_act"))
        exp_done, exp_sum, ff1_done, ff1_act = map(sem, ("exp_done", "exp_sum", "ff1_done", "ff1_act"))
        ff2_done, ff2_sum, pool_a, pooled = map(sem, ("ff2_done", "ff2_sum", "pool_a", "pooled"))
        ln_mean, ln_cen, ln_sq, ln_var, ln_log, ln_rstd, ln_norm, ln_aff, ln_hi, ln_lo = map(
            sem, ("ln_mean", "ln_cen", "ln_sq", "ln_var", "ln_log", "ln_rstd", "ln_norm", "ln_aff", "ln_hi", "ln_lo"))
        vz_done, q_done, k_done = map(sem, ("vz_done", "q_done", "k_done"))
        AT_SEMS = {"tensor": ("xt_done", "q_done", "sc_done", "pt_done", "pv_done", "o_done"),
                   "scalar": ("in_hi", "xt_hi", "q_hi", "ex_done", "pt_hi", "y_hi"),
                   "vector": ("in_f", "in_lo", "xt_lo", "q_lo", "sc_min", "rc_done", "pt_lo", "y_lo", "o_taken"),
                   "gpsimd": ("pn_done", "qm_done")}
        att = [{n: sem(f"at{m}_{n}") for names in AT_SEMS.values() for n in names} for m in range(2)]
        lg_done, gate, gate_ex, gate_wt, gate_sb, gate_ld = map(
            sem, ("lg_done", "gate", "gate_ex", "gate_wt", "gate_sb", "gate_ld"))
        gate_pe, half_set = sem("gate_pe"), sem("half_set")
        moe = [{n: sem(f"moe{m}_" + n) for n in (
            "w_hi", "w_lo", "up", "act", "mul", "hi", "lo", "down", "scaled", "added")} for m in range(2)]
        ld_w = [[sem(f"ld_w{m}{p}") for p in range(2)] for m in range(2)]
        ld_g = [[sem(f"ld_g{m}{p}") for p in range(2)] for m in range(2)]
        stored = sem("stored")


        FROM_ONE = {"tensor": ("down",), "scalar": (), "vector": ("mul", "lo", "scaled"), "gpsimd": ("added",)}

        def start_counts(eng, name):
            for m in range(2):
                for n in AT_SEMS[name]:
                    eng.sem_inc(att[m][n], 1)
                for n in FROM_ONE[name]:
                    eng.sem_inc(moe[m][n], 1)

        def past(eng, s, n):
            eng.wait_ge(s, n + 1)

        def waits_passed(eng):
            eng.sem_inc(passed, 1)

        def three(pe, out_, lh, ll, rh, rl, start=True, stop=True):
            nc.tensor.matmul(out_, lh, rh, start=start, stop=False)
            nc.tensor.matmul(out_, lh, rl, start=False, stop=False)
            return nc.tensor.matmul(out_, ll, rh, start=False, stop=stop)

        def ln_tensor(pe, k, src, n, ready, mean=True, weights=None):
            w = mean_w if weights is None else weights
            if mean:
                for b in range(B):
                    ready(pe, b)
                    nc.tensor.matmul(PS[:, b, 0:n], w[:], src[:, b, 0:n], start=True, stop=True).then_inc(ln_mean, 1)
            for b in range(B):
                pe.wait_ge(ln_sq, k * B + b + 1)
                nc.tensor.matmul(PS[:, b, 0:n], w[:], sqr[:, b, 0:n], start=True, stop=True).then_inc(ln_var, 1)

        def ln_scalar(act, k, n, hi=False):
            for b in range(B):
                act.wait_ge(ln_cen, k * B + b + 1)
                nc.scalar.activation(sqr[:, b, 0:n], cen[:, b, 0:n], ACT.Square).then_inc(ln_sq, 1)
            for b in range(B):
                act.wait_ge(ln_var, k * B + b + 1)
                nc.scalar.activation(sqr[:, b, 0:n], PS[:, b, 0:n], ACT.Ln, bias=eps[:, 0:1]).then_inc(ln_log, 1)
            for b in range(B):
                act.wait_ge(ln_log, k * B + b + 1)
                nc.scalar.activation(sqr[:, b, 0:n], sqr[:, b, 0:n], ACT.Exp, scale=-0.5).then_inc(ln_rstd, 1)
            if hi:
                for b in range(B):
                    act.wait_ge(ln_norm, k * B + b + 1)
                    nc.scalar.activation(xh[:, b, 0:n], xn[:, b, 0:n], ACT.Copy).then_inc(ln_hi, 1)

        def ln_vector(dve, k, src, n, dst, hi=False, mean=True):
            if mean:
                if k:
                    dve.wait_ge(ln_norm, k * B)
                for b in range(B):
                    dve.wait_ge(ln_mean, LN_MEANS[k] * B + b + 1)
                    nc.vector.tensor_tensor(cen[:, b, 0:n], src[:, b, 0:n], PS[:, b, 0:n], ALU.subtract).then_inc(ln_cen, 1)
            for b in range(B):
                dve.wait_ge(ln_rstd, k * B + b + 1)
                nc.vector.tensor_tensor(dst[:, b, 0:n], cen[:, b, 0:n], sqr[:, b, 0:n], ALU.mult).then_inc(ln_norm, 1)
            if hi:
                base = B * [LN_MOE0, LN_MOE1].index(k)
                for b in range(B):
                    dve.wait_ge(ln_hi, base + b + 1)
                    nc.vector.tensor_tensor(xl[:, b, 0:n], xn[:, b, 0:n], xh[:, b, 0:n].bitcast(F32), ALU.subtract).then_inc(ln_lo, 1)

        LN_MEANS = {LN_CONV: 0, LN_FF: 1, LN_ATT0: 2, LN_MOE0: 3, LN_ATT1: 4, LN_MOE1: 5}
        LN_AFF = {LN_CONV: 0, LN_FF: 1, LN_Q: 2, LN_K: 3}

        def ln_gpsimd(pool, k, n, dst, gamma, beta):
            for b in range(B):
                pool.wait_ge(ln_norm, k * B + b + 1)
                nc.gpsimd.tensor_scalar(dst[:, b, 0:n], dst[:, b, 0:n], gamma, beta, ALU.mult, ALU.add).then_inc(ln_aff, 1)


        class At:
            def __init__(self, p, c):
                self.p, self.c = p, c
                self.n = c if p is None else p * (2 * HEADS) + c
                self.h, self.clip_par, self.par = c % HEADS, c // HEADS % 2, c % 2
                self.b = c // HEADS if p is None else p * 2 + c // HEADS
                self.live = p is not None or 0 <= c < B * HEADS
                self.stat = small[:, c % 4, :]

            def __add__(self, k):
                return At(self.p, self.c + k)

            def last_of_clip(self):
                return self.live and self.h == HEADS - 1

            def next_clip(self):
                nxt = self + 3
                return nxt if self.h == HEADS - 3 and nxt.live else None

        def slots(eng, slot):
            for i in range(-3, 3):
                slot(At(None, i))
            with eng.Fori(0, B // 2 - 1) as p:
                for i in range(3, 3 + 2 * HEADS):
                    slot(At(p, i))
            for i in range((B - 2) * HEADS + 3, B * HEADS + 4):
                slot(At(None, i))

        def bank_of(i):
            return (1, S_AT[i]) if i < 2 else (2, 0)

        def clip_of(t, at, n=NT):
            if isinstance(at.b, int):
                return t[:, at.b, 0:n]
            return t[:, bass.ds(at.b, 1), 0:n].rearrange("p b c -> p (b c)")

        def attention_tensor(pe, m):
            s = att[m]

            def turn_clip(at):
                past(pe, s["xt_lo"], at.b)
                par = at.clip_par
                if m == 0:
                    past(pe, s["in_f"], at.b + 1)
                    for t in range(TILES):
                        last = nc.tensor.transpose(PS[:, 7, 128 * t:128 * t + 128], xb[:, 128 * t:128 * t + 128], ident[:])
                else:
                    past(pe, s["in_lo"], at.b + 1)
                    for t in range(TILES):
                        c = slice(128 * t, 128 * t + 128)
                        last = three(pe, PS[:, 7, c], xbh[par][:, c], xbl[par][:, c], a1h[:, 0, :], a1l[:, 0, :])
                last.then_inc(s["xt_done"], 1)

            def project_q(at):
                if at.h == 0:
                    past(pe, s["in_lo"], at.b + 1)
                past(pe, s["q_lo"], at.n)
                x = xbh[at.clip_par][:, 0:NT], xbl[at.clip_par][:, 0:NT]
                three(pe, PS[:, 0, 0:NT], mh[:, at.h, :], ml[:, at.h, :], *x).then_inc(s["q_done"], 1)

            def scores(at):
                if m == 0:
                    past(pe, s["q_lo"], at.n + 1)
                    q, k = (qh[at.par], ql[at.par]), (xbh[at.clip_par], xbl[at.clip_par])
                else:
                    past(pe, s["qm_done"], at.n + 1)
                    q, k = (qmh[at.par], qml[at.par]), (kbh[at.clip_par], kbl[at.clip_par])
                past(pe, s["sc_min"], at.n)
                for i in range(TILES):
                    r, c = ROWS[i], S_N[i]
                    bank, col = bank_of(i)
                    last = three(pe, PS[0:r, bank, col:col + c], q[0][:, 128 * i:128 * i + r], q[1][:, 128 * i:128 * i + r],
                                 k[0][:, 0:c], k[1][:, 0:c])
                last.then_inc(s["sc_done"], 1)

            def transpose(at):
                past(pe, s["pn_done"], at.n + 1)
                past(pe, s["pt_lo"], at.n)
                for i in range(TILES):
                    for j in range(i + 1):
                        bank, col = T_AT[j]
                        r, c = ROWS[i], min(128, S_N[i] - 128 * j)
                        o = col + 128 * (i - j)
                        last = nc.tensor.transpose(PS[0:c, 3 + bank, o:o + r],
                                                   prob[at.par][0:r, S_AT[i] + 128 * j:S_AT[i] + 128 * j + c], ident[0:r, 0:r])
                last.then_inc(s["pt_done"], 1)

            def values(at):
                past(pe, s["pt_lo"], at.n + 1)
                if at.h == 0:
                    past(pe, s["xt_lo"], at.b + 1)
                if m == 0:
                    past(pe, s["y_lo"], at.n)
                    bank, first, final = 5, True, True
                else:
                    bank, first, final = (6, 0)[at.clip_par], at.h == 0, at.h == HEADS - 1
                    if first and at.c >= 2 * HEADS or first and at.p is not None:
                        past(pe, s["y_lo"], at.b - 1)
                for j in range(TILES):
                    tb, col = T_AT[j]
                    k = ROWS[j]
                    if m == 0:
                        v_ = xth[at.clip_par][0:k, 128 * j:128 * j + 128], xtl[at.clip_par][0:k, 128 * j:128 * j + 128]
                    else:
                        c = 1024 * j + 128 * at.h
                        v_ = vph[0:k, c:c + 128], vpl[0:k, c:c + 128]
                    last = three(pe, PS[:, bank, 128 * j:NT], *v_, pth[at.par][0:k, tb, col:col + T_N[j]],
                                 ptl[at.par][0:k, tb, col:col + T_N[j]], start=first and j == 0, stop=final and j == TILES - 1)
                if final:
                    last.then_inc(s["pv_done"], 1)

            def project_out(at):
                if m == 0:
                    past(pe, s["y_lo"], at.n + 1)
                    if at.h == 0:
                        past(pe, s["o_taken"], at.b)
                    last = three(pe, PS[:, 6, 0:NT], nh[:, at.h, :], nl[:, at.h, :], yh[:, 0:NT], yl[:, 0:NT],
                                 start=at.h == 0, stop=at.h == HEADS - 1)
                    if at.h == HEADS - 1:
                        last.then_inc(s["o_done"], 1)
                elif at.h == HEADS - 1:
                    past(pe, s["y_lo"], at.b + 1)
                    past(pe, s["o_taken"], at.b)
                    three(pe, PS[:, 5, 0:NT], a1h[:, 1, :], a1l[:, 1, :], yh[:, 0:NT], yl[:, 0:NT]).then_inc(s["o_done"], 1)

            def slot(i):
                if i.c == -3 and i.p is None:
                    turn_clip(i + 3)
                nxt = (i + 3).live and (i + 3).next_clip()
                if nxt:
                    turn_clip(nxt)
                if (i + 3).live and m == 0:
                    project_q(i + 3)
                if (i + 2).live:
                    scores(i + 2)
                if i.live:
                    transpose(i)
                if (i + -2).live:
                    project_out(i + -2)
                if (i + -1).live:
                    values(i + -1)

            slots(pe, slot)

        def attention_scalar(act, m):
            s = att[m]

            def fetch(at):
                if at.c >= 2 * HEADS or at.p is not None:
                    past(act, s["o_done"], at.b - 1)
                par = at.clip_par
                for dst, src in ((xbh, xn),) if m == 0 else ((xbh, xn), (kbh, hid1), (qh, frames)):
                    n = ST if src is xn else NT
                    nc.scalar.activation(dst[par][:, 0:n], clip_of(src, at, n), ACT.Copy).then_inc(s["in_hi"], 1)

            def turned_hi(at):
                past(act, s["xt_done"], at.b + 1)
                if m == 0:
                    nc.scalar.activation(xth[at.clip_par], PS[:, 7, 0:ST], ACT.Copy).then_inc(s["xt_hi"], 1)
                    return
                past(act, s["pv_done"], at.b)
                for t in range(TILES):
                    last = nc.scalar.activation(
                        vph[:, 1024 * t:1024 * t + 1152].rearrange("p (h q) -> p h q", h=HEADS)[:, :, 0:HD1],
                        PS[:, 7, 128 * t:128 * t + 128].rearrange("p (h i) -> p h i", h=HEADS), ACT.Copy)
                last.then_inc(s["xt_hi"], 1)

            def slot(i):
                if i.c == -3 and i.p is None:
                    fetch(i + 3)
                    turned_hi(i + 3)
                nxt = (i + 3).live and (i + 3).next_clip()
                if nxt:
                    fetch(nxt)
                    if m == 0:
                        turned_hi(nxt)
                if m == 1 and i.live and i.h == 0 and i.c > 0:
                    turned_hi(i)
                a = i + 3
                if a.live and m == 0:
                    past(act, s["q_done"], a.n + 1)
                    if a.p is not None or a.c >= 2:
                        past(act, s["sc_done"], a.n - 1)
                    nc.scalar.activation(qh[a.par][:, 0:NT], PS[:, 0, 0:NT], ACT.Copy).then_inc(s["q_hi"], 1)
                if i.live:
                    past(act, s["pt_done"], i.n + 1)
                    nc.scalar.activation(pth[i.par][:, :, 0:NT], PT, ACT.Copy).then_inc(s["pt_hi"], 1)
                a = i + 2
                if a.live:
                    if a.p is not None or a.c >= 2:
                        past(act, s["pt_done"], a.n - 1)
                    for t in range(TILES):
                        r, c = ROWS[t], slice(S_AT[t], S_AT[t] + S_N[t])
                        past(act, s["sc_min"], a.n + 1)
                        last = nc.scalar.activation(prob[a.par][0:r, c], neg_s[a.par][0:r, c], ACT.Exp, bias=a.stat[0:r, t:t + 1],
                                                    scale=-1.0, accum_out=a.stat[0:r, 3 + t:4 + t])
                    last.then_inc(s["ex_done"], 1)
                a = i + -1
                if a.live and m == 0 or a.last_of_clip():
                    past(act, s["pv_done"], (a.n if m == 0 else a.b) + 1)
                    if m == 1 and (a.p is not None or a.c >= HEADS):
                        past(act, s["o_done"], a.b)
                    bank = 5 if m == 0 else (6, 0)[a.clip_par]
                    nc.scalar.activation(yh[:, 0:NT], PS[:, bank, 0:NT], ACT.Copy).then_inc(s["y_hi"], 1)

            slots(act, slot)

        def attention_vector(dve, m):
            s = att[m]

            def less(out_, a, hi):
                return nc.vector.tensor_tensor(out_, a, hi.bitcast(F32), ALU.subtract)

            def fetch(at):
                par = at.clip_par
                if m == 0:
                    past(dve, s["xt_done"], at.b)
                    nc.vector.tensor_copy(xb, clip_of(xn, at, ST)).then_inc(s["in_f"], 1)
                both = ((xbl, xbh, xn),) if m == 0 else ((xbl, xbh, xn), (kbl, kbh, hid1), (ql, qh, frames))
                for j, (lo, hi, src) in enumerate(both):
                    n = ST if src is xn else NT
                    past(dve, s["in_hi"], at.b * len(both) + j + 1)
                    last = less(lo[par][:, 0:n], clip_of(src, at, n), hi[par][:, 0:n])
                last.then_inc(s["in_lo"], 1)

            def turned_lo(at):
                past(dve, s["xt_hi"], at.b + 1)
                if m == 0:
                    less(xtl[at.clip_par], PS[:, 7, 0:ST], xth[at.clip_par]).then_inc(s["xt_lo"], 1)
                    return
                for t in range(TILES):
                    c = slice(1024 * t, 1024 * t + 1152)
                    last = less(vpl[:, c].rearrange("p (h q) -> p h q", h=HEADS)[:, :, 0:HD1],
                                PS[:, 7, 128 * t:128 * t + 128].rearrange("p (h i) -> p h i", h=HEADS),
                                vph[:, c].rearrange("p (h q) -> p h q", h=HEADS)[:, :, 0:HD1])
                last.then_inc(s["xt_lo"], 1)

            def add_up(at):
                past(dve, s["o_done"], at.b + 1)
                r = clip_of(res, at)
                if m == 0:
                    nc.vector.tensor_tensor(r, r, PS[:, 6, 0:NT], ALU.add).then_inc(s["o_taken"], 1)
                else:
                    nc.vector.scalar_tensor_tensor(out=r, in0=PS[:, 5, 0:NT], scalar=v("bo"), in1=r,
                                                   op0=ALU.add, op1=ALU.add).then_inc(s["o_taken"], 1)

            def slot(i):
                if i.c == -3 and i.p is None:
                    fetch(i + 3)
                    turned_lo(i + 3)
                nxt = (i + 3).live and (i + 3).next_clip()
                if nxt:
                    fetch(nxt)
                    if m == 0:
                        turned_lo(nxt)
                if m == 1 and i.live and i.h == 0 and i.c > 0:
                    turned_lo(i)
                a = i + 1
                if a.live:
                    past(dve, s["ex_done"], a.n + 1)
                    nc.vector.reciprocal(a.stat[:, 3:6], a.stat[:, 3:6]).then_inc(s["rc_done"], 1)
                a = i + 3
                if a.live and m == 0:
                    past(dve, s["q_hi"], a.n + 1)
                    less(ql[a.par][:, 0:NT], PS[:, 0, 0:NT], qh[a.par][:, 0:NT]).then_inc(s["q_lo"], 1)
                a = i + -2
                if a.live and m == 0 or a.last_of_clip():
                    past(dve, s["y_hi"], (a.n if m == 0 else a.b) + 1)
                    bank = 5 if m == 0 else (6, 0)[a.clip_par]
                    less(yl[:, 0:NT], PS[:, bank, 0:NT], yh[:, 0:NT]).then_inc(s["y_lo"], 1)
                a = i + 2
                if a.live:
                    past(dve, s["sc_done"], a.n + 1)
                    if a.p is not None or a.c >= 2:
                        past(dve, s["ex_done"], a.n - 1)
                    if a.p is not None or a.c >= 4:
                        past(dve, s["pn_done"], a.n - 3)
                    waits_passed(dve)
                    for t in range(TILES):
                        r, n = ROWS[t], S_N[t]
                        bank, col = bank_of(t)
                        last = nc.vector.tensor_tensor_reduce(
                            out=neg_s[a.par][0:r, S_AT[t]:S_AT[t] + n], in0=PS[0:r, bank, col:col + n],
                            in1=causal[0:r, (2 - t) * 128:(2 - t) * 128 + n], scale=1.0, scalar=3e38,
                            op0=ALU.add, op1=ALU.min, accum_out=a.stat[0:r, t:t + 1])
                    last.then_inc(s["sc_min"], 1)
                if i.live:
                    past(dve, s["pt_hi"], i.n + 1)
                    less(ptl[i.par][:, :, 0:NT], PT, pth[i.par][:, :, 0:NT]).then_inc(s["pt_lo"], 1)
                a = i + -3
                if a.last_of_clip():
                    add_up(a)

            slots(dve, slot)

        def attention_gpsimd(pool, m):
            s = att[m]

            def slot(i):
                a = i + 1
                if a.live:
                    past(pool, s["rc_done"], a.n + 1)
                    waits_passed(pool)
                    for t in range(TILES):
                        r = ROWS[t]
                        p_ = prob[a.par][0:r, S_AT[t]:S_AT[t] + S_N[t]]
                        last = nc.gpsimd.tensor_scalar(p_, p_, a.stat[0:r, 3 + t:4 + t], 0.0, ALU.mult, ALU.add)
                    last.then_inc(s["pn_done"], 1)
                a = i + 3
                if a.live and m == 1:
                    if a.h == 0:
                        past(pool, s["in_lo"], a.b + 1)
                    if a.p is not None or a.c >= 2:
                        past(pool, s["sc_done"], a.n - 1)
                    waits_passed(pool)
                    mask = head_mask[:, a.h:a.h + 1]
                    for dst, src in ((qmh, qh), (qml, ql)):
                        last = nc.gpsimd.tensor_scalar(dst[a.par][:, 0:NT], src[a.clip_par][:, 0:NT].bitcast(F32), mask, 0.0,
                                                       ALU.mult, ALU.add)
                    last.then_inc(s["qm_done"], 1)

            slots(pool, slot)

        PT = PS[:, 3:5, 0:NT]


        class Experts:
            def __init__(self, m):
                self.m, self.s = m, moe[m]
                self.gated = m == 0
                self.n_up = 2 if self.gated else 1
                self.count = E0 if m == 0 else E1 + SHARED
                self.cols = self.n_up * FF + FF
                self.loads = 16 * (self.n_up + 1)

            def split_w(self, par, low):
                at = (2 * par + low) * 1536
                return wsplit[:, at:at + self.cols]

            def raw_w(self, par):
                return sqr[:, :, :].rearrange("p b c -> p (b c)")[:, par * 1536:par * 1536 + self.cols]

        UNITS, OUTS = 2 * B * FCH, 2 * B
        MOES = [Experts(0), Experts(1)]
        expert_gates = (frames, hid1)

        def moe_load_sync(sp, q, e, par, done):
            s, raw = q.s, q.raw_w(par)
            if done is not None:
                sp.wait_ge(s["w_lo"], done - 1)
            for u in range(q.n_up):
                src = A[("L0_ffn_W", "L0_ffn_V")[u] if q.gated else "re_w1"]
                sp.dma_start(raw[:, u * FF:(u + 1) * FF],
                             src[bass.ds(e, 1), :, :].rearrange("e d f -> d (e f)")).then_inc(ld_w[q.m][par], 16)
            src = A["L0_ffn_W2" if q.gated else "re_w2"]
            sp.dma_start(raw[:, q.n_up * FF:q.cols].rearrange("p (c d) -> p c d", c=FCH),
                         src[bass.ds(e, 1), :, :].rearrange("e (c p) d -> p (e c) d", p=128)).then_inc(ld_w[q.m][par], 16)
            if done is not None:
                past(sp, s["scaled"], (done - 1) * B)
            sp.dma_start(expert_gates[par][:, :, :].rearrange("p b c -> p (b c)"),
                         A[f"gates{q.m}"][bass.ds(e, 1), :].rearrange("e c -> (e c)").partition_broadcast(D)
                         ).then_inc(ld_g[q.m][par], 16)

        def moe_sync(sp, q):
            sp.wait_ge(gate_sb, q.m + 1)
            n_rows = (E0 if q.gated else E1) * B * TILES
            rows = A[f"gates{q.m}"][0:n_rows // (B * TILES), :].rearrange("e (t c) -> (e t) c", c=128)
            for i in range(-(-n_rows // 128)):
                r = min(128, n_rows - 128 * i)
                sp.dma_start(rows[128 * i:128 * i + r, :], hid1[0:r, i, 0:128]).then_inc(gate_ld, 16)
            if not q.gated:
                for e in range(SHARED):
                    sp.dma_start(A["gates1"][E1 + e, :].rearrange("(b c) -> b c", b=B), hid1[0:B, 6, :]).then_inc(gate_ld, 16)
            sp.wait_ge(gate_ld, 32 if q.gated else 32 + 80)
            moe_load_sync(sp, q, 0, 0, None)
            moe_load_sync(sp, q, 1, 1, None)
            with sp.Fori(0, q.count // 2 - 1) as p:
                for par in range(2):
                    moe_load_sync(sp, q, p * 2 + 2 + par, par, p * 2 + 2 + par)

        def moe_gpsimd(pool, q):
            s = q.s

            def split(n, loads, par, used):
                pool.wait_ge(ld_w[q.m][par], loads * q.loads)
                past(pool, s["down"], used)
                waits_passed(pool)
                nc.gpsimd.tensor_scalar(q.split_w(par, 0), q.raw_w(par), 1.0, 0.0, ALU.mult, ALU.add).then_inc(s["w_hi"], 1)
                pool.wait_ge(s["w_hi"], n + 1)
                nc.gpsimd.tensor_tensor(q.split_w(par, 1), q.raw_w(par), q.split_w(par, 0).bitcast(F32),
                                        ALU.subtract).then_inc(s["w_lo"], 1)

            def add(p, outs):
                for k in outs:
                    past(pool, s["scaled"], p * OUTS + k + 1)
                    if k % B == k:
                        past(pool, s["added"], p * OUTS)
                    else:
                        past(pool, s["added"], p * OUTS + k - B + 1)
                    nc.gpsimd.tensor_tensor(res[:, k % B, 0:NT], res[:, k % B, 0:NT], tt[:, k % 4, 0:NT], ALU.add).then_inc(s["added"], 1)

            split(0, 1, 0, 0)
            split(1, 1, 1, 0)
            with pool.Fori(0, q.count // 2 - 1) as p:
                add(p, range(B))
                split(p * 2 + 2, p + 2, 0, p * UNITS + UNITS // 2)
                add(p, range(B, 2 * B))
                split(p * 2 + 3, p + 2, 1, p * UNITS + UNITS)
            add(q.count // 2 - 1, range(2 * B))

        def moe_tensor(pe, q):
            s = q.s
            with pe.Fori(0, q.count // 2) as p:
                def up(u):
                    par, b, f = u // (B * FCH), u // FCH % B, u % FCH
                    if u % (B * FCH) == 0:
                        pe.wait_ge(s["w_lo"], p * 2 + par + 1)
                    past(pe, s["mul" if q.gated else "lo"], p * UNITS + max(0, u - 2))
                    for k in range(q.n_up):
                        at = k * FF + f * 128
                        last = three(pe, PS[:, 3 * k + u % 3, 0:NT], q.split_w(par, 0)[:, at:at + 128],
                                     q.split_w(par, 1)[:, at:at + 128], xh[:, b, 0:NT], xl[:, b, 0:NT])
                    last.then_inc(s["up"], 1)

                def down(u):
                    par, k, f = u // (B * FCH), u // FCH, u % FCH
                    if f == 0:
                        past(pe, s["scaled"], p * OUTS + max(0, k - 1))
                    past(pe, s["lo"], p * UNITS + u + 1)
                    at = q.n_up * FF + f * 128
                    three(pe, PS[:, 6 + k % 2, 0:NT], q.split_w(par, 0)[:, at:at + 128], q.split_w(par, 1)[:, at:at + 128],
                          workr[:, 2 * (u % 3), 0:NT], workr[:, 2 * (u % 3) + 1, 0:NT],
                          start=f == 0, stop=f == FCH - 1).then_inc(s["down"], 1)

                for u in range(UNITS + 2):
                    if u < UNITS:
                        up(u)
                    if u >= 2:
                        down(u - 2)

        def moe_scalar(act, q):
            s = q.s
            with act.Fori(0, q.count // 2) as p:
                for u in range(UNITS + 1):
                    if u < UNITS:
                        act.wait_ge(s["up"], p * UNITS + u + 1)
                        past(act, s["mul" if q.gated else "lo"], p * UNITS + max(0, u - 2))
                        if q.gated:
                            nc.scalar.activation(workf[:, u % 3, 0:NT], PS[:, u % 3, 0:NT], ACT.Silu).then_inc(s["act"], 1)
                        else:
                            e = p * 2 + u // (B * FCH)
                            waits_passed(act)
                            nc.scalar.activation(workf[:, u % 3, 0:NT], PS[:, u % 3, 0:NT], ACT.Gelu,
                                                 bias=b1col[:, bass.ds(e * FCH + u % FCH, 1)]).then_inc(s["act"], 1)
                    if q.gated and u >= 1:
                        past(act, s["mul"], p * UNITS + u)
                        past(act, s["down"], p * UNITS + max(0, u - 3))
                        nc.scalar.activation(workr[:, 2 * ((u - 1) % 3), 0:NT], workf[:, 3 + (u - 1) % 3, 0:NT],
                                             ACT.Copy).then_inc(s["hi"], 1)

        def moe_vector(dve, q):
            s = q.s
            with dve.Fori(0, q.count // 2) as p:
                def scale(k):
                    past(dve, s["down"], p * UNITS + FCH * (k + 1))
                    past(dve, s["added"], p * OUTS + max(0, k - 3))
                    if k % B == 0:
                        dve.wait_ge(ld_g[q.m][k // B], p * 16 + 16)
                    g = expert_gates[k // B][:, k % B, 0:NT]
                    if q.gated:
                        nc.vector.tensor_tensor(tt[:, k % 4, 0:NT], PS[:, 6 + k % 2, 0:NT], g, ALU.mult).then_inc(s["scaled"], 1)
                    else:
                        nc.vector.scalar_tensor_tensor(
                            out=tt[:, k % 4, 0:NT], in0=PS[:, 6 + k % 2, 0:NT], scalar=b2col[:, bass.ds(p * 2 + k // B, 1)],
                            in1=g, op0=ALU.add, op1=ALU.mult).then_inc(s["scaled"], 1)

                for u in range(UNITS + 1):
                    if q.gated:
                        if u < UNITS:
                            dve.wait_ge(s["act"], p * UNITS + u + 1)
                            past(dve, s["lo"], p * UNITS + max(0, u - 2))
                            nc.vector.tensor_tensor(workf[:, 3 + u % 3, 0:NT], workf[:, u % 3, 0:NT], PS[:, 3 + u % 3, 0:NT],
                                                    ALU.mult).then_inc(s["mul"], 1)
                        if u >= 1:
                            w = u - 1
                            dve.wait_ge(s["hi"], p * UNITS + u)
                            nc.vector.tensor_tensor(workr[:, 2 * (w % 3) + 1, 0:NT], workf[:, 3 + w % 3, 0:NT],
                                                    workr[:, 2 * (w % 3), 0:NT].bitcast(F32), ALU.subtract).then_inc(s["lo"], 1)
                    elif u < UNITS:
                        dve.wait_ge(s["act"], p * UNITS + u + 1)
                        past(dve, s["down"], p * UNITS + max(0, u - 2))
                        nc.vector.tensor_copy(workr[:, 2 * (u % 3), 0:NT], workf[:, u % 3, 0:NT]).then_inc(s["hi"], 1)
                        dve.wait_ge(s["hi"], p * UNITS + u + 1)
                        nc.vector.tensor_tensor(workr[:, 2 * (u % 3) + 1, 0:NT], workf[:, u % 3, 0:NT],
                                                workr[:, 2 * (u % 3), 0:NT].bitcast(F32), ALU.subtract).then_inc(s["lo"], 1)
                    if u >= 6 and (u - 6) % FCH == 0:
                        scale((u - 6) // FCH)
                scale(OUTS - 1)


        def gates_tensor(pe, q, wg, n_exp):
            k = LN_MOE0 if q.gated else LN_MOE1
            pe.wait_ge(ln_norm, (k + 1) * B)
            for t in range(B * TILES):
                b, i = divmod(t, TILES)
                last = nc.tensor.matmul(PS[:, 0, t * n_exp:(t + 1) * n_exp], xn[:, b, 128 * i:128 * i + 128], wg[:], start=True, stop=True)
            last.then_inc(lg_done, 1)
            pe.wait_ge(gate_wt, q.m + 1)
            n = B * TILES * n_exp
            flat = cen[:, :, :].rearrange("p b c -> p (b c)")[:, 7 * ST:7 * ST + n]
            for i in range(-(-n // 128)):
                r = min(128, n - 128 * i)
                last = nc.tensor.transpose(PS[0:r, 1, 128 * i:128 * i + 128], flat[:, 128 * i:128 * i + r], ident[:])
            last.then_inc(gate_pe, 1)

        def gate_views(n_exp):
            n = B * TILES * n_exp
            flat = cen[:, :, :].rearrange("p b c -> p (b c)")
            return [flat[:, j * ST:j * ST + n].rearrange("p (t e) -> p t e", e=n_exp) for j in range(7)] + \
                   [flat[:, 7 * ST:7 * ST + n].rearrange("p (e t) -> p t e", e=n_exp)]

        def gates_scalar(act, q, n_exp):
            base = 0 if q.gated else 1
            val, work, eq, sel, picked, ex, _, _ = gate_views(n_exp)
            if not q.gated:
                act.wait_ge(gate_ex, 2)
                nc.scalar.activation(val, val, ACT.Exp).then_inc(gate_wt_ex, 1)
            act.wait_ge(gate_ex, 1 if q.gated else 3)
            nc.scalar.activation(ex, ex, ACT.Exp).then_inc(gate_wt_ex, 1)

        def gates_vector(dve, q, n_exp, top):
            val, work, eq, sel, picked, ex, _, by_expert = gate_views(n_exp)
            full = [D, B * TILES, n_exp]

            def wide(row):
                return row.unsqueeze(2).to_broadcast(full)

            def link(ins):
                links[0] += 1
                ins.then_inc(gate, 1)
                dve.wait_ge(gate, links[0])

            def row(j):
                return gate_rows[:, j, :]

            dve.wait_ge(lg_done, q.m + 1)
            dve.wait_ge(ln_lo, (q.m + 1) * B)
            link(nc.vector.tensor_copy(val, PS[:, 0, 0:B * TILES * n_exp].rearrange("p (t e) -> p t e", e=n_exp)))
            if not q.gated:
                link(nc.vector.tensor_reduce(out=row(0), in_=val, axis=AX.X, op=ALU.max))
                nc.vector.tensor_tensor(val, val, wide(row(0)), ALU.subtract).then_inc(gate_ex, 1)
                dve.wait_ge(gate_wt_ex, 2)
                link(nc.vector.tensor_reduce(out=row(0), in_=val, axis=AX.X, op=ALU.add))
                link(nc.vector.reciprocal(row(0), row(0)))
                link(nc.vector.tensor_tensor(val, val, wide(row(0)), ALU.mult))
            link(nc.vector.tensor_copy(work, val))
            for k in range(top):
                link(nc.vector.tensor_reduce(out=row(1), in_=work, axis=AX.X, op=ALU.max))
                if k == 0:
                    nc.vector.tensor_tensor(ex, val, wide(row(1)), ALU.subtract).then_inc(gate_ex, 1)
                link(nc.vector.tensor_tensor(eq, work, wide(row(1)), ALU.is_equal))
                link(nc.vector.tensor_tensor(eq, eq, rev_idx[:, 0:n_exp].unsqueeze(1).to_broadcast(full), ALU.mult))
                link(nc.vector.tensor_reduce(out=row(2), in_=eq, axis=AX.X, op=ALU.max))
                link(nc.vector.tensor_tensor(sel, eq, wide(row(2)), ALU.is_equal))
                if k == 0:
                    link(nc.vector.tensor_copy(picked, sel))
                else:
                    link(nc.vector.tensor_tensor(picked, picked, sel, ALU.add))
                link(nc.vector.scalar_tensor_tensor(out=work, in0=sel, scalar=-BIG, in1=work, op0=ALU.mult, op1=ALU.add))
            dve.wait_ge(gate_wt_ex, 1 if q.gated else 3)
            link(nc.vector.tensor_tensor(ex, ex, picked, ALU.mult))
            link(nc.vector.tensor_reduce(out=row(3), in_=ex, axis=AX.X, op=ALU.add))
            link(nc.vector.reciprocal(row(3), row(3)))
            nc.vector.tensor_tensor(by_expert, ex, wide(row(3)), ALU.mult).then_inc(gate_wt, 1)
            if not q.gated:
                link(nc.vector.memset(hid1[0:B, 6, :], 1.0 / SHARED))
            dve.wait_ge(gate_pe, q.m + 1)
            n = B * TILES * n_exp
            last = None
            for i in range(-(-n // 128)):
                r = min(128, n - 128 * i)
                last = nc.vector.tensor_copy(hid1[0:r, i, 0:128], PS[0:r, 1, 128 * i:128 * i + 128])
            last.then_inc(gate_sb, 1)

        links = [0]
        gate_wt_ex = sem("gate_wt_ex")
        gate_rows = sb("gate_rows", [D, 4, B * TILES])


        block = ctx.enter_context(nc.Block())

        @block.sync
        def _(sp):
            def load(dst, src, s):
                sp.dma_start(dst, src).then_inc(s, 16)

            for h, (dst, name) in enumerate(((raw_wq, "wq0"), (raw_wk, "wk0"), (raw_wv, "wv0"), (raw_wu, "wu0"))):
                load(dst, A[name].rearrange("(h e) d -> e h d", h=HEADS), ld_att)
            for j, name in enumerate(("wq1", "wk1", "wv1", "wo1")):
                load(att_raw[:, j, :], A[name], ld_att)
            load(center_w[:], A["center_w"], ld_att)
            load(frames[:, :, 0:T], A["frames"], ld_frames)
            load(w_comp[:], A["w_comp"], ld_tok)
            load(w_main[:], A["w_main"], ld_tok)
            load(w_exp[:], A["w_exp"], ld_tok)
            load(w_ff1[:], A["w_ff1"], ld_tok)
            load(w_ff2[:], A["w_ff2"], ld_tok)
            load(vec[:], A["vec"], ld_tok)
            load(vec64[:], A["vec64"], ld_tok)
            for dst, name in ((ident, "ident"), (mean_w, "mean_w"), (head_w, "head_w"), (causal, "causal"),
                              (head_mask, "head_mask"), (rev_idx, "rev_idx")):
                load(dst[:], A[name], ld_const)
            load(wg0[:], A["wg0"], ld_moe)
            load(wg1[:], A["wg1"], ld_moe)
            load(b1col[:], A["b1col"], ld_moe)
            load(b2col[:], A["b2col"], ld_moe)
            for q in MOES:
                moe_sync(sp, q)
            for b in range(B):
                past(sp, moe[1]["added"], (E1 + SHARED - 1) * B + b + 1)
                sp.dma_start(out[:, b, :], res[:, b, 0:TP]).then_inc(stored, 16)
            sp.wait_ge(stored, 16 * B)

        @block.tensor
        def _(pe):
            start_counts(pe, "tensor")
            pe.wait_ge(ld_att, 16 * 9)
            for h in range(HEADS):
                nc.tensor.matmul(PS[:, h // 4, h % 4 * D:(h % 4 + 1) * D], raw_wq[:, h, :], raw_wk[:, h, :], start=True, stop=True)
            for h in range(HEADS):
                nc.tensor.matmul(PS[:, 2 + h // 4, h % 4 * D:(h % 4 + 1) * D], raw_wv[:, h, :], raw_wu[:, h, :], start=True, stop=True)
            for j in range(2):
                last = nc.tensor.matmul(PS[:, 4, j * D:(j + 1) * D], att_raw[:, j, :], center_w[:], start=True, stop=True)
            last.then_inc(prod_done, 1)

            pe.wait_ge(ld_frames, 16)
            pe.wait_ge(ld_tok, 16 * 7)
            pe.wait_ge(pads_set, 1)
            pe.wait_ge(prod_taken, 3)
            for b in range(B):
                nc.tensor.matmul(PS[0:BN, b, 0:TC], w_comp[:], frames[:, b, 0:TC], start=True, stop=True).then_inc(comp_done, 1)
            for b in range(B):
                pe.wait_ge(comp_act, b + 1)
                for k in range(3):
                    last = nc.tensor.matmul(PS[0:BN, b, 0:TC], w_main[:, k, :], hid1[0:BN, b, k:k + TC], start=k == 0, stop=k == 2)
                last.then_inc(main_done, 1)
            for b in range(B):
                pe.wait_ge(main_act, b + 1)
                nc.tensor.matmul(PS[:, b, 0:TC], w_exp[:], cen[0:BN, b, 0:TC], start=True, stop=True).then_inc(exp_done, 1)
            pe.wait_ge(ld_const, 16 * 6)
            ln_tensor(pe, LN_CONV, frames, TC, lambda pe, b: pe.wait_ge(exp_sum, b + 1))
            for b in range(B):
                pe.wait_ge(ln_aff, b + 1)
                nc.tensor.matmul(PS[0:BN, b, 0:TC], w_ff1[:], xn[:, b, 0:TC], start=True, stop=True).then_inc(ff1_done, 1)
            for b in range(B):
                pe.wait_ge(ff1_act, b + 1)
                nc.tensor.matmul(PS[:, b, 0:TC], w_ff2[:], hid1[0:BN, b, 0:TC], start=True, stop=True).then_inc(ff2_done, 1)
            ln_tensor(pe, LN_FF, xn, TC, lambda pe, b: pe.wait_ge(ff2_sum, b + 1))

            ln_tensor(pe, LN_ATT0, res, NT, lambda pe, b: pe.wait_ge(pooled, b + 1))
            pe.wait_ge(parts_made, 3)
            attention_tensor(pe, 0)

            ln_tensor(pe, LN_MOE0, res, NT, lambda pe, b: past(pe, att[0]["o_taken"], B))
            pe.wait_ge(ld_moe, 16 * 4)
            gates_tensor(pe, MOES[0], wg0, E0)
            pe.wait_ge(ln_lo, B)
            moe_tensor(pe, MOES[0])

            ln_tensor(pe, LN_ATT1, res, NT, lambda pe, b: past(pe, moe[0]["added"], (E0 - 1) * B + b + 1))
            for b in range(B):
                pe.wait_ge(ln_norm, LN_ATT1 * B + b + 1)
                nc.tensor.matmul(PS[:, b, 0:NT], a1c[:, 0, :], xn[:, b, 0:NT], start=True, stop=True).then_inc(q_done, 1)
            ln_tensor(pe, LN_Q, None, NT, None, mean=False, weights=head_w)
            for b in range(B):
                pe.wait_ge(ln_log, LN_Q * B + b + 1)
                nc.tensor.matmul(PS[:, b, 0:NT], a1c[:, 1, :], xn[:, b, 0:NT], start=True, stop=True).then_inc(k_done, 1)
            ln_tensor(pe, LN_K, None, NT, None, mean=False, weights=head_w)
            pe.wait_ge(ln_log, (LN_K + 1) * B)
            attention_tensor(pe, 1)

            ln_tensor(pe, LN_MOE1, res, NT, lambda pe, b: past(pe, att[1]["o_taken"], B))
            gates_tensor(pe, MOES[1], wg1, E1)
            pe.wait_ge(ln_lo, 2 * B)
            moe_tensor(pe, MOES[1])

        @block.scalar
        def _(act):
            start_counts(act, "scalar")
            for j, (dst, src) in enumerate(((mh, prod[:, 0:1024]), (nh, prod[:, 1024:2048]))):
                act.wait_ge(prod_taken, j + 1)
                nc.scalar.activation(dst[:, :, :].rearrange("p h d -> p (h d)"), src, ACT.Copy).then_inc(prod_link, 1)
            act.wait_ge(ld_att, 16 * 9)
            nc.scalar.activation(a1h[:, :, :], att_raw[:, 2:4, :], ACT.Copy).then_inc(prod_link, 1)

            act.wait_ge(ld_tok, 16 * 7)
            act.wait_ge(pads_set, 1)
            for b in range(B):
                act.wait_ge(comp_done, b + 1)
                nc.scalar.activation(hid1[0:BN, b, 1:T + 1], PS[0:BN, b, 0:T], ACT.Silu, bias=vec64[:, 0:1]).then_inc(comp_act, 1)
            for b in range(B):
                act.wait_ge(main_done, b + 1)
                nc.scalar.activation(cen[0:BN, b, 0:TC], PS[0:BN, b, 0:TC], ACT.Silu, bias=vec64[:, 1:2]).then_inc(main_act, 1)
            ln_scalar(act, LN_CONV, TC)
            for b in range(B):
                act.wait_ge(ff1_done, b + 1)
                nc.scalar.activation(hid1[0:BN, b, 0:TC], PS[0:BN, b, 0:TC], ACT.Gelu, bias=vec64[:, 2:3]).then_inc(ff1_act, 1)
            ln_scalar(act, LN_FF, TC)

            ln_scalar(act, LN_ATT0, NT)
            act.wait_ge(ln_norm, (LN_ATT0 + 1) * B)
            attention_scalar(act, 0)

            ln_scalar(act, LN_MOE0, NT, hi=True)
            gates_scalar(act, MOES[0], E0)
            moe_scalar(act, MOES[0])

            ln_scalar(act, LN_ATT1, NT)
            for k, done in ((LN_Q, q_done), (LN_K, k_done)):
                for b in range(B):
                    act.wait_ge(done, b + 1)
                    act.wait_ge(ln_norm, (k - 1) * B + b + 1)
                    nc.scalar.activation(cen[:, b, 0:NT], PS[:, b, 0:NT], ACT.Copy).then_inc(ln_cen, 1)
                ln_scalar(act, k, NT)
            act.wait_ge(ln_aff, (LN_AFF[LN_K] + 1) * B)
            act.wait_ge(vz_done, 2)
            attention_scalar(act, 1)

            ln_scalar(act, LN_MOE1, NT, hi=True)
            gates_scalar(act, MOES[1], E1)
            moe_scalar(act, MOES[1])

        @block.gpsimd
        def _(pool):
            start_counts(pool, "gpsimd")
            pool.wait_ge(ld_tok, 16 * 7)
            ln_gpsimd(pool, LN_CONV, TC, xn, v("g_conv"), v("b_conv"))
            ln_gpsimd(pool, LN_FF, TC, frames, v("g_ff"), v("b_ff"))
            attention_gpsimd(pool, 0)
            moe_gpsimd(pool, MOES[0])
            pool.wait_ge(prod_taken, 4)
            ln_gpsimd(pool, LN_Q, NT, frames, qaff[:, 0:1], qaff[:, 1:2])
            ln_gpsimd(pool, LN_K, NT, hid1, v("k_gamma"), v("k_beta"))
            attention_gpsimd(pool, 1)
            moe_gpsimd(pool, MOES[1])

        @block.vector
        def _(dve):
            start_counts(dve, "vector")
            nc.vector.memset(frames[:, :, T:ST], 0.0)
            nc.vector.memset(hid1[:, :, 0:1], 0.0)
            nc.vector.memset(hid1[:, :, T + 1:ST], 0.0)
            nc.vector.memset(small[:, :, :], 1.0)
            nc.vector.memset(eps[:], EPS).then_inc(pads_set, 1)
            dve.wait_ge(prod_done, 1)
            nc.vector.tensor_scalar(prod[:, 0:1024], PS[:, 0:2, :].rearrange("p a c -> p (a c)"), -float(D) ** -0.5, None, ALU.mult).then_inc(prod_taken, 1)
            nc.vector.tensor_copy(prod[:, 1024:2048], PS[:, 2:4, :].rearrange("p a c -> p (a c)")).then_inc(prod_taken, 1)
            nc.vector.tensor_copy(a1c[:, :, :].rearrange("p j d -> p (j d)"), PS[:, 4, 0:2 * D]).then_inc(prod_taken, 1)
            for j, (hi, lo, src) in enumerate(((mh, ml, prod[:, 0:1024]), (nh, nl, prod[:, 1024:2048]), (a1h, a1l, None))):
                dve.wait_ge(prod_link, j + 1)
                src = att_raw[:, 2:4, :].rearrange("p h d -> p (h d)") if src is None else src
                nc.vector.tensor_tensor(lo[:, :, :].rearrange("p h d -> p (h d)"), src,
                                        hi[:, :, :].rearrange("p h d -> p (h d)").bitcast(F32), ALU.subtract).then_inc(parts_made, 1)
            dve.wait_ge(ld_tok, 16 * 7)
            nc.vector.tensor_scalar(qaff[:, :], vec[:, VECS.index("q_gamma"):VECS.index("q_gamma") + 2],
                                    -float(HD1) ** -0.5, None, ALU.mult).then_inc(prod_taken, 1)

            for b in range(B):
                dve.wait_ge(exp_done, b + 1)
                nc.vector.scalar_tensor_tensor(out=frames[:, b, 0:TC], in0=PS[:, b, 0:TC], scalar=v("b_expand"),
                                               in1=frames[:, b, 0:TC], op0=ALU.add, op1=ALU.add).then_inc(exp_sum, 1)
            dve.wait_ge(parts_made, 3)
            ln_vector(dve, LN_CONV, frames, TC, xn)
            for b in range(B):
                dve.wait_ge(ff2_done, b + 1)
                nc.vector.scalar_tensor_tensor(out=xn[:, b, 0:TC], in0=PS[:, b, 0:TC], scalar=v("b_ff2"),
                                               in1=xn[:, b, 0:TC], op0=ALU.add, op1=ALU.add).then_inc(ff2_sum, 1)
            ln_vector(dve, LN_FF, xn, TC, frames)
            for b in range(B):
                dve.wait_ge(ln_aff, B + b + 1)
                nc.vector.tensor_tensor(hid1[:, b, 0:NT], frames[:, b, 0:NT], frames[:, b, 1:NT + 1], ALU.max).then_inc(pool_a, 1)
            for b in range(B):
                dve.wait_ge(pool_a, b + 1)
                nc.vector.tensor_tensor(res[:, b, 0:NT], hid1[:, b, 0:NT], frames[:, b, 2:NT + 2], ALU.max).then_inc(pooled, 1)

            dve.wait_ge(ln_cen, 2 * B)
            nc.vector.memset(xn[:, :, NT:ST], 0.0).then_inc(pads_set, 1)
            ln_vector(dve, LN_ATT0, res, NT, xn)
            dve.wait_ge(ln_norm, (LN_ATT0 + 1) * B)
            dve.wait_ge(pads_set, 2)
            attention_vector(dve, 0)

            past(dve, att[0]["o_taken"], B)
            ln_vector(dve, LN_MOE0, res, NT, xn, hi=True)
            gates_vector(dve, MOES[0], E0, TOP0)
            moe_vector(dve, MOES[0])

            past(dve, moe[0]["down"], (E0 // 2) * UNITS)
            nc.vector.memset(vph.bitcast(F32), 0.0).then_inc(vz_done, 1)
            nc.vector.memset(vpl.bitcast(F32), 0.0).then_inc(vz_done, 1)
            past(dve, moe[0]["added"], E0 * B)
            ln_vector(dve, LN_ATT1, res, NT, xn)
            ln_vector(dve, LN_Q, None, NT, frames, mean=False)
            ln_vector(dve, LN_K, None, NT, hid1, mean=False)
            dve.wait_ge(vz_done, 2)
            dve.wait_ge(ln_aff, (LN_AFF[LN_K] + 1) * B)
            attention_vector(dve, 1)

            past(dve, att[1]["o_taken"], B)
            ln_vector(dve, LN_MOE1, res, NT, xn, hi=True)
            gates_vector(dve, MOES[1], E1, TOP1)
            moe_vector(dve, MOES[1])


def kernel(**inputs):
    import concourse.bacc as bacc
    from concourse.bass_utils import run_bass_kernel_spmd

    x = {k: np.asarray(a) for k, a in inputs.items()}

    def t(a):
        return np.ascontiguousarray(a)

    def cols(names):
        return t(np.stack([x[n] if x[n].shape[0] != HD1 else np.tile(x[n], HEADS) for n in names], axis=1))

    part = np.arange(D)
    same_head = (part[:, None] // HD1 == part[None, :] // HD1).astype(np.float32) / HD1
    col = np.arange(ST)
    arrays = {
        "frames": t(x["x"].transpose(2, 0, 1)),
        "w_comp": t(x["L0_tok_w_compress"][:, :, 0].T),
        "w_main": t(x["L0_tok_w_main"].transpose(1, 2, 0)),
        "w_exp": t(x["L0_tok_w_expand"][:, :, 0].T),
        "w_ff1": t(x["L0_tok_w_ff1"].T),
        "w_ff2": t(x["L0_tok_w_ff2"].T),
        "vec": cols(["L0_tok_b_expand", "L0_tok_g_conv_norm", "L0_tok_b_conv_norm", "L0_tok_b_ff2", "L0_tok_g_ff_norm",
                     "L0_tok_b_ff_norm", "L1_attn_bo", "L1_attn_q_gamma", "L1_attn_q_beta", "L1_attn_k_gamma",
                     "L1_attn_k_beta"]),
        "vec64": cols(["L0_tok_b_compress", "L0_tok_b_main", "L0_tok_b_ff1"]),
        "wq0": x["L0_attn_Wq"], "wk0": x["L0_attn_Wk"], "wv0": x["L0_attn_Wv"], "wu0": t(x["L0_attn_Wu"].T),
        "wq1": x["L1_attn_Wq"], "wk1": x["L1_attn_Wk"], "wv1": t(x["L1_attn_Wv"].T), "wo1": t(x["L1_attn_Wo"].T),
        "wg0": x["L0_ffn_Wg"], "wg1": t(x["L1_ffn_gate_w"].T),
        "L0_ffn_W": x["L0_ffn_W"], "L0_ffn_V": x["L0_ffn_V"], "L0_ffn_W2": x["L0_ffn_W2"],
        "re_w1": np.concatenate([x["L1_ffn_re_w1"], x["L1_ffn_se_w1"]]),
        "re_w2": np.concatenate([x["L1_ffn_re_w2"], x["L1_ffn_se_w2"]]),
        "b1col": t(np.concatenate([x["L1_ffn_re_b1"], x["L1_ffn_se_b1"]]).reshape((E1 + SHARED) * FCH, 128).T),
        "b2col": t(np.concatenate([x["L1_ffn_re_b2"], x["L1_ffn_se_b2"]]).T),
        "ident": np.eye(D, dtype=np.float32),
        "mean_w": np.full((D, D), 1.0 / D, np.float32),
        "head_w": same_head,
        "center_w": np.eye(D, dtype=np.float32) - same_head,
        "causal": np.where(col[None, :] - 2 * 128 > part[:, None], np.float32(BIG), np.float32(0)).astype(np.float32),
        "head_mask": (part[:, None] // HD1 == np.arange(HEADS)[None, :]).astype(np.float32),
        "rev_idx": np.tile((E1 - np.arange(E1)).astype(np.float32), (D, 1)),
    }
    nc = bacc.Bacc("TRN2", target_bir_lowering=False, num_devices=1)
    A = {n: nc.dram_tensor("in_" + n, a.shape, F32, kind="ExternalInput").ap() for n, a in arrays.items()}
    A["gates0"] = nc.dram_tensor("gates0", (E0, B * ST), F32, kind="Internal").ap()
    A["gates1"] = nc.dram_tensor("gates1", (E1 + SHARED, B * ST), F32, kind="Internal").ap()
    out = nc.dram_tensor("out", (D, B, TP), F32, kind="ExternalOutput").ap()
    audio_tower(nc, A, out)
    r = run_bass_kernel_spmd(nc, [{"in_" + n: a for n, a in arrays.items()}], core_ids=[0])
    return np.ascontiguousarray(r.results[0]["out"].transpose(1, 2, 0))
```

```python
import numpy as np
import concourse.bass as bass
from concourse import mybir
from contextlib import ExitStack

B, T, D = 8, 375, 128
TP = T - 2
ST = 384
TC = T + 1
NT = TP + 1
TILES = ST // 128
BN = D // 2
HEADS = 8
HD1 = D // HEADS
FF = 512
FCH = FF // 128
E0, TOP0 = 8, 2
E1, TOP1, SHARED = 16, 4, 2
MOE_TILES = [(top * B * NT - n) // ST + n for n, top in ((E0, TOP0), (E1, TOP1))]
TILES_MAX = MOE_TILES[1]
CAP_TILES = -(-B * NT // ST)
NOWHERE = 1e6
LEAD = 16
BIG = 1e30
EPS = 1e-5

F32 = mybir.dt.float32
F32R = mybir.dt.float32r
U32, I32 = mybir.dt.uint32, mybir.dt.int32
ALU = mybir.AluOpType
ACT = mybir.ActivationFunctionType
AX = mybir.AxisListType

VECS = ["b_expand", "g_conv", "b_conv", "b_ff2", "g_ff", "b_ff", "bo", "q_gamma", "q_beta", "k_gamma", "k_beta"]
LN_CONV, LN_FF, LN_ATT0, LN_MOE0, LN_ATT1, LN_Q, LN_K, LN_MOE1 = range(8)


def audio_tower(nc, A, out):
    ctx = ExitStack()
    with ctx:
        def sb(name, shape, dt=F32):
            return ctx.enter_context(nc.sbuf_tensor(name, shape, dt))

        def sem(name):
            return ctx.enter_context(nc.semaphore(name))

        res = sb("res", [D, B, ST])
        xn = sb("xn", [D, B, ST])
        cen = sb("cen", [D, B, ST])
        sqr = sb("sqr", [D, B, ST])
        frames = sb("frames", [D, B, ST])
        hid1 = sb("hid1", [D, B, ST])
        xh = sb("xh", [D, B, ST], F32R)
        xl = sb("xl", [D, B, ST], F32R)

        ident = sb("ident", [D, D])
        mean_w = sb("mean_w", [D, D])
        head_w = sb("head_w", [D, D])
        center_w = sb("center_w", [D, D])
        causal = sb("causal", [D, ST])
        head_mask = sb("head_mask", [D, HEADS])
        rev_idx = sb("rev_idx", [D, E1])
        counts = sb("counts", [D, CAP_TILES + TILES_MAX])
        valid = sb("valid", [D, B * TILES])
        below = sb("below", [D, D])
        homes = sb("homes", [D, 2 * B * TILES])
        choice_at = sb("choice_at", [D, TOP1])
        vec = sb("vec", [D, len(VECS)])
        vec64 = sb("vec64", [BN, 3])
        eps = sb("eps", [D, 1])
        qaff = sb("qaff", [D, 2])
        w_comp = sb("w_comp", [D, BN])
        w_main = sb("w_main", [BN, 3, BN])
        w_exp = sb("w_exp", [BN, D])
        w_ff1 = sb("w_ff1", [D, BN])
        w_ff2 = sb("w_ff2", [BN, D])
        wg0 = sb("wg0", [D, E0])
        wg1 = sb("wg1", [D, E1])
        att_raw = sb("att_raw", [D, 4, D])

        mh = sb("mh", [D, HEADS, D], F32R)
        ml = sb("ml", [D, HEADS, D], F32R)
        nh = sb("nh", [D, HEADS, D], F32R)
        nl = sb("nl", [D, HEADS, D], F32R)
        a1c = sb("a1c", [D, 2, D])
        a1h = sb("a1h", [D, 2, D], F32R)
        a1l = sb("a1l", [D, 2, D], F32R)

        workf = sb("workf", [D, 13, ST])
        workr = sb("workr", [D, 26, ST], F32R)
        wsplit = sb("wsplit", [D, 6400], F32R)
        small = sb("small", [D, 4, 6])

        raw_wq = xn[:, :, :].rearrange("p b c -> p (b c)")[:, 0:1024].rearrange("p (h d) -> p h d", h=HEADS)
        raw_wk = xn[:, :, :].rearrange("p b c -> p (b c)")[:, 1024:2048].rearrange("p (h d) -> p h d", h=HEADS)
        raw_wv = xn[:, :, :].rearrange("p b c -> p (b c)")[:, 2048:3072].rearrange("p (h d) -> p h d", h=HEADS)
        raw_wu = cen[:, :, :].rearrange("p b c -> p (b c)")[:, 0:1024].rearrange("p (h d) -> p h d", h=HEADS)
        prod = sqr[:, :, :].rearrange("p b c -> p (b c)")

        neg_s = [workf[:, 2 * k:2 * k + 2, :].rearrange("p a c -> p (a c)") for k in range(2)]
        prob = [workf[:, 4 + 2 * k:6 + 2 * k, :].rearrange("p a c -> p (a c)") for k in range(2)]
        xb = workf[:, 8, :]
        xbh, xbl = [[workr[:, 2 * k + i, :] for k in range(2)] for i in range(2)]
        xth, xtl = [[workr[:, 4 + 2 * k + i, :] for k in range(2)] for i in range(2)]
        kbh, kbl = xth, xtl
        qh, ql = [[workr[:, 8 + 2 * k + i, :] for k in range(2)] for i in range(2)]
        yh, yl = workr[:, 12, :], workr[:, 13, :]
        pth, ptl = [[workr[:, 14 + 4 * k + 2 * i:16 + 4 * k + 2 * i, :] for k in range(2)] for i in range(2)]
        qmh, qml = [[workr[:, 22 + 2 * k + i, :] for k in range(2)] for i in range(2)]
        vph, vpl = [[wsplit[:, 3200 * i:3200 * i + 3200], t[:, :, :].rearrange("p b c -> p (b c)")] for i, t in ((0, xh), (1, xl))]

        PS = ctx.enter_context(nc.psum_tensor("PS", [D, 8, 512], F32))

        S_AT = (0, 128, 384)
        S_N = (128, 256, NT)
        ROWS = (128, 128, NT - 256)
        T_AT = ((0, 0), (1, 0), (1, NT - 128))
        T_N = (NT, NT - 128, NT - 256)

        def v(name):
            return vec[:, VECS.index(name):VECS.index(name) + 1]

        ld_const, ld_frames, ld_tok, ld_att, ld_moe = map(sem, ("ld_const", "ld_frames", "ld_tok", "ld_att", "ld_moe"))
        pads_set, passed = sem("pads_set"), sem("passed")
        prod_done, prod_taken, parts_made, prod_link = map(sem, ("prod_done", "prod_taken", "parts_made", "prod_link"))
        comp_done, comp_act, main_done, main_act = map(sem, ("comp_done", "comp_act", "main_done", "main_act"))
        exp_done, exp_sum, ff1_done, ff1_act = map(sem, ("exp_done", "exp_sum", "ff1_done", "ff1_act"))
        ff2_done, ff2_sum, pool_a, pooled = map(sem, ("ff2_done", "ff2_sum", "pool_a", "pooled"))
        ln_mean, ln_cen, ln_sq, ln_var, ln_log, ln_rstd, ln_norm, ln_aff, ln_hi, ln_lo = map(
            sem, ("ln_mean", "ln_cen", "ln_sq", "ln_var", "ln_log", "ln_rstd", "ln_norm", "ln_aff", "ln_hi", "ln_lo"))
        vz_done, q_done, k_done = map(sem, ("vz_done", "q_done", "k_done"))
        AT_SEMS = {"tensor": ("xt_done", "q_done", "sc_done", "pt_done", "pv_done", "o_done"),
                   "scalar": ("in_hi", "xt_hi", "q_hi", "ex_done", "pt_hi", "y_hi"),
                   "vector": ("in_f", "in_lo", "xt_lo", "q_lo", "sc_min", "rc_done", "pt_lo", "y_lo", "o_taken", "qm_done"),
                   "gpsimd": ("pn_done", "qm_lo")}
        att = [{n: sem(f"at{m}_{n}") for names in AT_SEMS.values() for n in names} for m in range(2)]
        lg_done, gate, gate_ex, gate_exp = map(sem, ("lg_done", "gate", "gate_ex", "gate_exp"))
        picked_set, rank_done, map_set, slots_set, turned, turned_out = map(
            sem, ("picked_set", "rank_done", "map_set", "slots_set", "turned", "turned_out"))
        scattered, zero_set, filled = sem("scattered"), sem("zero_set"), sem("filled")
        gathered = [sem(f"gathered{i}") for i in range(4)]
        diag_act, diag_dve, summed, added = map(sem, ("diag_act", "diag_dve", "summed", "added"))
        moe = [{n: sem(f"moe{m}_" + n) for n in (
            "w_hi", "w_lo", "w_lo2", "ids", "xt", "x_hi", "x_lo", "up", "act", "mul", "hi", "lo", "down", "y_sum", "yt", "y_out")
                if n != ("w_lo2", "mul")[m]} for m in range(2)]
        sh = {n: sem("sh_" + n) for n in ("w_hi", "w_lo", "b2", "up", "act", "hi", "lo", "down", "out", "added")}
        ld_sh = sem("ld_sh")
        ld_w, ld_x, st_y = [[sem(f"{n}{k}") for k in range(3)] for n in ("ld_w", "ld_x", "st_y")]
        stored = sem("stored")


        MOE_SEMS = {"tensor": ("xt", "up", "down", "yt"), "scalar": ("w_hi", "x_hi", "act", "y_sum"),
                    "vector": ("x_lo", "mul", "lo", "y_out", "ids", "w_lo2"), "gpsimd": ("w_lo",)}

        def start_counts(eng, name):
            for m in range(2):
                for n in AT_SEMS[name]:
                    eng.sem_inc(att[m][n], 1)
                for n in MOE_SEMS[name] + (("hi",) if name == ("scalar", "vector")[m] else ()):
                    if n in moe[m]:
                        eng.sem_inc(moe[m][n], LEAD)

        def reached(eng, s, n):
            eng.wait_ge(s, n + LEAD)

        def past(eng, s, n):
            eng.wait_ge(s, n + 1)

        def waits_passed(eng):
            eng.sem_inc(passed, 1)

        def three(pe, out_, lh, ll, rh, rl, start=True, stop=True):
            nc.tensor.matmul(out_, lh, rh, start=start, stop=False)
            nc.tensor.matmul(out_, lh, rl, start=False, stop=False)
            return nc.tensor.matmul(out_, ll, rh, start=False, stop=stop)

        def ln_tensor(pe, k, src, n, ready, mean=True, weights=None):
            w = mean_w if weights is None else weights
            if mean:
                for b in range(B):
                    ready(pe, b)
                    nc.tensor.matmul(PS[:, b, 0:n], w[:], src[:, b, 0:n], start=True, stop=True).then_inc(ln_mean, 1)
            for b in range(B):
                pe.wait_ge(ln_sq, k * B + b + 1)
                nc.tensor.matmul(PS[:, b, 0:n], w[:], sqr[:, b, 0:n], start=True, stop=True).then_inc(ln_var, 1)

        def ln_scalar(act, k, n):
            nc.scalar.preload_act_table_set("natural_log_exp_and_others")
            for b in range(B):
                act.wait_ge(ln_cen, k * B + b + 1)
                nc.scalar.activation(sqr[:, b, 0:n], cen[:, b, 0:n], ACT.Square).then_inc(ln_sq, 1)
            for b in range(B):
                act.wait_ge(ln_var, k * B + b + 1)
                nc.scalar.activation(sqr[:, b, 0:n], PS[:, b, 0:n], ACT.Ln, bias=eps[:, 0:1]).then_inc(ln_log, 1)
            for b in range(B):
                act.wait_ge(ln_log, k * B + b + 1)
                nc.scalar.activation(sqr[:, b, 0:n], sqr[:, b, 0:n], ACT.Exp, scale=-0.5).then_inc(ln_rstd, 1)

        def high_parts(act):
            for b in range(B):
                act.wait_ge(ln_norm, LN_MOE1 * B + b + 1)
                nc.scalar.activation(xh[:, b, 0:NT], xn[:, b, 0:NT], ACT.Copy).then_inc(ln_hi, 1)

        def low_parts(dve):
            for b in range(B):
                dve.wait_ge(ln_hi, b + 1)
                nc.vector.tensor_tensor(xl[:, b, 0:NT], xn[:, b, 0:NT], xh[:, b, 0:NT].bitcast(F32), ALU.subtract).then_inc(ln_lo, 1)

        def ln_vector(dve, k, src, n, dst, mean=True):
            if mean:
                if k:
                    dve.wait_ge(ln_norm, k * B)
                for b in range(B):
                    dve.wait_ge(ln_mean, LN_MEANS[k] * B + b + 1)
                    nc.vector.tensor_tensor(cen[:, b, 0:n], src[:, b, 0:n], PS[:, b, 0:n], ALU.subtract).then_inc(ln_cen, 1)
            for b in range(B):
                dve.wait_ge(ln_rstd, k * B + b + 1)
                nc.vector.tensor_tensor(dst[:, b, 0:n], cen[:, b, 0:n], sqr[:, b, 0:n], ALU.mult).then_inc(ln_norm, 1)

        LN_MEANS = {LN_CONV: 0, LN_FF: 1, LN_ATT0: 2, LN_MOE0: 3, LN_ATT1: 4, LN_MOE1: 5}
        LN_AFF = {LN_CONV: 0, LN_FF: 1, LN_Q: 2, LN_K: 3}

        def ln_gpsimd(pool, k, n, dst, gamma, beta):
            for b in range(B):
                pool.wait_ge(ln_norm, k * B + b + 1)
                nc.gpsimd.tensor_scalar(dst[:, b, 0:n], dst[:, b, 0:n], gamma, beta, ALU.mult, ALU.add).then_inc(ln_aff, 1)


        class At:
            def __init__(self, p, c):
                self.p, self.c = p, c
                self.n = c if p is None else p * (2 * HEADS) + c
                self.h, self.clip_par, self.par = c % HEADS, c // HEADS % 2, c % 2
                self.b = c // HEADS if p is None else p * 2 + c // HEADS
                self.live = p is not None or 0 <= c < B * HEADS
                self.stat = small[:, c % 4, :]

            def __add__(self, k):
                return At(self.p, self.c + k)

            def last_of_clip(self):
                return self.live and self.h == HEADS - 1

            def next_clip(self, lead):
                nxt = self + lead
                return nxt if self.h == HEADS - lead and nxt.live else None

        def slots(eng, slot):
            for i in range(-3, 3):
                slot(At(None, i))
            with eng.Fori(0, B // 2 - 1) as p:
                for i in range(3, 3 + 2 * HEADS):
                    slot(At(p, i))
            for i in range((B - 2) * HEADS + 3, B * HEADS + 4):
                slot(At(None, i))

        def bank_of(i):
            return (1, S_AT[i]) if i < 2 else (2, 0)

        def clip_of(t, at, n=NT):
            if isinstance(at.b, int):
                return t[:, at.b, 0:n]
            return t[:, bass.ds(at.b, 1), 0:n].rearrange("p b c -> p (b c)")

        def head_columns(v_):
            pairs = []
            for t in range(TILES):
                for a, e in ((0, HEADS - 1), (HEADS - 1, HEADS)):
                    n = e - a
                    at = 1024 * t + (128 + HD1) * a
                    dst = v_[:, at:at + HD1] if n == 1 else \
                        v_[:, at:at + (128 + HD1) * n].rearrange("p (h q) -> p h q", h=n)[:, :, 0:HD1]
                    src = PS[:, 7, 128 * t + HD1 * a:128 * t + HD1 * e]
                    pairs.append((dst, src if n == 1 else src.rearrange("p (h i) -> p h i", h=n)))
            return pairs

        def attention_tensor(pe, m):
            s = att[m]

            def turn_clip(at):
                past(pe, s["xt_lo"], at.b)
                par = at.clip_par
                if m == 0:
                    past(pe, s["in_f"], at.b + 1)
                    for t in range(TILES):
                        last = nc.tensor.transpose(PS[:, 7, 128 * t:128 * t + 128], xb[:, 128 * t:128 * t + 128], ident[:])
                else:
                    past(pe, s["in_lo"], at.b + 1)
                    for t in range(TILES):
                        c = slice(128 * t, 128 * t + 128)
                        last = three(pe, PS[:, 7, c], xbh[par][:, c], xbl[par][:, c], a1h[:, 0, :], a1l[:, 0, :])
                last.then_inc(s["xt_done"], 1)

            def project_q(at):
                if at.h == 0:
                    past(pe, s["in_lo"], at.b + 1)
                past(pe, s["q_lo"], at.n)
                x = xbh[at.clip_par][:, 0:NT], xbl[at.clip_par][:, 0:NT]
                three(pe, PS[:, 0, 0:NT], mh[:, at.h, :], ml[:, at.h, :], *x).then_inc(s["q_done"], 1)

            def scores(at):
                if m == 0:
                    past(pe, s["q_lo"], at.n + 1)
                    q, k = (qh[at.par], ql[at.par]), (xbh[at.clip_par], xbl[at.clip_par])
                else:
                    past(pe, s["qm_done"], at.n + 1)
                    past(pe, s["qm_lo"], at.n + 1)
                    q, k = (qmh[at.par], qml[at.par]), (kbh[at.clip_par], kbl[at.clip_par])
                past(pe, s["sc_min"], at.n * TILES)
                for i in range(TILES):
                    r, c = ROWS[i], S_N[i]
                    bank, col = bank_of(i)
                    last = three(pe, PS[0:r, bank, col:col + c], q[0][:, 128 * i:128 * i + r], q[1][:, 128 * i:128 * i + r],
                                 k[0][:, 0:c], k[1][:, 0:c])
                last.then_inc(s["sc_done"], 1)

            def transpose(at):
                past(pe, s["pn_done"], at.n + 1)
                past(pe, s["pt_lo"], at.n)
                for i in range(TILES):
                    for j in range(i + 1):
                        bank, col = T_AT[j]
                        r, c = ROWS[i], min(128, S_N[i] - 128 * j)
                        o = col + 128 * (i - j)
                        last = nc.tensor.transpose(PS[0:c, 3 + bank, o:o + r],
                                                   prob[at.par][0:r, S_AT[i] + 128 * j:S_AT[i] + 128 * j + c], ident[0:r, 0:r])
                last.then_inc(s["pt_done"], 1)

            def values(at):
                past(pe, s["pt_lo"], at.n + 1)
                if at.h == 0:
                    past(pe, s["xt_lo"], at.b + 1)
                if m == 0:
                    past(pe, s["y_lo"], at.n)
                    bank, first, final = 5, True, True
                else:
                    bank, first, final = (6, 0)[at.clip_par], at.h == 0, at.h == HEADS - 1
                    if first and at.c >= 2 * HEADS or first and at.p is not None:
                        past(pe, s["y_lo"], at.b - 1)
                for j in range(TILES):
                    tb, col = T_AT[j]
                    k = ROWS[j]
                    if m == 0:
                        v_ = xth[at.clip_par][0:k, 128 * j:128 * j + 128], xtl[at.clip_par][0:k, 128 * j:128 * j + 128]
                    else:
                        c = 1024 * j + 128 * at.h
                        v_ = vph[at.clip_par][0:k, c:c + 128], vpl[at.clip_par][0:k, c:c + 128]
                    last = three(pe, PS[:, bank, 128 * j:NT], *v_, pth[at.par][0:k, tb, col:col + T_N[j]],
                                 ptl[at.par][0:k, tb, col:col + T_N[j]], start=first and j == 0, stop=final and j == TILES - 1)
                if final:
                    last.then_inc(s["pv_done"], 1)

            def project_out(at):
                if m == 0:
                    past(pe, s["y_lo"], at.n + 1)
                    if at.h == 0:
                        past(pe, s["o_taken"], at.b)
                    last = three(pe, PS[:, 6, 0:NT], nh[:, at.h, :], nl[:, at.h, :], yh[:, 0:NT], yl[:, 0:NT],
                                 start=at.h == 0, stop=at.h == HEADS - 1)
                    if at.h == HEADS - 1:
                        last.then_inc(s["o_done"], 1)
                elif at.h == HEADS - 1:
                    past(pe, s["y_lo"], at.b + 1)
                    past(pe, s["o_taken"], at.b)
                    three(pe, PS[:, 5, 0:NT], a1h[:, 1, :], a1l[:, 1, :], yh[:, 0:NT], yl[:, 0:NT]).then_inc(s["o_done"], 1)

            def slot(i):
                if i.c == -3 and i.p is None:
                    turn_clip(i + 3)
                nxt = (i + 3).live and (i + 3).next_clip(2)
                if nxt:
                    turn_clip(nxt)
                if (i + 3).live and m == 0:
                    project_q(i + 3)
                if (i + 2).live:
                    scores(i + 2)
                if i.live:
                    transpose(i)
                if (i + -2).live:
                    project_out(i + -2)
                if (i + -1).live:
                    values(i + -1)

            slots(pe, slot)

        def attention_scalar(act, m):
            s = att[m]

            def fetch(at):
                if at.c >= 2 * HEADS or at.p is not None:
                    past(act, s["o_done"], at.b - 1)
                par = at.clip_par
                for dst, src in ((xbh, xn),) if m == 0 else ((xbh, xn), (kbh, hid1), (qh, frames)):
                    n = ST if src is xn else NT
                    nc.scalar.activation(dst[par][:, 0:n], clip_of(src, at, n), ACT.Copy).then_inc(s["in_hi"], 1)

            def turned_hi(at):
                past(act, s["xt_done"], at.b + 1)
                if m == 0:
                    nc.scalar.activation(xth[at.clip_par], PS[:, 7, 0:ST], ACT.Copy).then_inc(s["xt_hi"], 1)
                    return
                if at.p is not None or at.c >= HEADS:
                    past(act, s["pv_done"], at.b - 1)
                for dst, src in head_columns(vph[at.clip_par]):
                    last = nc.scalar.activation(dst, src, ACT.Copy)
                last.then_inc(s["xt_hi"], 1)

            def slot(i):
                if i.c == -3 and i.p is None:
                    fetch(i + 3)
                    turned_hi(i + 3)
                nxt = (i + 3).live and (i + 3).next_clip(3)
                if nxt:
                    fetch(nxt)
                nxt = (i + 3).live and (i + 3).next_clip(2)
                if nxt:
                    turned_hi(nxt)
                a = i + 3
                if a.live and m == 0:
                    past(act, s["q_done"], a.n + 1)
                    if a.p is not None or a.c >= 2:
                        past(act, s["sc_done"], a.n - 1)
                    nc.scalar.activation(qh[a.par][:, 0:NT], PS[:, 0, 0:NT], ACT.Copy).then_inc(s["q_hi"], 1)
                if i.live:
                    past(act, s["pt_done"], i.n + 1)
                    nc.scalar.activation(pth[i.par][:, :, 0:NT], PT, ACT.Copy).then_inc(s["pt_hi"], 1)
                a = i + 2
                if a.live:
                    if a.p is not None or a.c >= 2:
                        past(act, s["pt_done"], a.n - 1)
                    for t in range(TILES):
                        r, c = ROWS[t], slice(S_AT[t], S_AT[t] + S_N[t])
                        past(act, s["sc_min"], a.n * TILES + t + 1)
                        last = nc.scalar.activation(prob[a.par][0:r, c], neg_s[a.par][0:r, c], ACT.Exp, bias=a.stat[0:r, t:t + 1],
                                                    scale=-1.0, accum_out=a.stat[0:r, 3 + t:4 + t])
                    last.then_inc(s["ex_done"], 1)
                a = i + -1
                if a.live and m == 0 or a.last_of_clip():
                    past(act, s["pv_done"], (a.n if m == 0 else a.b) + 1)
                    if m == 1 and (a.p is not None or a.c >= HEADS):
                        past(act, s["o_done"], a.b)
                    bank = 5 if m == 0 else (6, 0)[a.clip_par]
                    nc.scalar.activation(yh[:, 0:NT], PS[:, bank, 0:NT], ACT.Copy).then_inc(s["y_hi"], 1)

            slots(act, slot)

        def attention_vector(dve, m):
            s = att[m]

            def less(out_, a, hi):
                return nc.vector.tensor_tensor(out_, a, hi.bitcast(F32), ALU.subtract)

            def fetch(at):
                par = at.clip_par
                if m == 0:
                    past(dve, s["xt_done"], at.b)
                    nc.vector.tensor_copy(xb, clip_of(xn, at, ST)).then_inc(s["in_f"], 1)
                both = ((xbl, xbh, xn),) if m == 0 else ((xbl, xbh, xn), (kbl, kbh, hid1), (ql, qh, frames))
                for j, (lo, hi, src) in enumerate(both):
                    n = ST if src is xn else NT
                    past(dve, s["in_hi"], at.b * len(both) + j + 1)
                    last = less(lo[par][:, 0:n], clip_of(src, at, n), hi[par][:, 0:n])
                last.then_inc(s["in_lo"], 1)

            def turned_lo(at):
                past(dve, s["xt_hi"], at.b + 1)
                if m == 0:
                    less(xtl[at.clip_par], PS[:, 7, 0:ST], xth[at.clip_par]).then_inc(s["xt_lo"], 1)
                    return
                for (dst, src), (hi, _) in zip(head_columns(vpl[at.clip_par]), head_columns(vph[at.clip_par])):
                    last = less(dst, src, hi)
                last.then_inc(s["xt_lo"], 1)

            def add_up(at):
                past(dve, s["o_done"], at.b + 1)
                r = clip_of(res, at)
                if m == 0:
                    nc.vector.tensor_tensor(r, r, PS[:, 6, 0:NT], ALU.add).then_inc(s["o_taken"], 1)
                else:
                    nc.vector.scalar_tensor_tensor(out=r, in0=PS[:, 5, 0:NT], scalar=v("bo"), in1=r,
                                                   op0=ALU.add, op1=ALU.add).then_inc(s["o_taken"], 1)

            def slot(i):
                if i.c == -3 and i.p is None:
                    fetch(i + 3)
                    turned_lo(i + 3)
                a = i + -3
                if a.last_of_clip():
                    add_up(a)
                nxt = (i + 3).live and (i + 3).next_clip(3)
                if nxt:
                    fetch(nxt)
                nxt = (i + 3).live and (i + 3).next_clip(2)
                if nxt:
                    turned_lo(nxt)
                a = i + 3
                if a.live and m == 1:
                    if a.h == 0:
                        past(dve, s["in_lo"], a.b + 1)
                    if a.p is not None or a.c >= 2:
                        past(dve, s["sc_done"], a.n - 1)
                    waits_passed(dve)
                    nc.vector.tensor_scalar(qmh[a.par][:, 0:NT], qh[a.clip_par][:, 0:NT].bitcast(F32),
                                            head_mask[:, a.h:a.h + 1], None, ALU.mult).then_inc(s["qm_done"], 1)
                a = i + -2
                if a.live and m == 0 or a.last_of_clip():
                    past(dve, s["y_hi"], (a.n if m == 0 else a.b) + 1)
                    bank = 5 if m == 0 else (6, 0)[a.clip_par]
                    less(yl[:, 0:NT], PS[:, bank, 0:NT], yh[:, 0:NT]).then_inc(s["y_lo"], 1)
                a = i + 3
                if a.live and m == 0:
                    past(dve, s["q_hi"], a.n + 1)
                    less(ql[a.par][:, 0:NT], PS[:, 0, 0:NT], qh[a.par][:, 0:NT]).then_inc(s["q_lo"], 1)
                a = i + 2
                if a.live:
                    past(dve, s["sc_done"], a.n + 1)
                    if a.p is not None or a.c >= 2:
                        past(dve, s["ex_done"], a.n - 1)
                    if a.p is not None or a.c >= 4:
                        past(dve, s["pn_done"], a.n - 3)
                    waits_passed(dve)
                    for t in range(TILES):
                        r, n = ROWS[t], S_N[t]
                        bank, col = bank_of(t)
                        nc.vector.tensor_tensor_reduce(
                            out=neg_s[a.par][0:r, S_AT[t]:S_AT[t] + n], in0=PS[0:r, bank, col:col + n],
                            in1=causal[0:r, (2 - t) * 128:(2 - t) * 128 + n], scale=1.0, scalar=3e38,
                            op0=ALU.add, op1=ALU.min, accum_out=a.stat[0:r, t:t + 1]).then_inc(s["sc_min"], 1)
                a = i + 1
                if a.live:
                    past(dve, s["ex_done"], a.n + 1)
                    nc.vector.reciprocal(a.stat[:, 3:6], a.stat[:, 3:6]).then_inc(s["rc_done"], 1)
                if i.live:
                    past(dve, s["pt_hi"], i.n + 1)
                    less(ptl[i.par][:, :, 0:NT], PT, pth[i.par][:, :, 0:NT]).then_inc(s["pt_lo"], 1)

            slots(dve, slot)

        def attention_gpsimd(pool, m):
            s = att[m]

            def slot(i):
                a = i + 3
                if a.live and m == 1:
                    if a.h == 0:
                        past(pool, s["in_lo"], a.b + 1)
                    if a.p is not None or a.c >= 2:
                        past(pool, s["sc_done"], a.n - 1)
                    waits_passed(pool)
                    nc.gpsimd.tensor_scalar(qml[a.par][:, 0:NT], ql[a.clip_par][:, 0:NT].bitcast(F32),
                                            head_mask[:, a.h:a.h + 1], 0.0, ALU.mult, ALU.add).then_inc(s["qm_lo"], 1)
                a = i + 1
                if a.live:
                    past(pool, s["rc_done"], a.n + 1)
                    waits_passed(pool)
                    for t in range(TILES):
                        r = ROWS[t]
                        p_ = prob[a.par][0:r, S_AT[t]:S_AT[t] + S_N[t]]
                        last = nc.gpsimd.tensor_scalar(p_, p_, a.stat[0:r, 3 + t:4 + t], 0.0, ALU.mult, ALU.add)
                    last.then_inc(s["pn_done"], 1)

            slots(pool, slot)

        PT = PS[:, 3:5, 0:NT]


        class Experts:
            def __init__(self, m):
                self.m, self.s = m, moe[m]
                self.gated = m == 0
                self.n_exp, self.top = ((E0, TOP0), (E1, TOP1))[m]
                self.tiles = MOE_TILES[m]
                self.n_up = 2 if self.gated else 1
                self.cols = self.n_up * FF + FF
                self.pool_cols = self.cols if self.gated else 6 * 128
                self.x_bank = 7 if self.gated else 3
                self.n_bias = 1 if self.gated else FCH + 2
                self.packed = self.cols + self.n_bias
                self.row = D + 1 + TOP1
                self.rows = NTT * self.top * 128
                assert self.tiles % 3 == 2
                self.loads_before = [len(range(k, MOE_TILES[0], 3)) if m else 0 for k in range(3)]
                self.stores_before = [TILES * n for n in self.loads_before]

        NTT = B * TILES
        MOES = [Experts(0), Experts(1)]

        def flat(t):
            return t.rearrange("p b c -> p (b c)")

        raw = [flat(t[:, :, :])[:, 0:1540] for t in (xn, sqr, hid1)]
        split_at = [wsplit[:, 0:3072], wsplit[:, 3072:6144], flat(workr[:, 14:22, :])]
        parts = [(w[:, 0:1536], w[:, 1536:3072]) for w in split_at]
        x_rows = [flat(workf[:, :, :])[:, 7 * ST + 400 * k:7 * ST + 400 * k + 400] for k in range(3)]
        y_rows = [frames[:, k, :] for k in range(3)]
        y_cols = workf[:, 6, :]
        xt_h, xt_l = [[workr[:, 8 + 2 * k + i, :] for k in range(3)] for i in range(2)]
        empty = flat(workf[:, :, :])[:, 9 * ST:9 * ST + TILES * (D + 1 + TOP1)]
        hid_f, mul_f = [[workf[:, 3 * i + k, :] for k in range(3)] for i in range(2)]
        hid_h, hid_l = [[workr[:, 2 * k + i, :] for k in range(4)] for i in range(2)]

        class Tile:
            def __init__(self, q, p, c):
                self.q, self.p, self.c = q, p, c
                self.n = c if p is None else p * 3 + c
                self.turn = c // 3 if p is None else p + c // 3
                self.buf = c % 3
                self.live = p is not None or 0 <= c < q.tiles

            def __add__(self, k):
                return Tile(self.q, self.p, self.c + k)

            def unit(self, f):
                return Unit(self + f // FCH, f % FCH)

        class Unit:
            def __init__(self, tile, f):
                self.tile, self.f, self.live = tile, f, tile.live
                self.n = tile.n * FCH + f
                self.buf, self.part = (tile.c * FCH + f) % 3, (tile.c * FCH + f) % 4

        def tiles(eng, q, slot):
            for c in range(3):
                slot(Tile(q, None, c))
            with eng.Fori(0, (q.tiles - 5) // 3) as p:
                for c in range(3, 6):
                    slot(Tile(q, p, c))
            for c in range(q.tiles - 2, q.tiles + 2):
                slot(Tile(q, None, c))

        def tile_of(rows, i):
            return A[rows][i.n] if i.p is None else A[rows][bass.ds(i.n, 1), :, :].rearrange("i p c -> p (i c)")

        def moe_sync(sp, q):
            s = q.s

            def load_weights(i):
                reached(sp, s["w_lo"], i.n - 2)
                if not q.gated:
                    reached(sp, s["w_lo2"], i.n - 2)
                e = sp.value_load(tile_expert[0:1, bass.ds(i.n, 1)] if i.p is not None else tile_expert[0:1, i.n:i.n + 1],
                                  min_val=0, max_val=q.n_exp - 1)
                sp.dma_start(raw[i.buf][:, 0:q.packed],
                             A[f"experts{q.m}"][bass.ds(e, 1), :, :].rearrange("e p c -> p (e c)")).then_inc(ld_w[i.buf], 16)

            def load_rows(i):
                reached(sp, s["xt"], i.n - 2)
                reached(sp, s["ids"], 3 * (i.n - 2))
                sp.dma_start(x_rows[i.buf][:, 0:TILES * q.row], tile_of(f"xs{q.m}", i)).then_inc(ld_x[i.buf], 16)

            def slot(i):
                if (i + 1).live:
                    if not q.gated and i.p is None and i.c == 0:
                        sp.wait_ge(sh["added"], B)
                    load_weights(i + 1)
                    load_rows(i + 1)

            sp.wait_ge(map_set, q.m + 1)
            if not q.gated:
                sp.wait_ge(ln_lo, B)
            load_weights(Tile(q, None, 0))
            sp.wait_ge(scattered, 16 * B * TILES * (TOP0 + q.m * TOP1))
            load_rows(Tile(q, None, 0))
            tiles(sp, q, slot)

        def copied(dst, src):
            return nc.gpsimd.tensor_scalar(dst, src, 1.0, 0.0, ALU.mult, ALU.add)

        def split(pool, hi, lo, src, w_hi, w_lo, n):
            copied(hi, src).then_inc(w_hi, 1)
            pool.wait_ge(w_hi, n)
            nc.gpsimd.tensor_tensor(lo, src, hi.bitcast(F32), ALU.subtract).then_inc(w_lo, 1)

        def moe_gpsimd(pool, q):
            s = q.s

            def low_weights(i):
                reached(pool, s["w_hi"], 2 * (i.n + 1))
                reached(pool, s["ids"], 3 * (i.n - 2))
                if not q.gated:
                    reached(pool, s["y_sum"], i.n - 2)
                waits_passed(pool)
                copied(biases[i.buf][:, 0:q.n_bias], raw[i.buf][:, q.cols:q.packed])
                w = slice(0, q.pool_cols)
                nc.gpsimd.tensor_tensor(parts[i.buf][1][:, w], raw[i.buf][:, w], parts[i.buf][0][:, w].bitcast(F32),
                                        ALU.subtract).then_inc(s["w_lo"], 1)

            def scatter_results(i):
                reached(pool, s["y_out"], i.n + 1)
                reached(pool, s["ids"], 3 * (i.n + 1))
                waits_passed(pool)
                for j in range(TILES):
                    nc.gpsimd.indirect_dma_start(
                        A[f"ys{q.m}"], bass.IndirectOffsetOnAxis(y_place[i.buf][:, j:j + 1], 0),
                        y_rows[i.buf][:, 128 * j:128 * j + 128], None, bounds_check=q.rows - 1, oob_is_err=False
                        ).then_inc(st_y[i.buf], 16)

            def slot(i):
                if (i + 1).live:
                    low_weights(i + 1)
                if (i + -2).live:
                    scatter_results(i + -2)

            pool.wait_ge(turned_out, 6 * (q.m + 1))
            pool.wait_ge(slots_set, q.m + 1)
            pool.wait_ge(filled, 16 * 6)
            for t in range(NTT):
                if t == NTT - TILES:
                    low_weights(Tile(q, None, 0))
                for k in range(q.top):
                    r, at = ROWS[t % TILES], k * NTT + t
                    nc.gpsimd.indirect_dma_start(
                        A[f"xs{q.m}"].rearrange("i p (r c) -> (i p r) c", c=q.row),
                        bass.IndirectOffsetOnAxis(place[0:r, at:at + 1], 0),
                        token_rows(q)[0:r, t, :], None).then_inc(scattered, 16)
            tiles(pool, q, slot)

        def moe_tensor(pe, q):
            s = q.s

            def turn_in(i):
                pe.wait_ge(ld_x[i.buf], 16 * (q.loads_before[i.buf] + i.turn + 1))
                if q.gated:
                    reached(pe, s["y_out"], i.n - 2)
                else:
                    reached(pe, s["x_lo"], i.n)
                for j in range(TILES):
                    c = slice(128 * j, 128 * j + 128)
                    last = nc.tensor.transpose(PS[:, q.x_bank, c], x_rows[i.buf][:, q.row * j:q.row * j + D], ident[:])
                last.then_inc(s["xt"], 1)

            def turn_out(i):
                reached(pe, s["y_sum"], i.n + 1)
                if q.gated and (i + 2).live:
                    reached(pe, s["x_lo"], i.n + 3)
                else:
                    reached(pe, s["y_out"], i.n)
                for j in range(TILES):
                    c = slice(128 * j, 128 * j + 128)
                    last = nc.tensor.transpose(PS[:, 7, c], y_cols[:, c], ident[:])
                last.then_inc(s["yt"], 1)

            def up(u):
                i = u.tile
                if u.f == 0:
                    reached(pe, s["w_lo"], i.n + 1)
                    if not q.gated:
                        reached(pe, s["w_lo2"], i.n + 1)
                    reached(pe, s["x_lo"], i.n + 1)
                reached(pe, s["mul" if q.gated else "act"], u.n - 2)
                for k in range(q.n_up):
                    c = slice(k * FF + u.f * 128, k * FF + u.f * 128 + 128)
                    last = three(pe, PS[:, 3 * k + u.buf, 0:ST], parts[i.buf][0][:, c], parts[i.buf][1][:, c],
                                 xt_h[i.buf], xt_l[i.buf])
                last.then_inc(s["up"], 1)

            def down(u):
                i = u.tile
                if u.f == 0:
                    reached(pe, s["y_sum"], i.n)
                reached(pe, s["lo"], u.n + 1)
                c = slice(q.n_up * FF + u.f * 128, q.n_up * FF + u.f * 128 + 128)
                three(pe, PS[:, 6, 0:ST], parts[i.buf][0][:, c], parts[i.buf][1][:, c], hid_h[u.part], hid_l[u.part],
                      start=u.f == 0, stop=u.f == FCH - 1).then_inc(s["down"], 1)

            def slot(i):
                for f in range(FCH):
                    if i.live:
                        up(i.unit(f))
                    if i.unit(f - 3).live:
                        down(i.unit(f - 3))
                    if f == 1 and (i + 1).live:
                        turn_in(i + 1)
                    if f == FCH - 1 and (i + -1).live:
                        turn_out(i + -1)

            turn_in(Tile(q, None, 0))
            tiles(pe, q, slot)

        def moe_scalar(act, q):
            s = q.s

            def high_weights(i, half):
                if half == 0:
                    act.wait_ge(ld_w[i.buf], 16 * (q.loads_before[i.buf] + i.turn + 1))
                    reached(act, s["down"], FCH * (i.n - 2))
                    waits_passed(act)
                w = slice(half * q.cols // 2, (half + 1) * q.cols // 2)
                nc.scalar.activation(parts[i.buf][0][:, w], raw[i.buf][:, w], ACT.Copy).then_inc(s["w_hi"], 1)

            def x_high(i):
                reached(act, s["xt"], i.n + 1)
                nc.scalar.activation(xt_h[i.buf], PS[:, q.x_bank, 0:ST], ACT.Copy).then_inc(s["x_hi"], 1)

            def slot(i):
                for f in range(FCH):
                    u = i.unit(f)
                    if u.live:
                        reached(act, s["up"], u.n + 1)
                        reached(act, s["mul" if q.gated else "lo"], u.n - 2)
                        if q.gated:
                            nc.scalar.activation(hid_f[u.buf], PS[:, u.buf, 0:ST], ACT.Silu).then_inc(s["act"], 1)
                        else:
                            nc.scalar.activation(hid_f[u.buf], PS[:, u.buf, 0:ST], ACT.Gelu,
                                                 bias=biases[i.buf][:, f:f + 1]).then_inc(s["act"], 1)
                    u = i.unit(f - 1)
                    if q.gated and u.live:
                        reached(act, s["mul"], u.n + 1)
                        reached(act, s["down"], u.n - 3)
                        nc.scalar.activation(hid_h[u.part], mul_f[u.buf], ACT.Copy).then_inc(s["hi"], 1)
                    if f == 0 and (i + 1).live:
                        high_weights(i + 1, 1)
                    if f == 1 and (i + 1).live:
                        x_high(i + 1)
                    if f == 2 and (i + -1).live:
                        j = i + -1
                        reached(act, s["down"], FCH * (j.n + 1))
                        reached(act, s["yt"], j.n)
                        if q.gated:
                            nc.scalar.activation(y_cols, PS[:, 6, 0:ST], ACT.Copy).then_inc(s["y_sum"], 1)
                        else:
                            nc.scalar.activation(y_cols, PS[:, 6, 0:ST], ACT.Identity,
                                                 bias=biases[j.buf][:, FCH:FCH + 1]).then_inc(s["y_sum"], 1)
                if (i + 2).live:
                    high_weights(i + 2, 0)

            for c in range(2):
                if not q.gated and c == 1:
                    act.wait_ge(sh["down"], SHARED_UNITS)
                for half in range(2 - c):
                    high_weights(Tile(q, None, c), half)
            x_high(Tile(q, None, 0))
            tiles(act, q, slot)

        def moe_vector(dve, q):
            s = q.s

            def x_low(i):
                reached(dve, s["x_hi"], i.n + 1)
                nc.vector.tensor_tensor(xt_l[i.buf], PS[:, q.x_bank, 0:ST], xt_h[i.buf].bitcast(F32), ALU.subtract).then_inc(s["x_lo"], 1)

            def low_weights(i):
                reached(dve, s["w_hi"], 2 * (i.n + 1))
                w = slice(q.pool_cols, q.cols)
                nc.vector.tensor_tensor(parts[i.buf][1][:, w], raw[i.buf][:, w], parts[i.buf][0][:, w].bitcast(F32),
                                        ALU.subtract).then_inc(s["w_lo2"], 1)

            def last_stored(i):
                if i.p is not None or q.m or i.c >= 3:
                    dve.wait_ge(st_y[i.buf], 16 * (q.stores_before[i.buf] + TILES * i.turn))
                waits_passed(dve)

            def result_places(i, step):
                rows = x_rows[i.buf][:, 0:TILES * q.row].rearrange("p (r c) -> p r c", r=TILES)
                if step == 0:
                    last_stored(i)
                    nc.vector.scalar_tensor_tensor(
                        out=id_part[:, :, 0:q.top], in0=rows[:, :, D + 1:D + 1 + q.top],
                        scalar=biases[i.buf][:, q.n_bias - 1:q.n_bias],
                        in1=choice_at[:, 0:q.top].unsqueeze(1).to_broadcast([D, TILES, q.top]),
                        op0=ALU.is_equal, op1=ALU.mult).then_inc(s["ids"], 1)
                if step == 1:
                    reached(dve, s["ids"], 3 * i.n + 1)
                    waits_passed(dve)
                    nc.vector.tensor_reduce(out=id_sum, in_=id_part[:, :, 0:q.top], axis=AX.X, op=ALU.add).then_inc(s["ids"], 1)
                if step == 2:
                    reached(dve, s["ids"], 3 * i.n + 2)
                    nc.vector.tensor_tensor(y_place[i.buf], id_sum, rows[:, :, D], ALU.add).then_inc(s["ids"], 1)

            def rows_out(j):
                reached(dve, s["yt"], j.n + 1)
                last_stored(j)
                nc.vector.tensor_copy(y_rows[j.buf], PS[:, 7, 0:ST]).then_inc(s["y_out"], 1)

            def besides(i, f):
                if f == 0 and not q.gated and (i + -2).live:
                    rows_out(i + -2)
                if f == 1 and (i + 1).live:
                    x_low(i + 1)
                if f == 2 and not q.gated and (i + 1).live:
                    low_weights(i + 1)
                if f >= 1 and i.live:
                    result_places(i, f - 1)

            def low(u, src):
                reached(dve, s["hi"], u.n + 1)
                nc.vector.tensor_tensor(hid_l[u.part], src, hid_h[u.part].bitcast(F32), ALU.subtract).then_inc(s["lo"], 1)

            def slot(i):
                if q.gated and (i + -2).live:
                    rows_out(i + -2)
                for f in range(FCH):
                    u = i.unit(f)
                    if q.gated and u.live:
                        reached(dve, s["act"], u.n + 1)
                        reached(dve, s["lo"], u.n - 2)
                        nc.vector.tensor_tensor(mul_f[u.buf], hid_f[u.buf], PS[:, 3 + u.buf, 0:ST], ALU.mult).then_inc(s["mul"], 1)
                    if q.gated and i.unit(f - 1).live:
                        low(i.unit(f - 1), mul_f[i.unit(f - 1).buf])
                    if not q.gated and u.live:
                        reached(dve, s["act"], u.n + 1)
                        reached(dve, s["down"], u.n - 3)
                        nc.vector.tensor_copy(hid_h[u.part], hid_f[u.buf]).then_inc(s["hi"], 1)
                    besides(i, f)
                    if not q.gated and u.live:
                        low(u, hid_f[u.buf])

            if not q.gated:
                low_weights(Tile(q, None, 0))
            x_low(Tile(q, None, 0))
            tiles(dve, q, slot)


        def result_rows(q, b):
            at = b % 2 * 1536
            return flat((frames if b % 4 < 2 else hid1)[:, :, :])[:, at:at + TILES * q.top * 128]

        def combine_sync(sp, q):
            for k in range(3):
                n = TILES * len(range(k, q.tiles, 3))
                sp.wait_ge(st_y[k], 16 * (q.stores_before[k] + n))
            for b in range(B):
                if b >= 4:
                    sp.wait_ge(summed, q.m * B + b - 3)
                for r, a, e in ((128, 0, TILES - 1), (ROWS[-1], TILES - 1, TILES)):
                    n = (e - a) * q.top
                    at = (b * TILES + a) * q.top * 128
                    sp.dma_start(
                        result_rows(q, b)[0:r, a * q.top * 128:e * q.top * 128].rearrange("p (j c) -> p j c", j=n),
                        A[f"ys{q.m}"][at:at + n * 128].rearrange("(j p) c -> p j c", p=128)[0:r]).then_inc(gathered[b % 4], 16)

        def diagonal(q, b, j, r):
            at = b % 2 * 1536 + j * 128
            return flat(cen[:, :, :])[0:r, at:at + r]

        def parts_of_clip(q, b):
            for j in range(TILES * q.top):
                i, k = divmod(j, q.top)
                at = k * NTT + b * TILES + i
                yield j, i, k, ROWS[i], gates[0:ROWS[i], at:at + 1]

        def combine_scalar(act, q):
            for b in range(B):
                if b >= 2:
                    act.wait_ge(summed, q.m * B + b - 1)
                for j, i, k, r, g in parts_of_clip(q, b):
                    if j % 4 == 3:
                        last = nc.scalar.activation(diagonal(q, b, j, r), ident[0:r, 0:r], ACT.Copy, scale=g)
                last.then_inc(diag_act, 1)

        def combine_vector(dve, q):
            def add(b):
                dve.wait_ge(summed, q.m * B + b + 1)
                nc.vector.tensor_tensor(res[:, b, 0:NT], res[:, b, 0:NT], PS[:, b % 2, 0:NT], ALU.add).then_inc(added, 1)

            for b in range(B):
                if b >= 2:
                    dve.wait_ge(summed, q.m * B + b - 1)
                for j, i, k, r, g in parts_of_clip(q, b):
                    if j % 4 != 3:
                        last = nc.vector.tensor_scalar(diagonal(q, b, j, r), ident[0:r, 0:r], g, None, ALU.mult)
                last.then_inc(diag_dve, 1)
                if b:
                    add(b - 1)
            add(B - 1)

        def combine_tensor(pe, q):
            for b in range(B):
                pe.wait_ge(gathered[b % 4], 32 * (q.m * B // 4 + b // 4 + 1))
                pe.wait_ge(diag_act, q.m * B + b + 1)
                pe.wait_ge(diag_dve, q.m * B + b + 1)
                if b >= 2:
                    pe.wait_ge(added, q.m * B + b - 1)
                for j, i, k, r, g in parts_of_clip(q, b):
                    last = nc.tensor.matmul(PS[:, b % 2, 128 * i:128 * i + r], result_rows(q, b)[0:r, j * 128:(j + 1) * 128],
                                            diagonal(q, b, j, r), start=k == 0, stop=k == q.top - 1)
                last.then_inc(summed, 1)


        SHARED_UNITS = B * SHARED * FCH
        q1 = MOES[1]

        def shared_sync(sp):
            sp.wait_ge(ln_norm, (LN_MOE1 + 1) * B)
            for e in range(SHARED):
                sp.dma_start(raw[1 + e][:, 0:q1.packed], A["experts1"][E1 + e]).then_inc(ld_sh, 16)

        def shared_gpsimd(pool):
            pool.wait_ge(ld_sh, 16 * SHARED)
            for e in range(SHARED):
                split(pool, parts[1 + e][0][:, 0:q1.cols], parts[1 + e][1][:, 0:q1.cols], raw[1 + e][:, 0:q1.cols],
                      sh["w_hi"], sh["w_lo"], e + 1)

        def shared_tensor(pe):
            pe.wait_ge(sh["w_lo"], SHARED)
            pe.wait_ge(ln_lo, B)
            pe.wait_ge(slots_set, 2)
            pe.wait_ge(turned_out, 12)
            for step in range(SHARED_UNITS + 3):
                if step < SHARED_UNITS:
                    b, e, f = step // (2 * FCH), step // FCH % 2, step % FCH
                    if step >= 3:
                        pe.wait_ge(sh["act"], step - 2)
                    c = slice(f * 128, f * 128 + 128)
                    three(pe, PS[:, step % 3, 0:NT], parts[1 + e][0][:, c], parts[1 + e][1][:, c],
                          xh[:, b, 0:NT], xl[:, b, 0:NT]).then_inc(sh["up"], 1)
                if step >= 3:
                    u = step - 3
                    b, e, f = u // (2 * FCH), u // FCH % 2, u % FCH
                    if e == 0 and f == 0 and b >= 2:
                        pe.wait_ge(sh["out"], b - 1)
                    pe.wait_ge(sh["lo"], u + 1)
                    c = slice(FF + f * 128, FF + f * 128 + 128)
                    three(pe, PS[:, 6 + b % 2, 0:NT], parts[1 + e][0][:, c], parts[1 + e][1][:, c],
                          hid_h[u % 4][:, 0:NT], hid_l[u % 4][:, 0:NT], start=e == 0 and f == 0,
                          stop=e == 1 and f == FCH - 1).then_inc(sh["down"], 1)
            pe.wait_ge(sh["out"], B)

        def shared_scalar(act):
            def out_(b):
                act.wait_ge(sh["down"], (b + 1) * SHARED * FCH)
                act.wait_ge(sh["b2"], 2)
                if b >= 2:
                    act.wait_ge(sh["added"], b - 1)
                nc.scalar.activation(xn[:, 4 + b % 2, 0:NT], PS[:, 6 + b % 2, 0:NT], ACT.Identity, scale=1.0 / SHARED,
                                     bias=shared_b2).then_inc(sh["out"], 1)

            for u in range(SHARED_UNITS):
                act.wait_ge(sh["up"], u + 1)
                if u >= 3:
                    act.wait_ge(sh["lo"], u - 2)
                at = q1.cols + u % FCH
                nc.scalar.activation(hid_f[u % 3][:, 0:NT], PS[:, u % 3, 0:NT], ACT.Gelu,
                                     bias=raw[1 + u // FCH % 2][:, at:at + 1]).then_inc(sh["act"], 1)
                if u >= 11 and u % 8 == 3:
                    out_(u // 8 - 1)
            out_(B - 1)

        def shared_vector(dve):
            def add(b):
                dve.wait_ge(sh["out"], b + 1)
                nc.vector.tensor_tensor(res[:, b, 0:NT], res[:, b, 0:NT], xn[:, 4 + b % 2, 0:NT], ALU.add).then_inc(sh["added"], 1)

            dve.wait_ge(ld_sh, 16 * SHARED)
            at = slice(q1.cols + FCH, q1.cols + FCH + 1)
            nc.vector.tensor_tensor(shared_b2, raw[1][:, at], raw[2][:, at], ALU.add).then_inc(sh["b2"], 1)
            dve.wait_ge(sh["b2"], 1)
            nc.vector.tensor_scalar(shared_b2, shared_b2, 1.0 / SHARED, None, ALU.mult).then_inc(sh["b2"], 1)
            for u in range(SHARED_UNITS):
                dve.wait_ge(sh["act"], u + 1)
                if u >= 4:
                    dve.wait_ge(sh["down"], u - 3)
                nc.vector.tensor_copy(hid_h[u % 4][:, 0:NT], hid_f[u % 3][:, 0:NT]).then_inc(sh["hi"], 1)
                dve.wait_ge(sh["hi"], u + 1)
                nc.vector.tensor_tensor(hid_l[u % 4][:, 0:NT], hid_f[u % 3][:, 0:NT], hid_h[u % 4][:, 0:NT].bitcast(F32),
                                        ALU.subtract).then_inc(sh["lo"], 1)
                if u >= 12 and u % 8 == 4:
                    add(u // 8 - 1)
            add(B - 1)


        left = att_raw[:, :, :].rearrange("p j d -> p (j d)")
        place = left[:, 0:TOP1 * NTT].bitcast(U32)
        gates = left[:, 128:128 + TOP1 * NTT]
        shared_b2 = left[:, 255:256]
        biases = [left[:, 320 + 8 * k:320 + 8 * k + FCH + 2] for k in range(3)]
        id_part = left[:, 352:352 + TILES * TOP1].rearrange("p (r k) -> p r k", r=TILES)
        id_sum = left[:, 368:368 + TILES]
        y_place = [left[:, 376 + 4 * k:376 + 4 * k + TILES].bitcast(U32) for k in range(3)]
        tile_expert = left[0:1, 256:256 + TILES_MAX].bitcast(I32)
        scratch = flat(frames[:, :, :])
        best, places_f = [scratch[:, j * 128:j * 128 + TOP1 * NTT] for j in range(2)]
        row_a, row_b = [scratch[:, 256 + j * 32:256 + j * 32 + NTT] for j in range(2)]
        need_all, run_a_all, run_b_all, first_all = [scratch[:, 320 + j * E1:320 + (j + 1) * E1] for j in range(4)]
        over = scratch[:, ST:ST + E1 * CAP_TILES]
        tile_sum = scratch[0:1, 2 * ST:2 * ST + TILES_MAX]
        starts = scratch[0:1, 3 * ST:3 * ST + TILES_MAX * E1]
        links = [0]

        def token_rows(q):
            return flat(workf[:, :, :])[:, 3 * ST:3 * ST + NTT * q.row].rearrange("p (t c) -> p t c", t=NTT)

        def link(dve, ins):
            links[0] += 1
            ins.then_inc(gate, 1)
            dve.wait_ge(gate, links[0])

        def gates_tensor(pe, q, wg, n_exp):
            k = LN_MOE0 if q.gated else LN_MOE1
            for t in range(NTT):
                b, i = divmod(t, TILES)
                pe.wait_ge(ln_norm, k * B + b + 1)
                last = nc.tensor.matmul(PS[:, 0, t * n_exp:(t + 1) * n_exp], xn[:, b, 128 * i:128 * i + 128], wg[:], start=True, stop=True)
            last.then_inc(lg_done, 1)
            for t in range(NTT):
                b, i = divmod(t, TILES)
                last = nc.tensor.transpose(PS[:, 2 + t // 4, t % 4 * 128:t % 4 * 128 + 128], xn[:, b, 128 * i:128 * i + 128], ident[:])
                if t % 4 == 3:
                    last.then_inc(turned, 1)
            pe.wait_ge(picked_set, q.m + 1)
            picked = flat(choice_views(q)["picked"])
            nc.tensor.matmul(PS[:, 0, 0:NTT * n_exp], below[:], picked, start=True, stop=True)
            nc.tensor.matmul(PS[:, 1, 0:NTT * n_exp], mean_w[:], picked, start=True, stop=True).then_inc(rank_done, 1)

        def choice_views(q):
            n = NTT * q.n_exp
            names = ("val", "work", "eq", "picked", "total", "run_a", "run_b", "place")
            v_ = {name: flat(cen[:, :, :])[:, j * ST:j * ST + n] for j, name in enumerate(names)}
            for k in range(q.top):
                v_[k] = flat(hid1[:, :, :])[:, 1536 + k * ST:1536 + k * ST + n]
            return {name: a.rearrange("p (t e) -> p t e", e=q.n_exp) for name, a in v_.items()}

        def gates_scalar(act, q):
            if not q.gated:
                act.wait_ge(gate_ex, 2)
                val = choice_views(q)["val"]
                nc.scalar.activation(val, val, ACT.Exp).then_inc(gate_exp, 1)
            act.wait_ge(filled, 16 * 6)
            for j in range(6):
                act.wait_ge(turned, 6 * q.m + j + 1)
                nc.scalar.activation(token_rows(q)[:, 4 * j:4 * j + 4, 0:D],
                                     PS[:, 2 + j, :].rearrange("p (t c) -> p t c", t=4), ACT.Copy).then_inc(turned_out, 1)
            act.wait_ge(gate_ex, 1 if q.gated else 3)
            g = gates[:, 0:q.top * NTT]
            nc.scalar.activation(g, g, ACT.Exp).then_inc(gate_exp, 1)

        def gates_vector(dve, q):
            n_exp, top = q.n_exp, q.top
            v_ = choice_views(q)
            val, work, eq, picked = v_["val"], v_["work"], v_["eq"], v_["picked"]
            full = [D, NTT, n_exp]
            op = nc.vector

            def wide(row):
                return row.unsqueeze(2).to_broadcast(full)

            def k_row(t, k):
                return t[:, k * NTT:(k + 1) * NTT]

            def each(row):
                return row.unsqueeze(1).to_broadcast([D, top, NTT])

            def by_choice(t):
                return t[:, 0:top * NTT].rearrange("p (k t) -> p k t", k=top)

            dve.wait_ge(lg_done, q.m + 1)
            dve.wait_ge(filled, 16 * 6)
            op.tensor_copy(token_rows(q)[:, :, D], homes[:, q.m * NTT:(q.m + 1) * NTT])
            if top < TOP1:
                op.memset(token_rows(q)[:, :, D + 1 + top:q.row], 0.0)
            link(dve, op.tensor_copy(val, PS[:, 0, 0:NTT * n_exp].rearrange("p (t e) -> p t e", e=n_exp)))
            if not q.gated:
                link(dve, op.tensor_reduce(out=row_a, in_=val, axis=AX.X, op=ALU.max))
                op.tensor_tensor(val, val, wide(row_a), ALU.subtract).then_inc(gate_ex, 1)
                dve.wait_ge(gate_exp, 2)
                link(dve, op.tensor_reduce(out=row_a, in_=val, axis=AX.X, op=ALU.add))
                link(dve, op.reciprocal(row_a, row_a))
                link(dve, op.tensor_tensor(val, val, wide(row_a), ALU.mult))
            for k in range(top):
                now = val if k == 0 else work
                link(dve, op.tensor_reduce(out=k_row(best, k), in_=now, axis=AX.X, op=ALU.max))
                link(dve, op.tensor_tensor(eq, now, wide(k_row(best, k)), ALU.is_equal))
                link(dve, op.tensor_tensor(eq, eq, rev_idx[:, 0:n_exp].unsqueeze(1).to_broadcast(full), ALU.mult))
                link(dve, op.tensor_reduce(out=row_b, in_=eq, axis=AX.X, op=ALU.max))
                link(dve, op.tensor_tensor(v_[k], eq, wide(row_b), ALU.is_equal))
                op.tensor_scalar(token_rows(q)[:, :, D + 1 + k], row_b, -1.0, float(E1), ALU.mult, ALU.add)
                link(dve, op.scalar_tensor_tensor(out=work, in0=v_[k], scalar=-BIG, in1=now, op0=ALU.mult, op1=ALU.add))
            op.scalar_tensor_tensor(out=picked, in0=work, scalar=-BIG / 2, in1=wide(valid[:]), op0=ALU.is_lt,
                                    op1=ALU.mult).then_inc(picked_set, 1)

            op.tensor_tensor(by_choice(gates), by_choice(best), each(k_row(best, 0)), ALU.subtract).then_inc(gate_ex, 1)
            dve.wait_ge(gate_exp, 1 if q.gated else 3)
            link(dve, op.tensor_reduce(out=row_a, in_=by_choice(gates).rearrange("p k t -> p t k"), axis=AX.X, op=ALU.add))
            link(dve, op.reciprocal(row_a, row_a))
            link(dve, op.tensor_tensor(by_choice(gates), by_choice(gates), each(row_a), ALU.mult))

            def running(cur, bufs, n, cut):
                step, j = 1, 0
                while step < n:
                    nxt = bufs[j % 2]
                    link(dve, op.tensor_tensor(cut(nxt, step, n), cut(cur, step, n), cut(cur, 0, n - step), ALU.add))
                    link(dve, op.tensor_copy(cut(nxt, 0, step), cut(cur, 0, step)))
                    cur, step, j = nxt, 2 * step, j + 1
                return cur

            total, at = v_["total"], v_["place"]
            dve.wait_ge(rank_done, q.m + 1)
            link(dve, op.tensor_scalar(total, PS[:, 1, 0:NTT * n_exp].rearrange("p (t e) -> p t e", e=n_exp), float(D), None, ALU.mult))
            upto = running(total, (v_["run_a"], v_["run_b"]), NTT, lambda t, a, b: t[:, a:b, :])
            tokens = upto[:, NTT - 1, :]
            need, run_a, run_b, first = [a[:, 0:n_exp] for a in (need_all, run_a_all, run_b_all, first_all)]
            o = over[:, 0:n_exp * CAP_TILES].rearrange("p (e j) -> p e j", e=n_exp)
            link(dve, op.tensor_tensor(o, tokens.unsqueeze(2).to_broadcast([D, n_exp, CAP_TILES]),
                                       counts[:, 0:CAP_TILES].unsqueeze(1).to_broadcast([D, n_exp, CAP_TILES]), ALU.is_gt))
            link(dve, op.tensor_reduce(out=need, in_=o, axis=AX.X, op=ALU.add))
            ends = running(need, (run_a, run_b), n_exp, lambda t, a, b: t[:, a:b])
            n = q.tiles
            cmp_ = starts[:, 0:n * n_exp].rearrange("p (i e) -> p i e", e=n_exp)
            link(dve, op.tensor_tensor(cmp_, counts[0:1, CAP_TILES:CAP_TILES + n].unsqueeze(2).to_broadcast([1, n, n_exp]),
                                       ends[0:1].unsqueeze(1).to_broadcast([1, n, n_exp]), ALU.is_ge))
            link(dve, op.tensor_reduce(out=tile_sum[:, 0:n], in_=cmp_, axis=AX.X, op=ALU.add))
            op.tensor_scalar(tile_expert[:, 0:n], tile_sum[:, 0:n], float(n_exp - 1), None, ALU.min).then_inc(map_set, 1)
            link(dve, op.tensor_tensor(first, ends, need, ALU.subtract))
            link(dve, op.tensor_scalar(first, first, float(ST), None, ALU.mult))
            link(dve, op.tensor_tensor(at, upto, total, ALU.subtract))
            link(dve, op.tensor_tensor(at, at, PS[:, 0, 0:NTT * n_exp].rearrange("p (t e) -> p t e", e=n_exp), ALU.add))
            link(dve, op.tensor_tensor(at, at, first.unsqueeze(1).to_broadcast(full), ALU.add))
            for k in range(top):
                link(dve, op.tensor_tensor(v_[k], v_[k], at, ALU.mult))
                link(dve, op.tensor_reduce(out=k_row(places_f, k), in_=v_[k], axis=AX.X, op=ALU.add))
            op.tensor_copy(place[:, 0:top * NTT], places_f[:, 0:top * NTT]).then_inc(slots_set, 1)


        block = ctx.enter_context(nc.Block())

        @block.sync
        def _(sp):
            def load(dst, src, s):
                sp.dma_start(dst, src).then_inc(s, 16)

            for h, (dst, name) in enumerate(((raw_wq, "wq0"), (raw_wk, "wk0"), (raw_wv, "wv0"), (raw_wu, "wu0"))):
                load(dst, A[name].rearrange("(h e) d -> e h d", h=HEADS), ld_att)
            for j, name in enumerate(("wq1", "wk1", "wv1", "wo1")):
                load(att_raw[:, j, :], A[name], ld_att)
            load(center_w[:], A["center_w"], ld_att)
            load(frames[:, :, 0:T], A["frames"], ld_frames)
            load(w_comp[:], A["w_comp"], ld_tok)
            load(w_main[:], A["w_main"], ld_tok)
            load(w_exp[:], A["w_exp"], ld_tok)
            load(w_ff1[:], A["w_ff1"], ld_tok)
            load(w_ff2[:], A["w_ff2"], ld_tok)
            load(vec[:], A["vec"], ld_tok)
            load(vec64[:], A["vec64"], ld_tok)
            for dst, name in ((ident, "ident"), (mean_w, "mean_w"), (head_w, "head_w"), (causal, "causal"),
                              (head_mask, "head_mask"), (rev_idx, "rev_idx"),
                              (counts, "counts"), (valid, "valid"), (below, "below"), (homes, "homes"),
                              (choice_at, "choice_at")):
                load(dst[:], A[name], ld_const)
            load(wg0[:], A["wg0"], ld_moe)
            load(wg1[:], A["wg1"], ld_moe)
            sp.wait_ge(zero_set, 2)
            for q in MOES:
                for k in range(3):
                    a, b = q.tiles * k // 3, q.tiles * (k + 1) // 3
                    sp.dma_start(A[f"xs{q.m}"][a:b].rearrange("i p c -> p i c"),
                                 empty.unsqueeze(1).to_broadcast([D, b - a, TILES * q.row])).then_inc(filled, 16)
            for q in MOES:
                if q.m == 1:
                    shared_sync(sp)
                moe_sync(sp, q)
                combine_sync(sp, q)
            sp.wait_ge(stored, 16 * B)

        @block.tensor
        def _(pe):
            start_counts(pe, "tensor")
            pe.wait_ge(ld_att, 16 * 9)
            for h in range(HEADS):
                nc.tensor.matmul(PS[:, h // 4, h % 4 * D:(h % 4 + 1) * D], raw_wq[:, h, :], raw_wk[:, h, :], start=True, stop=True)
            for h in range(HEADS):
                nc.tensor.matmul(PS[:, 2 + h // 4, h % 4 * D:(h % 4 + 1) * D], raw_wv[:, h, :], raw_wu[:, h, :], start=True, stop=True)
            for j in range(2):
                last = nc.tensor.matmul(PS[:, 4, j * D:(j + 1) * D], att_raw[:, j, :], center_w[:], start=True, stop=True)
            last.then_inc(prod_done, 1)

            pe.wait_ge(ld_frames, 16)
            pe.wait_ge(ld_tok, 16 * 7)
            pe.wait_ge(pads_set, 1)
            pe.wait_ge(prod_taken, 3)
            for b in range(B):
                nc.tensor.matmul(PS[0:BN, b, 0:TC], w_comp[:], frames[:, b, 0:TC], start=True, stop=True).then_inc(comp_done, 1)
            for b in range(B):
                pe.wait_ge(comp_act, b + 1)
                for k in range(3):
                    last = nc.tensor.matmul(PS[0:BN, b, 0:TC], w_main[:, k, :], hid1[0:BN, b, k:k + TC], start=k == 0, stop=k == 2)
                last.then_inc(main_done, 1)
            for b in range(B):
                pe.wait_ge(main_act, b + 1)
                nc.tensor.matmul(PS[:, b, 0:TC], w_exp[:], cen[0:BN, b, 0:TC], start=True, stop=True).then_inc(exp_done, 1)
            pe.wait_ge(ld_const, 16 * 11)
            ln_tensor(pe, LN_CONV, frames, TC, lambda pe, b: pe.wait_ge(exp_sum, b + 1))
            for b in range(B):
                pe.wait_ge(ln_aff, b + 1)
                nc.tensor.matmul(PS[0:BN, b, 0:TC], w_ff1[:], xn[:, b, 0:TC], start=True, stop=True).then_inc(ff1_done, 1)
            for b in range(B):
                pe.wait_ge(ff1_act, b + 1)
                nc.tensor.matmul(PS[:, b, 0:TC], w_ff2[:], hid1[0:BN, b, 0:TC], start=True, stop=True).then_inc(ff2_done, 1)
            ln_tensor(pe, LN_FF, xn, TC, lambda pe, b: pe.wait_ge(ff2_sum, b + 1))

            ln_tensor(pe, LN_ATT0, res, NT, lambda pe, b: pe.wait_ge(pooled, b + 1))
            pe.wait_ge(parts_made, 3)
            attention_tensor(pe, 0)

            ln_tensor(pe, LN_MOE0, res, NT, lambda pe, b: past(pe, att[0]["o_taken"], B))
            pe.wait_ge(ld_moe, 16 * 2)
            gates_tensor(pe, MOES[0], wg0, E0)
            moe_tensor(pe, MOES[0])
            combine_tensor(pe, MOES[0])

            ln_tensor(pe, LN_ATT1, res, NT, lambda pe, b: pe.wait_ge(added, B))
            for b in range(B):
                pe.wait_ge(ln_norm, LN_ATT1 * B + b + 1)
                nc.tensor.matmul(PS[:, b, 0:NT], a1c[:, 0, :], xn[:, b, 0:NT], start=True, stop=True).then_inc(q_done, 1)
            ln_tensor(pe, LN_Q, None, NT, None, mean=False, weights=head_w)
            for b in range(B):
                pe.wait_ge(ln_log, LN_Q * B + b + 1)
                nc.tensor.matmul(PS[:, b, 0:NT], a1c[:, 1, :], xn[:, b, 0:NT], start=True, stop=True).then_inc(k_done, 1)
            ln_tensor(pe, LN_K, None, NT, None, mean=False, weights=head_w)
            pe.wait_ge(ln_log, (LN_K + 1) * B)
            attention_tensor(pe, 1)

            ln_tensor(pe, LN_MOE1, res, NT, lambda pe, b: past(pe, att[1]["o_taken"], B))
            gates_tensor(pe, MOES[1], wg1, E1)
            shared_tensor(pe)
            moe_tensor(pe, MOES[1])
            combine_tensor(pe, MOES[1])

        @block.scalar
        def _(act):
            start_counts(act, "scalar")
            for j, (dst, src) in enumerate(((mh, prod[:, 0:1024]), (nh, prod[:, 1024:2048]))):
                act.wait_ge(prod_taken, j + 1)
                nc.scalar.activation(dst[:, :, :].rearrange("p h d -> p (h d)"), src, ACT.Copy).then_inc(prod_link, 1)
            act.wait_ge(ld_att, 16 * 9)
            nc.scalar.activation(a1h[:, :, :], att_raw[:, 2:4, :], ACT.Copy).then_inc(prod_link, 1)

            act.wait_ge(ld_tok, 16 * 7)
            act.wait_ge(pads_set, 1)
            for b in range(B):
                act.wait_ge(comp_done, b + 1)
                nc.scalar.activation(hid1[0:BN, b, 1:T + 1], PS[0:BN, b, 0:T], ACT.Silu, bias=vec64[:, 0:1]).then_inc(comp_act, 1)
            for b in range(B):
                act.wait_ge(main_done, b + 1)
                nc.scalar.activation(cen[0:BN, b, 0:TC], PS[0:BN, b, 0:TC], ACT.Silu, bias=vec64[:, 1:2]).then_inc(main_act, 1)
            ln_scalar(act, LN_CONV, TC)
            for b in range(B):
                act.wait_ge(ff1_done, b + 1)
                nc.scalar.activation(hid1[0:BN, b, 0:TC], PS[0:BN, b, 0:TC], ACT.Gelu, bias=vec64[:, 2:3]).then_inc(ff1_act, 1)
            ln_scalar(act, LN_FF, TC)

            ln_scalar(act, LN_ATT0, NT)
            act.wait_ge(ln_norm, (LN_ATT0 + 1) * B)
            attention_scalar(act, 0)

            ln_scalar(act, LN_MOE0, NT)
            gates_scalar(act, MOES[0])
            moe_scalar(act, MOES[0])
            combine_scalar(act, MOES[0])

            ln_scalar(act, LN_ATT1, NT)
            for k in (LN_Q, LN_K):
                ln_scalar(act, k, NT)
            act.wait_ge(ln_aff, (LN_AFF[LN_K] + 1) * B)
            act.wait_ge(vz_done, 4)
            attention_scalar(act, 1)

            ln_scalar(act, LN_MOE1, NT)
            gates_scalar(act, MOES[1])
            high_parts(act)
            shared_scalar(act)
            moe_scalar(act, MOES[1])
            combine_scalar(act, MOES[1])
            for b in range(B):
                act.wait_ge(added, B + b + 1)
                act.dma_start(out[:, b, :], res[:, b, 0:TP]).then_inc(stored, 16)

        @block.gpsimd
        def _(pool):
            start_counts(pool, "gpsimd")
            pool.wait_ge(ld_tok, 16 * 7)
            ln_gpsimd(pool, LN_CONV, TC, xn, v("g_conv"), v("b_conv"))
            ln_gpsimd(pool, LN_FF, TC, frames, v("g_ff"), v("b_ff"))
            attention_gpsimd(pool, 0)
            moe_gpsimd(pool, MOES[0])
            pool.wait_ge(prod_taken, 4)
            ln_gpsimd(pool, LN_Q, NT, frames, qaff[:, 0:1], qaff[:, 1:2])
            ln_gpsimd(pool, LN_K, NT, hid1, v("k_gamma"), v("k_beta"))
            attention_gpsimd(pool, 1)
            shared_gpsimd(pool)
            moe_gpsimd(pool, MOES[1])

        @block.vector
        def _(dve):
            start_counts(dve, "vector")
            nc.vector.memset(empty, 0.0).then_inc(zero_set, 1)
            dve.wait_ge(zero_set, 1)
            nc.vector.memset(empty.rearrange('p (r c) -> p r c', r=TILES)[:, :, D:D + 1], NOWHERE).then_inc(zero_set, 1)
            nc.vector.memset(frames[:, :, T:ST], 0.0)
            nc.vector.memset(hid1[:, :, 0:1], 0.0)
            nc.vector.memset(hid1[:, :, T + 1:ST], 0.0)
            nc.vector.memset(small[:, :, :], 1.0)
            nc.vector.memset(eps[:], EPS).then_inc(pads_set, 1)
            nc.vector.memset(vph[1].bitcast(F32), 0.0).then_inc(vz_done, 1)
            nc.vector.memset(vpl[1].bitcast(F32), 0.0).then_inc(vz_done, 1)
            dve.wait_ge(prod_done, 1)
            nc.vector.tensor_scalar(prod[:, 0:1024], PS[:, 0:2, :].rearrange("p a c -> p (a c)"), -float(D) ** -0.5, None, ALU.mult).then_inc(prod_taken, 1)
            nc.vector.tensor_copy(prod[:, 1024:2048], PS[:, 2:4, :].rearrange("p a c -> p (a c)")).then_inc(prod_taken, 1)
            nc.vector.tensor_copy(a1c[:, :, :].rearrange("p j d -> p (j d)"), PS[:, 4, 0:2 * D]).then_inc(prod_taken, 1)
            for j, (hi, lo, src) in enumerate(((mh, ml, prod[:, 0:1024]), (nh, nl, prod[:, 1024:2048]), (a1h, a1l, None))):
                dve.wait_ge(prod_link, j + 1)
                src = att_raw[:, 2:4, :].rearrange("p h d -> p (h d)") if src is None else src
                nc.vector.tensor_tensor(lo[:, :, :].rearrange("p h d -> p (h d)"), src,
                                        hi[:, :, :].rearrange("p h d -> p (h d)").bitcast(F32), ALU.subtract).then_inc(parts_made, 1)
            dve.wait_ge(ld_tok, 16 * 7)
            nc.vector.tensor_scalar(qaff[:, :], vec[:, VECS.index("q_gamma"):VECS.index("q_gamma") + 2],
                                    -float(HD1) ** -0.5, None, ALU.mult).then_inc(prod_taken, 1)

            for b in range(B):
                dve.wait_ge(exp_done, b + 1)
                nc.vector.scalar_tensor_tensor(out=frames[:, b, 0:TC], in0=PS[:, b, 0:TC], scalar=v("b_expand"),
                                               in1=frames[:, b, 0:TC], op0=ALU.add, op1=ALU.add).then_inc(exp_sum, 1)
            dve.wait_ge(parts_made, 3)
            ln_vector(dve, LN_CONV, frames, TC, xn)
            for b in range(B):
                dve.wait_ge(ff2_done, b + 1)
                nc.vector.scalar_tensor_tensor(out=xn[:, b, 0:TC], in0=PS[:, b, 0:TC], scalar=v("b_ff2"),
                                               in1=xn[:, b, 0:TC], op0=ALU.add, op1=ALU.add).then_inc(ff2_sum, 1)
            ln_vector(dve, LN_FF, xn, TC, frames)
            for b in range(B):
                dve.wait_ge(ln_aff, B + b + 1)
                nc.vector.tensor_tensor(hid1[:, b, 0:NT], frames[:, b, 0:NT], frames[:, b, 1:NT + 1], ALU.max).then_inc(pool_a, 1)
            for b in range(B):
                dve.wait_ge(pool_a, b + 1)
                nc.vector.tensor_tensor(res[:, b, 0:NT], hid1[:, b, 0:NT], frames[:, b, 2:NT + 2], ALU.max).then_inc(pooled, 1)

            dve.wait_ge(ln_cen, 2 * B)
            nc.vector.memset(xn[:, :, NT:ST], 0.0).then_inc(pads_set, 1)
            ln_vector(dve, LN_ATT0, res, NT, xn)
            dve.wait_ge(ln_norm, (LN_ATT0 + 1) * B)
            dve.wait_ge(pads_set, 2)
            attention_vector(dve, 0)

            past(dve, att[0]["o_taken"], B)
            ln_vector(dve, LN_MOE0, res, NT, xn)
            gates_vector(dve, MOES[0])
            moe_vector(dve, MOES[0])
            combine_vector(dve, MOES[0])

            nc.vector.memset(vph[0].bitcast(F32), 0.0).then_inc(vz_done, 1)
            nc.vector.memset(vpl[0].bitcast(F32), 0.0).then_inc(vz_done, 1)
            ln_vector(dve, LN_ATT1, res, NT, xn)
            for k, done, dst in ((LN_Q, q_done, frames), (LN_K, k_done, hid1)):
                for b in range(B):
                    dve.wait_ge(done, b + 1)
                    dve.wait_ge(ln_norm, (k - 1) * B + b + 1)
                    nc.vector.tensor_copy(cen[:, b, 0:NT], PS[:, b, 0:NT]).then_inc(ln_cen, 1)
                ln_vector(dve, k, None, NT, dst, mean=False)
            dve.wait_ge(vz_done, 4)
            dve.wait_ge(ln_aff, (LN_AFF[LN_K] + 1) * B)
            attention_vector(dve, 1)

            past(dve, att[1]["o_taken"], B)
            ln_vector(dve, LN_MOE1, res, NT, xn)
            gates_vector(dve, MOES[1])
            low_parts(dve)
            shared_vector(dve)
            moe_vector(dve, MOES[1])
            combine_vector(dve, MOES[1])


def kernel(**inputs):
    import concourse.bacc as bacc
    from concourse.bass_utils import run_bass_kernel_spmd

    x = {k: np.asarray(a) for k, a in inputs.items()}

    def t(a):
        return np.ascontiguousarray(a)

    def cols(names):
        return t(np.stack([x[n] if x[n].shape[0] != HD1 else np.tile(x[n], HEADS) for n in names], axis=1))

    def chunks(w):
        return w.reshape(-1, FCH, 128, D).transpose(0, 2, 1, 3).reshape(-1, 128, FCH * D)

    def numbers(n):
        return np.tile(np.arange(n, dtype=np.float32)[:, None, None], (1, D, 1))

    def both(n):
        return np.concatenate([x["L1_ffn_re_" + n], x["L1_ffn_se_" + n]])

    part = np.arange(D)
    same_head = (part[:, None] // HD1 == part[None, :] // HD1).astype(np.float32) / HD1
    col = np.arange(ST)
    arrays = {
        "frames": t(x["x"].transpose(2, 0, 1)),
        "w_comp": t(x["L0_tok_w_compress"][:, :, 0].T),
        "w_main": t(x["L0_tok_w_main"].transpose(1, 2, 0)),
        "w_exp": t(x["L0_tok_w_expand"][:, :, 0].T),
        "w_ff1": t(x["L0_tok_w_ff1"].T),
        "w_ff2": t(x["L0_tok_w_ff2"].T),
        "vec": cols(["L0_tok_b_expand", "L0_tok_g_conv_norm", "L0_tok_b_conv_norm", "L0_tok_b_ff2", "L0_tok_g_ff_norm",
                     "L0_tok_b_ff_norm", "L1_attn_bo", "L1_attn_q_gamma", "L1_attn_q_beta", "L1_attn_k_gamma",
                     "L1_attn_k_beta"]),
        "vec64": cols(["L0_tok_b_compress", "L0_tok_b_main", "L0_tok_b_ff1"]),
        "wq0": x["L0_attn_Wq"], "wk0": x["L0_attn_Wk"], "wv0": x["L0_attn_Wv"], "wu0": t(x["L0_attn_Wu"].T),
        "wq1": x["L1_attn_Wq"], "wk1": x["L1_attn_Wk"], "wv1": t(x["L1_attn_Wv"].T), "wo1": t(x["L1_attn_Wo"].T),
        "wg0": x["L0_ffn_Wg"], "wg1": t(x["L1_ffn_gate_w"].T),
        "experts0": t(np.concatenate([x["L0_ffn_W"], x["L0_ffn_V"], chunks(x["L0_ffn_W2"]), numbers(E0)], axis=2)),
        "experts1": t(np.concatenate([
            both("w1"), chunks(both("w2")), both("b1").reshape(-1, FCH, 128).transpose(0, 2, 1), both("b2")[:, :, None],
            numbers(E1 + SHARED)], axis=2)),
        "ident": np.eye(D, dtype=np.float32),
        "mean_w": np.full((D, D), 1.0 / D, np.float32),
        "head_w": same_head,
        "center_w": np.eye(D, dtype=np.float32) - same_head,
        "causal": np.where(col[None, :] - 2 * 128 > part[:, None], np.float32(BIG), np.float32(0)).astype(np.float32),
        "head_mask": (part[:, None] // HD1 == np.arange(HEADS)[None, :]).astype(np.float32),
        "counts": np.tile(np.concatenate([np.arange(CAP_TILES) * ST, np.arange(TILES_MAX)]).astype(np.float32), (D, 1)),
        "valid": (np.arange(B * TILES)[None, :] % TILES * 128 + part[:, None] < NT).astype(np.float32),
        "below": (part[:, None] < part[None, :]).astype(np.float32),
        "homes": np.concatenate([np.arange(B * TILES)[None, :] * top * 128 + part[:, None] for top in (TOP0, TOP1)],
                                axis=1).astype(np.float32),
        "choice_at": np.tile((np.arange(TOP1) * 128).astype(np.float32), (D, 1)),
        "rev_idx": np.tile((E1 - np.arange(E1)).astype(np.float32), (D, 1)),
    }
    nc = bacc.Bacc("TRN2", target_bir_lowering=False, num_devices=1)
    A = {n: nc.dram_tensor("in_" + n, a.shape, F32, kind="ExternalInput").ap() for n, a in arrays.items()}
    for m, top in enumerate((TOP0, TOP1)):
        A[f"xs{m}"] = nc.dram_tensor(f"xs{m}", (MOE_TILES[m], 128, TILES * (D + 1 + TOP1)), F32, kind="Internal").ap()
        A[f"ys{m}"] = nc.dram_tensor(f"ys{m}", (B * TILES * top * 128, D), F32, kind="Internal").ap()
    out = nc.dram_tensor("out", (D, B, TP), F32, kind="ExternalOutput").ap()
    audio_tower(nc, A, out)
    r = run_bass_kernel_spmd(nc, [{"in_" + n: a for n, a in arrays.items()}], core_ids=[0])
    return np.ascontiguousarray(r.results[0]["out"].transpose(1, 2, 0))
```
